# Optimizing a Trainium2 kernel written in Bass

```python
import numpy as np
import jax
import jax.numpy as jnp

def _softmax(x, axis=-1):
    return jax.nn.softmax(x, axis=axis)

def _gelu(x):
    return jax.nn.gelu(x, approximate=True)

def _silu(x):
    return jax.nn.silu(x)

def _sigmoid(x):
    return jax.nn.sigmoid(x)

def _layernorm(x, axis=-1, eps=1e-05):
    m = jnp.mean(x, axis=axis, keepdims=True)
    v = jnp.var(x, axis=axis, keepdims=True)
    return (x - m) / jnp.sqrt(v + eps)

def _scatter_add(tgt, idx, src, axis=0):
    return tgt.at[idx].add(src)

def _segment_sum(src, seg, n):
    return jax.ops.segment_sum(src, seg, n)
kernel_name = 'mk_adaln_d1_jaxref_r8_50730a'

def setup_inputs(seed: int=0):
    np.random.seed(seed)
    _w = jnp.asarray

    def _L0_attn_setup():
        import jax, jax.numpy as jnp
        import numpy as np
        from jax import lax
        BLOCK_LEN = 128
        NEG_INF = -1000000000.0
        key = jax.random.key(seed)
        ks = jax.random.split(key, 8)
        N, L, Dm = (2, 1024, 512)
        W, H, dh = (128, 16, 64)
        s = lambda fan: 1.0 / np.sqrt(fan)
        return {'inputs': jax.random.normal(ks[0], (N, L, Dm), jnp.float32), 'conv_w': jax.random.normal(ks[1], (3, Dm, 3 * W), jnp.float32) * s(3 * Dm), 'conv_b': jnp.zeros((3 * W,), jnp.float32), 'wq': jax.random.normal(ks[2], (W, H, dh), jnp.float32) * s(W), 'bq': jnp.zeros((H, dh), jnp.float32), 'wk': jax.random.normal(ks[3], (W, H, dh), jnp.float32) * s(W), 'bk': jnp.zeros((H, dh), jnp.float32), 'wv': jax.random.normal(ks[4], (W, H, dh), jnp.float32) * s(W), 'bv': jnp.zeros((H, dh), jnp.float32), 'wo': jax.random.normal(ks[5], (H, dh, W), jnp.float32) * s(H * dh), 'bo': jnp.zeros((W,), jnp.float32), 'proj_w': jax.random.normal(ks[6], (W, Dm), jnp.float32) * s(W), 'proj_b': jnp.zeros((Dm,), jnp.float32)}
    _L0_attn_in = _L0_attn_setup()

    def _L0_ffn_setup():
        import jax, jax.numpy as jnp
        import numpy as np
        GROUP = 128
        key = jax.random.key(seed)
        k1, k2, k3 = jax.random.split(key, 3)
        B, S, IN, OUT = (4, 256, 512, 512)
        x = jax.random.normal(k1, (B, S, IN), dtype=jnp.float16)
        weight = jax.random.normal(k2, (OUT, IN), dtype=jnp.float16) * jnp.float16(0.02)
        scales = jax.random.uniform(k3, (OUT, IN // GROUP), dtype=jnp.float16, minval=0.5, maxval=1.5)
        return {'x': x, 'weight': weight, 'scales': scales}
    _L0_ffn_in = _L0_ffn_setup()
    _L0_c = _w((lambda *s: np.random.randn(*s).astype(np.float32) * 0.05)(2, 512))
    _L0_wmod = _w((lambda *s: np.random.randn(*s).astype(np.float32) * 0.05)(512, 6 * 512) * 512 ** (-0.5))
    _d = {'L0_attn_inputs': _L0_attn_in['inputs'], 'L0_attn_conv_w': _L0_attn_in['conv_w'], 'L0_attn_conv_b': _L0_attn_in['conv_b'], 'L0_attn_wq': _L0_attn_in['wq'], 'L0_attn_bq': _L0_attn_in['bq'], 'L0_attn_wk': _L0_attn_in['wk'], 'L0_attn_bk': _L0_attn_in['bk'], 'L0_attn_wv': _L0_attn_in['wv'], 'L0_attn_bv': _L0_attn_in['bv'], 'L0_attn_wo': _L0_attn_in['wo'], 'L0_attn_bo': _L0_attn_in['bo'], 'L0_attn_proj_w': _L0_attn_in['proj_w'], 'L0_attn_proj_b': _L0_attn_in['proj_b'], 'L0_ffn_weight': _L0_ffn_in['weight'], 'L0_ffn_scales': _L0_ffn_in['scales'], 'L0_c': _L0_c, 'L0_wmod': _L0_wmod}
    _x0 = _d['L0_attn_inputs']
    _d['L0_attn_inputs'] = jax.random.normal(jax.random.fold_in(jax.random.key(seed), 1), (2, 1024, 512), dtype=_x0.dtype)
    del _x0
    return _d

def reference(L0_attn_inputs, L0_attn_conv_w, L0_attn_conv_b, L0_attn_wq, L0_attn_bq, L0_attn_wk, L0_attn_bk, L0_attn_wv, L0_attn_bv, L0_attn_wo, L0_attn_bo, L0_attn_proj_w, L0_attn_proj_b, L0_ffn_weight, L0_ffn_scales, L0_c, L0_wmod):

    def _L0_attn_ref(inputs, conv_w, conv_b, wq, bq, wk, bk, wv, bv, wo, bo, proj_w, proj_b):
        import jax, jax.numpy as jnp
        import numpy as np
        from jax import lax
        BLOCK_LEN = 128
        NEG_INF = -1000000000.0
        N, L, Dm = inputs.shape
        x = lax.conv_general_dilated(inputs, conv_w, window_strides=(1,), padding='SAME', dimension_numbers=('NWC', 'WIO', 'NWC')) + conv_b
        q, k, v = jnp.split(x, 3, axis=-1)
        W_ = q.shape[-1]
        nb = L // BLOCK_LEN
        q = q.reshape(N * nb, BLOCK_LEN, W_)
        k = k.reshape(N * nb, BLOCK_LEN, W_)
        v = v.reshape(N * nb, BLOCK_LEN, W_)
        dh = wq.shape[-1]
        qh = jnp.einsum('btd,dhe->bthe', q, wq) + bq
        kh = jnp.einsum('btd,dhe->bthe', k, wk) + bk
        vh = jnp.einsum('btd,dhe->bthe', v, wv) + bv
        scale = 1.0 / jnp.sqrt(jnp.asarray(dh, qh.dtype))
        scores = jnp.einsum('bqhe,bkhe->bhqk', qh * scale, kh)
        causal = jnp.tril(jnp.ones((BLOCK_LEN, BLOCK_LEN), bool))
        scores = jnp.where(causal, scores, NEG_INF)
        p = jax.nn.softmax(scores, axis=-1)
        o = jnp.einsum('bhqk,bkhe->bqhe', p, vh)
        o = jnp.einsum('bqhe,hed->bqd', o, wo) + bo
        o = o.reshape(N, L, W_)
        return o @ proj_w + proj_b

    def _L0_ffn_ref(x, weight, scales):
        import jax, jax.numpy as jnp
        import numpy as np
        GROUP = 128
        out_f, in_f = weight.shape
        w = weight.reshape(out_f, in_f // GROUP, GROUP) * scales[:, :, None]
        w = w.reshape(out_f, in_f)
        y = jnp.einsum('bsi,oi->bso', x, w)
        return y.astype(jnp.float16)
    x = L0_attn_inputs
    mod = (_silu(L0_c) @ L0_wmod).reshape(L0_c.shape[0], 6, 1, -1)
    sa, ca, ga, sb, cb, gb = (mod[:, 0], mod[:, 1], mod[:, 2], mod[:, 3], mod[:, 4], mod[:, 5])
    ga = (2 * (ga >= 0) - 1) * jnp.maximum(jnp.abs(ga), 0.25)
    gb = (2 * (gb >= 0) - 1) * jnp.maximum(jnp.abs(gb), 0.25)
    h = _layernorm(x, axis=-1) * (1 + ca) + sa
    x = x + ga * _L0_attn_ref(h, L0_attn_conv_w, L0_attn_conv_b, L0_attn_wq, L0_attn_bq, L0_attn_wk, L0_attn_bk, L0_attn_wv, L0_attn_bv, L0_attn_wo, L0_attn_bo, L0_attn_proj_w, L0_attn_proj_b)
    h = _layernorm(x, axis=-1) * (1 + cb) + sb
    x = x + gb * _L0_ffn_ref(h, L0_ffn_weight, L0_ffn_scales)
    return x

_drawn_inputs = setup_inputs


def setup_inputs(seed=0):
    import zlib

    import numpy as np

    out = dict(_drawn_inputs(seed))
    spreads = {'L0_attn_conv_b': (0.0, 0.3),
     'L0_attn_bq': (0.0, 0.8),
     'L0_attn_bk': (0.0, 0.8),
     'L0_attn_bv': (0.0, 0.327),
     'L0_attn_bo': (0.0, 0.329),
     'L0_attn_proj_b': (0.0, 0.314)}
    factors = {}
    for name, (base, spread) in spreads.items():
        noise = np.random.default_rng([zlib.crc32(name.encode()), seed]).standard_normal(out[name].shape)
        drawn = base * np.exp(spread * noise) if base else spread * noise
        out[name] = jnp.asarray(drawn.astype(out[name].dtype))
    for name, factor in factors.items():
        out[name] = (out[name] * factor).astype(out[name].dtype)
    return out
```

```python
from contextlib import ExitStack

import concourse.bass as bass
from concourse import mybir

F32 = mybir.dt.float32
F32R = mybir.dt.float32r
F16 = mybir.dt.float16
BF16 = mybir.dt.bfloat16
ALU = mybir.AluOpType
ACT = mybir.ActivationFunctionType
AX_X = mybir.AxisListType.X

P = 128
EPS = 1e-5
NEG_INF = -1.0e9
GATE_FLOOR = 0.25


def adaln_block(nc, x, conv_w, conv_b, wq, bq, wk, bk, wv, bv, wo, bo, proj_w, proj_b,
                ffn_w, ffn_s, c, wmod, out):
    NB, L, D = x.shape
    TAPS, _, W3 = conv_w.shape
    W = W3 // 3
    _, H, E = wq.shape
    DT = D // P
    GT = 512
    BLK = GT // P
    T = NB * L
    G = T // GT
    GPB = L // GT
    HE = H * E
    JT = HE // P
    UNITS = 2 * BLK
    HU = H // 2
    HB = HU // 2
    QSCALE = float(E) ** -0.5
    assert W == P and E * 2 == P and G == 4 and GPB == 2 and NB == 2 and DT == 4
    SHIFT, SCALE1, GATE1, SHIFT2, SCALE2, GATE2 = range(6)

    x_rows = x.rearrange("b (g k p) d -> (b g) p k d", k=BLK, p=P)
    out_rows = out.rearrange("b (g k p) d -> (b g) k p d", k=BLK, p=P)
    conv_rows = conv_w.rearrange("t (k p) w -> p t k w", p=P)
    mod_rows = wmod.rearrange("(k p) (c n) -> c p k n", p=P, n=D)
    wo_rows = wo.rearrange("h e w -> (h e) w").rearrange("(j p) w -> p j w", p=P)

    with ExitStack() as ctx:
        def sb(name, shape, dt=F32):
            return ctx.enter_context(nc.sbuf_tensor(name, shape, dt))

        def sem(name):
            return ctx.enter_context(nc.semaphore(name))

        bank = [ctx.enter_context(nc.psum_tensor(f"bank{i}", [P, 512], F32)) for i in range(8)]

        half_area = sb("half_area", [P, 2 * TAPS * DT * W3 + 2 * DT * (GT + 2)], F32R)
        n_cw = TAPS * DT * W3

        def area(at, *shape):
            n = 1
            for s in shape:
                n *= s
            v = half_area[:, at:at + n]
            if len(shape) == 3:
                return v.rearrange("p (a b c) -> p a b c", a=shape[0], b=shape[1])
            if len(shape) == 2:
                return v.rearrange("p (a b) -> p a b", a=shape[0])
            return v

        cw_hi, cw_lo = area(0, TAPS, DT, W3), area(n_cw, TAPS, DT, W3)
        hT_hi, hT_lo = area(2 * n_cw, DT, GT + 2), area(2 * n_cw + DT * (GT + 2), DT, GT + 2)
        at = 0
        oT_hi = area(at, JT, 2 * P); at += JT * 2 * P
        oT_lo = area(at, JT, 2 * P); at += JT * 2 * P
        h2_hi = area(at, DT, GT); at += DT * GT
        h2_lo = area(at, DT, GT); at += DT * GT
        yT_hi = area(at, GT); at += GT
        yT_lo = area(at, GT); at += GT
        cs_hi = area(at, 3, GT); at += 3 * GT
        cs_lo = area(at, 3, GT); at += 3 * GT
        assert at <= 2 * n_cw + 2 * DT * (GT + 2)
        wqkv_hi = sb("wqkv_hi", [P, 3, HE], F32R)
        wqkv_lo = sb("wqkv_lo", [P, 3, HE], F32R)
        wo_hi = sb("wo_hi", [P, JT, W], F32R)
        wo_lo = sb("wo_lo", [P, JT, W], F32R)
        pw_hi = sb("pw_hi", [P, NB * D], F32R)
        pw_lo = sb("pw_lo", [P, NB * D], F32R)
        wT = sb("wT", [P, DT, D], F32R)
        halo_hi = sb("halo_hi", [P, DT, 2 * G], F32R)
        halo_lo = sb("halo_lo", [P, DT, 2 * G], F32R)

        work = sb("work", [P, 2 * JT * GT + 2 * HE + 4 * HU * P])
        mod_stage = [work[:, i * DT * D:(i + 1) * DT * D].rearrange("p (k n) -> p k n", k=DT) for i in range(2)]
        at = 2 * DT * D
        cw_raw = work[:, at:at + n_cw].rearrange("p (t k w) -> p t k w", t=TAPS, k=DT)
        pw_tmp = work[:, at:at + NB * D].rearrange("p (b d) -> p b d", b=NB)
        at += n_cw
        wqkv_raw = work[:, at:at + 3 * HE].rearrange("p (m n) -> p m n", m=3); at += 3 * HE
        wo_raw = work[:, at:at + JT * W].rearrange("p (j w) -> p j w", j=JT); at += JT * W
        pw_raw = work[:, at:at + D]; at += D
        pb_rows = work[:, at:at + D]; at += D
        assert at <= work.shape[1]
        at = 0
        qh = work[:, at:at + JT * GT].rearrange("p (j t) -> p j t", j=JT); at += JT * GT
        kh = work[:, at:at + JT * GT].rearrange("p (j t) -> p j t", j=JT); at += JT * GT
        vh = work[:, at:at + 2 * HE].rearrange("p (s n) -> p s n", s=2); at += 2 * HE
        prob = work[:, at:at + 2 * HU * P].rearrange("p (s h k) -> p s h k", s=2, h=HU); at += 2 * HU * P
        probT = work[:, at:at + 2 * HU * P].rearrange("p (s h k) -> p s h k", s=2, h=HU); at += 2 * HU * P
        assert at <= work.shape[1]

        cT = sb("cT", [P, 3 * T])
        xin = sb("xin", [P, BLK, D])
        xr = sb("xr", [P, BLK, D])
        w_raw16 = xr[:, 0:2, :].bitcast(F16)
        w16 = xr[:, 2:4, :].bitcast(F16)
        spare = sb("spare", [P, 2, GT])
        y16 = sb("y16", [P, 2, D], F16)
        gb_rows = sb("gb_rows", [P, NB * D])
        shift_rows = sb("shift_rows", [P, NB * D])
        pbga_rows = sb("pbga_rows", [P, NB * D])
        mask = sb("mask", [P, HB, P], BF16)
        ident = sb("ident", [P, P])
        ident_b = sb("ident_b", [P, P], BF16)
        ident_h = sb("ident_h", [P, P], F16)
        scales16 = sb("scales16", [P, BLK, DT], F16)

        NC, NV = NB * DT, 3
        R_CB, R_BQ, R_BK, R_BV, R_BO, NR = NC, NC + NV, NC + NV + JT, NC + NV + 2 * JT, NC + NV + 3 * JT, NC + NV + 3 * JT + 1
        rows = sb("rows", [NR, P])
        cols = sb("cols", [P, NR])
        bq8 = sb("bq8", [P, JT])
        by = sb("by", [P, 1])
        silu = sb("silu", [P, 4, NC])
        modT = sb("modT", [P, 6, DT, NB])
        gate_tmp = sb("gate_tmp", [P, 2, DT, NB])
        cur1 = sb("cur1", [P, 2, DT, 1])
        cur2 = sb("cur2", [P, 1, DT, 1])
        halo_x = sb("halo_x", [2 * NB, D])
        halo_f = sb("halo_f", [P, DT, NB, 2])
        halo_m = sb("halo_m", [P, DT, NB, 2])
        halo_st = sb("halo_st", [2 * NB, 12])
        stats = sb("stats", [P, BLK, 6])
        mv = sb("mv", [P, BLK, 2])
        vare = sb("vare", [P, BLK])
        rstd = sb("rstd", [P, BLK])
        neg_half = sb("neg_half", [P, BLK])
        neg_max = sb("neg_max", [P, 2, HU])
        row_sum = sb("row_sum", [P, 2, HU])
        row_inv = sb("row_inv", [P, 2, HU])
        credit = sb("credit", [P, 3])

        rows_in, halo_in, x_in, cw_in = sem("rows_in"), sem("halo_in"), sem("x_in"), sem("cw_in")
        mod_in = [sem("mod_in0"), sem("mod_in1")]
        wqkv_in, wo_in, pw_in, ffn_in, xr_in, out_sent = (sem("wqkv_in"), sem("wo_in"), sem("pw_in"), sem("ffn_in"),
                                                          sem("xr_in"), sem("out_sent"))
        ident_done, const_done, mask_done = sem("ident_done"), sem("const_done"), sem("mask_done")
        cols_ready, cols_done, silu_exp, silu_step = sem("cols_ready"), sem("cols_done"), sem("silu_exp"), sem("silu_step")
        mod_ready, mod_done, gate_step = sem("mod_ready"), sem("mod_done"), sem("gate_step")
        cwhi_done, cwlo_done = sem("cwhi_done"), sem("cwlo_done")
        whi_done, wlo_done = sem("whi_done"), sem("wlo_done")
        halo_step, halo_rstd, halo_ready, halo_hid, halo_lod = (sem("halo_step"), sem("halo_rstd"), sem("halo_ready"),
                                                                sem("halo_hid"), sem("halo_lod"))
        ga_ready, ga_done, gb_ready, gb_done = sem("ga_ready"), sem("ga_done"), sem("gb_ready"), sem("gb_done")
        pwhi_done, pwlo_done = sem("pwhi_done"), sem("pwlo_done")
        w16_done, wt_ready, wt_done = sem("w16_done"), sem("wt_ready"), sem("wt_done")
        shift_ready, shift_done, by_ready, by_done = sem("shift_ready"), sem("shift_done"), sem("by_ready"), sem("by_done")
        st1, ag1, var1, rstd1, xn_done = sem("st1"), sem("ag1"), sem("var1"), sem("rstd1"), sem("xn_done")
        cur1_done, t1_ready, h_hid, h_full, h_lod, halo_put = (sem("cur1_done"), sem("t1_ready"), sem("h_hid"),
                                                               sem("h_full"), sem("h_lod"), sem("halo_put"))
        conv_tile, conv_ready, c_done = sem("conv_tile"), sem("conv_ready"), sem("c_done")
        cs_hid, cs_lod = sem("cs_hid"), sem("cs_lod")
        qk_ready, qk_act, qk_dve = sem("qk_ready"), sem("qk_act"), sem("qk_dve")
        v_ready, v_act, v_dve = sem("v_ready"), sem("v_act"), sem("v_dve")
        s_ready, max_done, exp_done, inv_done, norm_done = (sem("s_ready"), sem("max_done"), sem("exp_done"),
                                                            sem("inv_done"), sem("norm_done"))
        pt_ready, pt_done, o_ready, o_hid, o_lod = sem("pt_ready"), sem("pt_done"), sem("o_ready"), sem("o_hid"), sem("o_lod")
        wo_ready, y_hid, y_lod, pj_ready = sem("wo_ready"), sem("y_hid"), sem("y_lod"), sem("pj_ready")
        xrb_done, x1_done = sem("xrb_done"), sem("x1_done")
        st2, ag2, var2, rstd2, xn2_done, cur2_done = (sem("st2"), sem("ag2"), sem("var2"), sem("rstd2"),
                                                      sem("xn2_done"), sem("cur2_done"))
        t2_ready, h2_hid, h2_lod = sem("t2_ready"), sem("h2_hid"), sem("h2_lod")
        f_ready, y16_done, gy_done, out_ready = sem("f_ready"), sem("y16_done"), sem("gy_done"), sem("out_ready")
        Y16_FREE, OUT_FREE, C_FREE = BLK, 2, 3

        def f32(ap):
            return ap.bitcast(F32)

        def heads_of(bank_ap):
            return bank_ap[:, :].rearrange("p (h k) -> p h k", h=HB)

        block = ctx.enter_context(nc.Block())

        def qk_use(t):
            return t

        def s_use(u, half):
            return 2 * JT + 6 * (u // 2) + 4 * (u % 2) + half

        def v_use(b, half):
            return 2 * JT + 6 * b + 2 + half

        USES = 2 * JT + 6 * BLK
        assert USES % 4 == 0

        def released(g, use):
            if use < 0:
                g, use = g - 1, use + USES
            if use < 2 * JT:
                return (qk_dve if use % 2 else qk_act), JT * g + use // 2 + 1
            b, r = (use - 2 * JT) // 6, (use - 2 * JT) % 6
            if r in (2, 3):
                return (v_dve if r == 3 else v_act), BLK * g + b + 1
            u, half = 2 * b + (r > 1), r % 2
            return exp_done, 2 * UNITS * g + 2 * u + half + 1

        O_BANK = [6, 7, 6, 7, 7, 6, 7, 6]
        WO_BANK = [6, 7]

        @block.sync
        def _(sp):
            sp.dma_start(rows[0:NC, :], c.rearrange("b (k p) -> (b k) p", p=P)).then_inc(rows_in, 16)
            sp.dma_start(rows[R_CB:R_BQ, :], conv_b.rearrange("(m p) -> m p", p=P)).then_inc(rows_in, 16)
            for at, bias in ((R_BQ, bq), (R_BK, bk), (R_BV, bv)):
                sp.dma_start(rows[at:at + JT, :], bias.rearrange("h e -> (h e)").rearrange("(j p) -> j p", p=P)).then_inc(rows_in, 16)
            sp.dma_start(rows[R_BO:NR, :], bo.rearrange("(a p) -> a p", a=1)).then_inc(rows_in, 16)
            sp.dma_start(xin[:, :, :], x_rows[0]).then_inc(x_in, 16)
            for n, part in enumerate((SCALE1, SHIFT)):
                sp.dma_start(mod_stage[n], mod_rows[part]).then_inc(mod_in[n], 16)
            for t in range(TAPS):
                sp.dma_start(cw_raw[:, t], conv_rows[:, t]).then_inc(cw_in, 16)
            for n, part in enumerate((GATE1, SHIFT2)):
                sp.wait_ge(mod_ready, n + 1)
                sp.dma_start(mod_stage[n], mod_rows[part]).then_inc(mod_in[n], 16)
            with sp.Fori(0, G - 1) as i:
                sp.wait_ge(t1_ready, i * DT + DT)
                sp.dma_start(xin[:, :, :], x_rows[i + 1]).then_inc(x_in, 16)
            for n, part in enumerate((SCALE2, GATE2)):
                sp.wait_ge(mod_ready, n + 3)
                sp.dma_start(mod_stage[n], mod_rows[part]).then_inc(mod_in[n], 16)
            sp.wait_ge(wt_ready, DT)
            sp.dma_start(xr[:, :, :], x_rows[0]).then_inc(xr_in, 16)

            def store(g):
                for b in range(BLK):
                    sp.wait_ge(out_ready, OUT_FREE + BLK * g + b + 1)
                    sp.dma_start(out_rows[g, b], xr[:, b, :]).then_inc(out_sent, 16)

            with sp.Fori(0, G - 1) as i:
                store(i)
                sp.wait_ge(out_sent, i * (16 * BLK) + 16 * BLK)
                sp.dma_start(xr[:, :, :], x_rows[i + 1]).then_inc(xr_in, 16)
            store(G - 1)
            sp.wait_ge(out_sent, 16 * BLK * G)

        @block.gpsimd
        def _(pool):
            nc.gpsimd.memset(ident[:, :], 0.0).then_inc(ident_done, 1)
            pool.wait_ge(ident_done, 1)
            nc.gpsimd.affine_select(out=ident[:, :], in_=ident[:, :], compare_op=ALU.not_equal, fill=1.0, base=0,
                                    pattern=[[-1, P]], channel_multiplier=1).then_inc(ident_done, 1)
            nc.gpsimd.memset(neg_half[:, :], -0.5).then_inc(const_done, 1)
            nc.gpsimd.memset(f32(halo_hi[:, :, :]), 0.0).then_inc(const_done, 1)
            nc.gpsimd.memset(f32(halo_lo[:, :, :]), 0.0).then_inc(const_done, 1)
            nc.gpsimd.memset(mask[:, :, :], 0.0).then_inc(mask_done, 1)
            nc.gpsimd.memset(credit[:, 0:1], 0.0).then_inc(out_ready, OUT_FREE)

            pool.wait_ge(const_done, 3)
            pool.wait_ge(halo_step, 3)
            nc.gpsimd.tensor_tensor(halo_st[:, 9:10], halo_st[:, 8:9], neg_half[0:2 * NB, 0:1], ALU.pow).then_inc(halo_rstd, 1)

            def rsqrt(var_sem, rstd_sem, g):
                pool.wait_ge(var_sem, g + 1)
                nc.gpsimd.tensor_tensor(rstd[:, :], vare[:, :], neg_half[:, :], ALU.pow).then_inc(rstd_sem, 1)

            def modulation(g, first, last, dst, done):
                b = g // GPB
                nc.gpsimd.tensor_copy(dst, modT[:, first:last, :, bass.ds(b, 1)]).then_inc(done, 1)

            def activations(g, i=None):
                for d in range(DT):
                    n = DT * g + d
                    if i is not None and d < DT - 1:
                        pool.wait_ge(conv_tile, (DT - 1) * i + d + 1)
                    elif i is not None:
                        pool.wait_ge(conv_ready, 3 * i + 3)
                    for hT, halo in ((hT_hi, halo_hi), (hT_lo, halo_lo)):
                        nc.gpsimd.tensor_copy(hT[:, d, 0:GT + 2:GT + 1], halo[:, d, bass.ds(2 * g, 2)]).then_inc(halo_put, 1)
                    pool.wait_ge(h_hid, n + 1)
                    pool.wait_ge(h_full, n + 1)
                    nc.gpsimd.tensor_tensor(hT_lo[:, d, 1:GT + 1], spare[:, d % 2, :], f32(hT_hi[:, d, 1:GT + 1]),
                                            ALU.subtract).then_inc(h_lod, 1)

            rsqrt(var1, rstd1, 0)
            pool.wait_ge(mod_done, 2)
            modulation(0, SHIFT, SCALE1 + 1, cur1[:, :, :, :], cur1_done)
            pool.wait_ge(halo_lod, 1)
            activations(0)
            nc.gpsimd.tensor_copy(ident_b[:, :], ident[:, :]).then_inc(mask_done, 1)
            nc.gpsimd.tensor_copy(ident_h[:, :], ident[:, :]).then_inc(mask_done, 1)
            pool.wait_ge(mask_done, 3)
            nc.gpsimd.affine_select(out=mask[:, :, :], in_=mask[:, :, :], compare_op=ALU.is_ge, fill=NEG_INF, base=0,
                                    pattern=[[0, HB], [-1, P]], channel_multiplier=1).then_inc(mask_done, 1)
            for m in range(3):
                pool.wait_ge(whi_done, m + 1)
                nc.gpsimd.tensor_tensor(wqkv_lo[:, m, :], wqkv_raw[:, m, :], f32(wqkv_hi[:, m, :]), ALU.subtract).then_inc(wlo_done, 1)
            pool.wait_ge(whi_done, 4)
            nc.gpsimd.tensor_tensor(wo_lo[:, :, :], wo_raw, f32(wo_hi[:, :, :]), ALU.subtract).then_inc(wlo_done, 1)
            with pool.Fori(0, G - 1) as i:
                rsqrt(var1, rstd1, i + 1)
                modulation(i + 1, SHIFT, SCALE1 + 1, cur1[:, :, :, :], cur1_done)
                activations(i + 1, i)

            def normalise(g, u):
                for half in range(2):
                    n = 2 * UNITS * g + 2 * u + half + 1
                    pool.wait_ge(inv_done, n)
                    p = prob[:, u % 2, half * HB:(half + 1) * HB, :]
                    r = row_inv[:, u % 2, half * HB:(half + 1) * HB].unsqueeze(2).to_broadcast((P, HB, P))
                    nc.gpsimd.tensor_tensor(p, p, r, ALU.mult).then_inc(norm_done, 1)

            def residual_bias(g, b):
                pool.wait_ge(ga_done, NB)
                pool.wait_ge(xr_in, 16 * g + 16)
                nc.gpsimd.tensor_tensor(xr[:, b, :], xr[:, b, :], pbga_rows[:, bass.ds(g // GPB * D, D)],
                                        ALU.add).then_inc(xrb_done, 1)

            def final_add(g, b):
                pool.wait_ge(gy_done, BLK * g + b + 1)
                nc.gpsimd.tensor_tensor(xr[:, b, :], spare[:, b % 2, :], xr[:, b, :], ALU.add).then_inc(out_ready, 1)

            def attend(g):
                for u in range(2, UNITS):
                    normalise(g, u - 1)
                    if u >= UNITS - BLK:
                        residual_bias(g, u - UNITS + BLK)
                normalise(g, UNITS - 1)
                modulation(g, SCALE2, SCALE2 + 1, cur2[:, :, :, :], cur2_done)
                rsqrt(var2, rstd2, g)

            pool.wait_ge(mod_done, 6)
            pool.wait_ge(ga_done, 2 * NB)
            normalise(0, 0)
            with pool.Fori(0, G - 1) as i:
                attend(i)
                normalise(i + 1, 0)
                for b in range(BLK):
                    final_add(i, b)
            attend(G - 1)
            for b in range(BLK):
                final_add(G - 1, b)

        @block.scalar
        def _(act):
            for m, w in enumerate((wq, wk, wv)):
                act.dma_start(wqkv_raw[:, m, :], w.rearrange("w h e -> w (h e)")).then_inc(wqkv_in, 16)
            act.dma_start(wo_raw, wo_rows).then_inc(wo_in, 16)
            act.dma_start(pw_raw, proj_w).then_inc(pw_in, 16)
            act.dma_start(pb_rows, proj_b.rearrange("(a d) -> a d", a=1).to_broadcast((P, D))).then_inc(pw_in, 16)
            act.dma_start(scales16[:, :, :], ffn_s.rearrange("(o p) g -> p o g", p=P)).then_inc(ffn_in, 16)
            act.dma_start(w_raw16.rearrange("p a n -> p (a n)").rearrange("p (o n) -> p o n", o=BLK),
                          ffn_w.rearrange("(o p) n -> p o n", p=P)).then_inc(ffn_in, 16)
            for r in range(2 * NB):
                act.dma_start(halo_x[r:r + 1, :], x[r // 2, GT - r % 2:GT - r % 2 + 1, :]).then_inc(halo_in, 16)
            act.wait_ge(const_done, 3)
            nc.scalar.copy(credit[:, 2:3], neg_half[:, 0:1]).then_inc(c_done, C_FREE)
            act.wait_ge(cols_done, 1)
            nc.scalar.activation(silu[:, 0, :], cols[:, 0:NC], ACT.Exp, scale=-1.0).then_inc(silu_exp, 1)
            act.wait_ge(cw_in, 16 * TAPS)
            for d in range(DT):
                nc.scalar.copy(cw_hi[:, :, d, :], cw_raw[:, :, d, :]).then_inc(cwhi_done, 1)
            act.wait_ge(halo_step, 6)
            act.wait_ge(const_done, 3)
            nc.scalar.copy(halo_hi[:, :, :].rearrange("p d (b s) -> p d b s", b=NB)[:, :, :, 1:3],
                           halo_f[:, :, :, :]).then_inc(halo_hid, 1)

            def activations(g, tiles, i=None):
                act.wait_ge(cur1_done, g + 1)
                for d in tiles:
                    act.wait_ge(t1_ready, DT * g + d + 1)
                    if i is not None and d < DT - 1:
                        act.wait_ge(conv_tile, (DT - 1) * i + d + 1)
                    elif i is not None:
                        act.wait_ge(conv_ready, 3 * i + 3)
                    nc.scalar.activation(hT_hi[:, d, 1:GT + 1], bank[4 + d % 2][:, :], ACT.Identity,
                                         bias=cur1[:, 0, d, :], scale=cur1[:, 1, d, :]).then_inc(h_hid, 1)

            def conv_out(g):
                for m in range(3):
                    act.wait_ge(conv_ready, 3 * g + m + 1)
                    nc.scalar.activation(cT[:, bass.ds(GT * g + m * T, GT)], bank[m][:, :], ACT.Identity,
                                         bias=cols[:, R_CB + m:R_CB + m + 1]).then_inc(c_done, 1)

            activations(0, range(DT))
            act.wait_ge(wqkv_in, 48)
            for m in range(3):
                nc.scalar.copy(wqkv_hi[:, m, :], wqkv_raw[:, m, :]).then_inc(whi_done, 1)
            act.wait_ge(wo_in, 16)
            nc.scalar.copy(wo_hi[:, :, :], wo_raw).then_inc(whi_done, 1)
            with act.Fori(0, G - 1) as i:
                activations(i + 1, (0, 1), i)
                conv_out(i)
                activations(i + 1, (2, 3), i)
            for b in range(NB):
                act.wait_ge(ga_done, NB + b + 1)
                nc.scalar.copy(pw_hi[:, b * D:(b + 1) * D], pw_tmp[:, b, :]).then_inc(pwhi_done, 1)
            for d in range(DT):
                act.wait_ge(wt_ready, d + 1)
                nc.scalar.copy(wT[:, d, :], bank[(5, 7)[d % 2]][:, :].bitcast(F16)[:, 0:D]).then_inc(wt_done, 1)
            conv_out(G - 1)

            def split(g, m):
                if isinstance(g, int):
                    act.wait_ge(c_done, C_FREE + 3 * G)
                if not isinstance(g, int):
                    if m < 2:
                        act.wait_ge(qk_ready, 2 * JT * (g - 1) + JT * (m + 1))
                    else:
                        act.wait_ge(v_ready, 2 * BLK * (g - 1) + 2 * BLK)
                nc.scalar.copy(cs_hi[:, m, :], cT[:, bass.ds(GT * g + m * T, GT)]).then_inc(cs_hid, 1)

            def qk_even(g, t):
                act.wait_ge(qk_ready, 2 * JT * g + t + 1)
                if t < JT:
                    nc.scalar.activation(qh[:, t, :], bank[t % 4][:, :], ACT.Identity, bias=bq8[:, t:t + 1],
                                         scale=QSCALE).then_inc(qk_act, 1)
                else:
                    nc.scalar.activation(kh[:, t - JT, :], bank[t % 4][:, :], ACT.Identity,
                                         bias=cols[:, R_BK + t - JT:R_BK + t - JT + 1]).then_inc(qk_act, 1)

            def values(g, b):
                act.wait_ge(v_ready, 2 * BLK * g + 2 * b + 1)
                if b >= 2:
                    act.wait_ge(o_ready, UNITS * g + 2 * b - 2)
                elif b == 0 and not isinstance(g, int):
                    act.wait_ge(o_ready, UNITS * (g - 1) + UNITS - 2)
                nc.scalar.copy(vh[:, b % 2, 0:HE // 2], bank[v_use(b, 0) % 4][:, :]).then_inc(v_act, 1)

            def exponentials(g, u):
                for half in range(2):
                    n = 2 * UNITS * g + 2 * u + half + 1
                    act.wait_ge(max_done, n)
                    if u >= 2:
                        act.wait_ge(pt_ready, 2 * UNITS * g + 2 * (u - 2) + half + 1)
                    s = heads_of(bank[s_use(u, half) % 4])
                    for h in range(HB):
                        k = half * HB + h
                        ins = nc.scalar.activation(prob[:, u % 2, k, :], s[:, h, :], ACT.Exp,
                                                   bias=neg_max[:, u % 2, k:k + 1], accum_out=row_sum[:, u % 2, k:k + 1])
                    ins.then_inc(exp_done, 1)

            def o_high(g, u):
                act.wait_ge(o_ready, UNITS * g + u + 1)
                nc.scalar.copy(oT_hi[:, HB * (u % 2):HB * (u % 2 + 1), (u // 2 % 2) * P:(u // 2 % 2 + 1) * P],
                               heads_of(bank[O_BANK[u]])).then_inc(o_hid, 1)

            def y_high(g, k):
                act.wait_ge(wo_ready, 2 * g + k + 1)
                act.wait_ge(by_done, 1)
                nc.scalar.activation(yT_hi[:, 2 * P * k:2 * P * (k + 1)], bank[WO_BANK[k]][:, 0:2 * P], ACT.Identity,
                                     bias=by[:, 0:1]).then_inc(y_hid, 1)

            def h2_high(g):
                act.wait_ge(cur2_done, g + 1)
                for d in range(DT):
                    act.wait_ge(t2_ready, DT * g + d + 1)
                    nc.scalar.activation(h2_hi[:, d, :], bank[6 + d % 2][:, :], ACT.Copy,
                                         scale=cur2[:, 0, d, :]).then_inc(h2_hid, 1)

            def attend(g, ahead=None):
                for u in range(2, UNITS):
                    exponentials(g, u)
                    if u % 2 == 0:
                        values(g, u // 2)
                    if u == 7:
                        y_high(g, 0)
                    if u >= 3:
                        o_high(g, u - 3)
                    if ahead is not None and u in (3, 5):
                        split(ahead, (u - 3) // 2)
                if ahead is not None:
                    split(ahead, 2)
                    qk_even(ahead, 0)
                o_high(g, 5)
                if ahead is not None:
                    qk_even(ahead, 2)
                    qk_even(ahead, 4)
                o_high(g, 6)
                if ahead is not None:
                    qk_even(ahead, 6)
                o_high(g, 7)
                if ahead is not None:
                    qk_even(ahead, 8)
                    qk_even(ahead, 10)
                y_high(g, 1)
                if ahead is not None:
                    qk_even(ahead, 12)
                    qk_even(ahead, 14)

            for b in range(NB):
                act.wait_ge(shift_ready, b + 1)
                nc.scalar.copy(shift_rows[:, b * D:(b + 1) * D], bank[6 + b][:, :]).then_inc(shift_done, 1)
            for m in range(3):
                split(0, m)
            for t in range(0, 2 * JT, 2):
                qk_even(0, t)
            exponentials(0, 0)
            values(0, 0)
            exponentials(0, 1)
            with act.Fori(0, G - 1) as i:
                attend(i, i + 1)
                exponentials(i + 1, 0)
                values(i + 1, 0)
                h2_high(i)
                exponentials(i + 1, 1)
            attend(G - 1)
            h2_high(G - 1)

        @block.vector
        def _(dve):
            nc.vector.memset(credit[:, 1:2], 0.0).then_inc(y16_done, Y16_FREE)
            dve.wait_ge(cols_ready, 1)
            nc.vector.tensor_copy(cols[:, :], bank[6][:, 0:NR]).then_inc(cols_done, 1)
            dve.wait_ge(cols_done, 1)
            nc.vector.tensor_scalar(bq8[:, :], cols[:, R_BQ:R_BK], QSCALE, None, ALU.mult).then_inc(silu_step, 1)
            dve.wait_ge(silu_exp, 1)
            nc.vector.tensor_scalar(silu[:, 1, :], silu[:, 0, :], 1.0, None, ALU.add).then_inc(silu_step, 1)
            dve.wait_ge(silu_step, 2)
            nc.vector.reciprocal(silu[:, 2, :], silu[:, 1, :]).then_inc(silu_step, 1)
            dve.wait_ge(silu_step, 3)
            nc.vector.tensor_tensor(silu[:, 3, :], silu[:, 2, :], cols[:, 0:NC], ALU.mult).then_inc(silu_step, 1)

            def norm_stats(src, g, b, st):
                nc.vector.bn_stats(stats[:, b, :], src[:, b, :]).then_inc(st, 1)

            def norm_variance(g, st, ag, var):
                dve.wait_ge(st, BLK * g + BLK)
                nc.vector.memset(credit[:, 1:2], 0.0)
                for b in range(BLK):
                    nc.vector.bn_aggr(mv[:, b, :], stats[:, b, :]).then_inc(ag, 1)
                dve.wait_ge(ag, BLK * g + BLK)
                nc.vector.tensor_scalar(vare[:, :], mv[:, :, 1], EPS, None, ALU.add).then_inc(var, 1)

            def norm_apply(src, g, rs, done):
                dve.wait_ge(rs, g + 1)
                for b in range(BLK):
                    nc.vector.tensor_scalar(xin[:, b, :], src[:, b, :], mv[:, b, 0:1], rstd[:, b:b + 1],
                                            ALU.subtract, ALU.mult).then_inc(done, 1)

            def norm1(g):
                dve.wait_ge(x_in, 16 * g + 16)
                for b in range(BLK):
                    norm_stats(xin, g, b, st1)
                norm_variance(g, st1, ag1, var1)
                norm_apply(xin, g, rstd1, xn_done)

            dve.wait_ge(halo_in, 16 * 2 * NB)
            nc.vector.bn_stats(halo_st[:, 0:6], halo_x[:, :]).then_inc(halo_step, 1)
            dve.wait_ge(halo_step, 1)
            nc.vector.bn_aggr(halo_st[:, 6:8], halo_st[:, 0:6]).then_inc(halo_step, 1)
            dve.wait_ge(halo_step, 2)
            nc.vector.tensor_scalar(halo_st[:, 8:9], halo_st[:, 7:8], EPS, None, ALU.add).then_inc(halo_step, 1)
            dve.wait_ge(halo_rstd, 1)
            nc.vector.tensor_scalar(halo_x[:, :], halo_x[:, :], halo_st[:, 6:7], halo_st[:, 9:10],
                                    ALU.subtract, ALU.mult).then_inc(halo_step, 1)
            norm1(0)

            def mod_part(n, part):
                dve.wait_ge(mod_ready, n + 1)
                src = bank[6 + n % 2][:, 0:DT * NB].rearrange("p (k b) -> p k b", b=NB)
                if part in (SCALE1, SCALE2):
                    nc.vector.tensor_scalar(modT[:, part], src, 1.0, None, ALU.add).then_inc(mod_done, 1)
                elif part in (SHIFT, SHIFT2):
                    nc.vector.tensor_copy(modT[:, part], src).then_inc(mod_done, 1)
                else:
                    k = 4 * (part == GATE2)
                    nc.vector.tensor_scalar(gate_tmp[:, 0], src, -1.0, GATE_FLOOR, ALU.mult, ALU.max).then_inc(gate_step, 1)
                    nc.vector.tensor_scalar(gate_tmp[:, 1], src, 0.0, 2.0, ALU.is_ge, ALU.mult).then_inc(gate_step, 1)
                    dve.wait_ge(gate_step, k + 2)
                    nc.vector.tensor_scalar(gate_tmp[:, 1], gate_tmp[:, 1], -1.0, None, ALU.add).then_inc(gate_step, 1)
                    nc.vector.tensor_tensor(gate_tmp[:, 0], src, gate_tmp[:, 0], ALU.max).then_inc(gate_step, 1)
                    dve.wait_ge(gate_step, k + 4)
                    nc.vector.tensor_tensor(modT[:, part], gate_tmp[:, 0], gate_tmp[:, 1], ALU.mult).then_inc(mod_done, 1)

            for n, part in enumerate((SCALE1, SHIFT)):
                mod_part(n, part)
            dve.wait_ge(halo_ready, 1)
            dve.wait_ge(mod_done, 2)
            src = bank[5][:, 0:DT * 2 * NB].rearrange("p (k b r) -> p k b r", k=DT, b=NB)
            for k, (part, op, a) in enumerate(((SCALE1, ALU.mult, src), (SHIFT, ALU.add, halo_m[:, :, :, :]))):
                dve.wait_ge(halo_step, 4 + k)
                nc.vector.tensor_tensor((halo_m, halo_f)[k][:, :, :, :], a, modT[:, part].unsqueeze(3).to_broadcast((P, DT, NB, 2)),
                                        op).then_inc(halo_step, 1)
            dve.wait_ge(halo_hid, 1)
            hh, hl = (t[:, :, :].rearrange("p d (b s) -> p d b s", b=NB)[:, :, :, 1:3] for t in (halo_hi, halo_lo))
            nc.vector.tensor_tensor(hl, halo_f[:, :, :, :], f32(hh), ALU.subtract).then_inc(halo_lod, 1)

            def activations(g):
                dve.wait_ge(cur1_done, g + 1)
                for d in range(DT):
                    n = DT * g + d
                    dve.wait_ge(h_hid, n + 1)
                    if not isinstance(g, int) or n >= 2:
                        dve.wait_ge(h_lod, n - 1)
                    nc.vector.tensor_scalar(spare[:, d % 2, :], bank[4 + d % 2][:, :], cur1[:, 1, d, :], cur1[:, 0, d, :],
                                            ALU.mult, ALU.add).then_inc(h_full, 1)

            def cw_low(d):
                dve.wait_ge(cwhi_done, d + 1)
                nc.vector.tensor_tensor(cw_lo[:, :, d, :], cw_raw[:, :, d, :], f32(cw_hi[:, :, d, :]),
                                        ALU.subtract).then_inc(cwlo_done, 1)

            cw_low(0)
            activations(0)
            for d in range(1, DT):
                cw_low(d)
            dve.wait_ge(ffn_in, 32)
            wr = w_raw16.rearrange("p a n -> p (a n)").rearrange("p (o k n) -> p o k n", o=BLK, k=DT)
            ws = w16.rearrange("p a n -> p (a n)").rearrange("p (o k n) -> p o k n", o=BLK, k=DT)
            for o in range(BLK):
                nc.vector.tensor_tensor(ws[:, o], wr[:, o], scales16[:, o, :].unsqueeze(2).to_broadcast((P, DT, P)),
                                        ALU.mult).then_inc(w16_done, 1)
            with dve.Fori(0, G - 1) as i:
                norm1(i + 1)
                activations(i + 1)

            for n, part in ((2, GATE1), (3, SHIFT2), (4, SCALE2), (5, GATE2)):
                mod_part(n, part)
            dve.wait_ge(pw_in, 32)
            for b in range(NB):
                dve.wait_ge(ga_ready, b + 1)
                nc.vector.tensor_tensor(pbga_rows[:, b * D:(b + 1) * D], bank[6 + b][:, :], pb_rows, ALU.mult).then_inc(ga_done, 1)
            for b in range(NB):
                nc.vector.tensor_tensor(pw_tmp[:, b, :], bank[6 + b][:, :], pw_raw, ALU.mult).then_inc(ga_done, 1)
            for b in range(NB):
                dve.wait_ge(gb_ready, b + 1)
                nc.vector.tensor_copy(gb_rows[:, b * D:(b + 1) * D], bank[3 + b][:, :]).then_inc(gb_done, 1)
            for b in range(NB):
                dve.wait_ge(pwhi_done, b + 1)
                nc.vector.tensor_tensor(pw_lo[:, b * D:(b + 1) * D], pw_tmp[:, b, :], f32(pw_hi[:, b * D:(b + 1) * D]),
                                        ALU.subtract).then_inc(pwlo_done, 1)
            dve.wait_ge(by_ready, 1)
            nc.vector.tensor_scalar(by[:, :], bank[3][:, 0:1], cols[:, R_BO:R_BO + 1], None, ALU.add).then_inc(by_done, 1)

            def split(g, m):
                dve.wait_ge(cs_hid, 3 * g + m + 1)
                nc.vector.tensor_tensor(cs_lo[:, m, :], cT[:, bass.ds(GT * g + m * T, GT)], f32(cs_hi[:, m, :]),
                                        ALU.subtract).then_inc(cs_lod, 1)

            def qk_odd(g, t):
                dve.wait_ge(qk_ready, 2 * JT * g + t + 1)
                if t < JT:
                    nc.vector.tensor_scalar(qh[:, t, :], bank[t % 4][:, :], cols[:, R_BQ + t:R_BQ + t + 1], QSCALE,
                                            ALU.add, ALU.mult).then_inc(qk_dve, 1)
                else:
                    nc.vector.tensor_scalar(kh[:, t - JT, :], bank[t % 4][:, :], cols[:, R_BK + t - JT:R_BK + t - JT + 1], None,
                                            ALU.add).then_inc(qk_dve, 1)

            def values(g, b):
                dve.wait_ge(v_ready, 2 * BLK * g + 2 * b + 2)
                if b >= 2:
                    dve.wait_ge(o_ready, UNITS * g + 2 * b - 2)
                elif b == 0 and not isinstance(g, int):
                    dve.wait_ge(o_ready, UNITS * (g - 1) + UNITS - 2)
                nc.vector.tensor_copy(vh[:, b % 2, HE // 2:HE], bank[v_use(b, 1) % 4][:, :]).then_inc(v_dve, 1)

            def maxima(g, u):
                for half in range(2):
                    dve.wait_ge(s_ready, 2 * UNITS * g + 2 * u + half + 1)
                    nc.vector.tensor_reduce(neg_max[:, u % 2, half * HB:(half + 1) * HB], heads_of(bank[s_use(u, half) % 4]),
                                            AX_X, ALU.max, negate=True).then_inc(max_done, 1)

            def inverses(g, u):
                for half in range(2):
                    dve.wait_ge(exp_done, 2 * UNITS * g + 2 * u + half + 1)
                    nc.vector.reciprocal(row_inv[:, u % 2, half * HB:(half + 1) * HB],
                                         row_sum[:, u % 2, half * HB:(half + 1) * HB]).then_inc(inv_done, 1)

            def prob_columns(g, u):
                for half in range(2):
                    dve.wait_ge(pt_ready, 2 * UNITS * g + 2 * u + half + 1)
                    if u >= 2:
                        dve.wait_ge(o_ready, UNITS * g + u - 1)
                    nc.vector.tensor_copy(probT[:, u % 2, half * HB:(half + 1) * HB, :],
                                          heads_of(bank[4 + half])).then_inc(pt_done, 1)

            def o_low(g, u):
                dve.wait_ge(o_hid, UNITS * g + u + 1)
                js, ts = slice(HB * (u % 2), HB * (u % 2 + 1)), slice((u // 2 % 2) * P, (u // 2 % 2 + 1) * P)
                nc.vector.tensor_tensor(oT_lo[:, js, ts], heads_of(bank[O_BANK[u]]), f32(oT_hi[:, js, ts]),
                                        ALU.subtract).then_inc(o_lod, 1)

            def y_low(g, k):
                dve.wait_ge(y_hid, 2 * g + k + 1)
                ts = slice(2 * P * k, 2 * P * (k + 1))
                nc.vector.scalar_tensor_tensor(out=yT_lo[:, ts], in0=bank[WO_BANK[k]][:, 0:2 * P], scalar=by[:, 0:1],
                                               in1=f32(yT_hi[:, ts]), op0=ALU.add, op1=ALU.subtract).then_inc(y_lod, 1)

            def residual(g, b):
                dve.wait_ge(pj_ready, BLK * g + b + 1)
                dve.wait_ge(xrb_done, BLK * g + b + 1)
                nc.vector.tensor_tensor(xr[:, b, :], bank[6 + b % 2][:, :], xr[:, b, :], ALU.add).then_inc(x1_done, 1)
                dve.wait_ge(x1_done, BLK * g + b + 1)
                norm_stats(xr, g, b, st2)

            def h2_low(g):
                for d in range(DT):
                    dve.wait_ge(h2_hid, DT * g + d + 1)
                    nc.vector.scalar_tensor_tensor(out=h2_lo[:, d, :], in0=bank[6 + d % 2][:, :], scalar=cur2[:, 0, d, :],
                                                   in1=f32(h2_hi[:, d, :]), op0=ALU.mult, op1=ALU.subtract).then_inc(h2_lod, 1)

            def ffn_out(g):
                for b in range(BLK):
                    dve.wait_ge(f_ready, BLK * g + b + 1)
                    nc.vector.tensor_tensor(y16[:, b % 2, :], bank[6 + b % 2][:, :], shift_rows[:, bass.ds(g // GPB * D, D)],
                                            ALU.add).then_inc(y16_done, 1)
                    dve.wait_ge(y16_done, Y16_FREE + BLK * g + b + 1)
                    dve.wait_ge(out_ready, BLK * g + b + 1)
                    nc.vector.tensor_tensor(spare[:, b % 2, :], y16[:, b % 2, :], gb_rows[:, bass.ds(g // GPB * D, D)],
                                            ALU.mult).then_inc(gy_done, 1)

            def attend(g, ahead=None):
                for u in range(2, UNITS):
                    maxima(g, u)
                    inverses(g, u - 1)
                    if u % 2 == 0:
                        values(g, u // 2)
                    prob_columns(g, u - 2)
                    if u == 7:
                        y_low(g, 0)
                    if u >= 3:
                        o_low(g, u - 3)
                    if ahead is not None and u in (3, 5):
                        split(ahead, (u - 3) // 2)
                inverses(g, UNITS - 1)
                prob_columns(g, 6)
                if ahead is not None:
                    split(ahead, 2)
                    qk_odd(ahead, 1)
                o_low(g, 5)
                if ahead is not None:
                    qk_odd(ahead, 3)
                prob_columns(g, 7)
                if ahead is not None:
                    qk_odd(ahead, 5)
                o_low(g, 6)
                if ahead is not None:
                    qk_odd(ahead, 7)
                o_low(g, 7)
                if ahead is not None:
                    qk_odd(ahead, 9)
                    qk_odd(ahead, 11)
                y_low(g, 1)
                if ahead is not None:
                    qk_odd(ahead, 13)
                for b in range(BLK):
                    residual(g, b)
                if ahead is not None:
                    qk_odd(ahead, 15)
                norm_variance(g, st2, ag2, var2)

            for m in range(3):
                split(0, m)
            for t in range(1, 2 * JT, 2):
                qk_odd(0, t)
            maxima(0, 0)
            values(0, 0)
            maxima(0, 1)
            inverses(0, 0)
            with dve.Fori(0, G - 1) as i:
                attend(i, i + 1)
                maxima(i + 1, 0)
                norm_apply(xr, i, rstd2, xn2_done)
                values(i + 1, 0)
                maxima(i + 1, 1)
                h2_low(i)
                inverses(i + 1, 0)
                ffn_out(i)
            attend(G - 1)
            norm_apply(xr, G - 1, rstd2, xn2_done)
            h2_low(G - 1)
            ffn_out(G - 1)

        @block.tensor
        def _(pe):
            pe.wait_ge(rows_in, 96)
            pe.wait_ge(ident_done, 2)
            nc.tensor.transpose(bank[6][:, 0:NR], rows[:, :], ident[0:NR, 0:NR]).then_inc(cols_ready, 1)

            def product3(dst, w_hi, w_lo, m_hi, m_lo, start, stop):
                nc.tensor.matmul(dst, w_hi, m_hi, start=start, stop=False)
                nc.tensor.matmul(dst, w_hi, m_lo, start=False, stop=False)
                return nc.tensor.matmul(dst, w_lo, m_hi, start=False, stop=stop)

            def mod_part(n):
                pe.wait_ge(mod_in[n % 2], 16 * (n // 2 + 1))
                if n >= 2:
                    pe.wait_ge(mod_done, n - 1)
                for d in range(DT):
                    for k in range(DT):
                        mm = nc.tensor.matmul(bank[6 + n % 2][:, NB * d:NB * (d + 1)],
                                              mod_stage[n % 2][:, k, d * P:(d + 1) * P],
                                              silu[:, 3, :].rearrange("p (b k) -> p k b", b=NB)[:, k, :],
                                              start=(k == 0), stop=(k == DT - 1))
                mm.then_inc(mod_ready, 1)

            def activations(g, d, i=None):
                n = DT * g + d
                pe.wait_ge(xn_done, BLK * g + BLK)
                if not isinstance(g, int) or n >= 2:
                    pe.wait_ge(h_full, n - 1)
                for b in range(BLK):
                    mm = nc.tensor.transpose(bank[4 + d % 2][:, b * P:(b + 1) * P], xin[:, b, d * P:(d + 1) * P], ident[:, :])
                mm.then_inc(t1_ready, 1)

            pe.wait_ge(silu_step, 4)
            mod_part(0)
            mod_part(1)
            pe.wait_ge(halo_step, 4)
            for d in range(DT):
                mm = nc.tensor.transpose(bank[5][:, 2 * NB * d:2 * NB * (d + 1)], halo_x[:, d * P:(d + 1) * P],
                                         ident[0:2 * NB, 0:2 * NB])
            mm.then_inc(halo_ready, 1)
            activations(0, 0)
            pe.wait_ge(halo_step, 5)
            for d in range(1, DT):
                activations(0, d)

            def conv(g, d):
                pe.wait_ge(h_lod, DT * g + d + 1)
                pe.wait_ge(halo_put, 2 * (DT * g + d) + 2)
                pe.wait_ge(cwlo_done, d + 1)
                for m in range(3):
                    if d == 0:
                        pe.wait_ge(c_done, 3 * g + m + 1)
                    ws = slice(m * W, (m + 1) * W)
                    for t in range(TAPS):
                        mm = product3(bank[m][:, :], cw_hi[:, t, d, ws], cw_lo[:, t, d, ws],
                                      hT_hi[:, d, t:t + GT], hT_lo[:, d, t:t + GT],
                                      d == 0 and t == 0, d == DT - 1 and t == TAPS - 1)
                    if d == DT - 1:
                        mm.then_inc(conv_ready, 1)
                if d < DT - 1:
                    mm.then_inc(conv_tile, 1)

            with pe.Fori(0, G - 1) as i:
                for d in range(DT - 1):
                    conv(i, d)
                activations(i + 1, 0)
                activations(i + 1, 1)
                conv(i, DT - 1)
                activations(i + 1, 2)
                activations(i + 1, 3)

            mod_part(2)
            mod_part(3)
            conv(G - 1, 0)
            mod_part(4)
            mod_part(5)
            conv(G - 1, 1)
            pe.wait_ge(mod_done, 6)
            pe.wait_ge(h_full, DT * G)
            for part, banks, ready in ((GATE1, (6, 7), ga_ready), (GATE2, (3, 4), gb_ready)):
                for b in range(NB):
                    for d in range(DT):
                        mm = nc.tensor.matmul(bank[banks[b]][:, d * P:(d + 1) * P],
                                              modT[:, part, d, b:b + 1].to_broadcast((P, P)), ident[:, :], start=True, stop=True)
                    mm.then_inc(ready, 1)
            conv(G - 1, 2)
            pe.wait_ge(w16_done, BLK)
            pe.wait_ge(mask_done, 3)
            pe.wait_ge(ga_done, 2 * NB)
            w16_rows = w16.rearrange("p a n -> p (a n)").rearrange("p (o n) -> p o n", o=BLK)
            for d in range(DT):
                if d >= 2:
                    pe.wait_ge(wt_done, d - 1)
                for o in range(BLK):
                    mm = nc.tensor.transpose(bank[(5, 7)[d % 2]][:, :].bitcast(F16)[:, o * P:(o + 1) * P],
                                             w16_rows[:, o, d * P:(d + 1) * P], ident_h[:, :])
                mm.then_inc(wt_ready, 1)
            conv(G - 1, DT - 1)
            pe.wait_ge(gb_done, 1)
            pe.wait_ge(wo_in, 16)
            for j in range(JT):
                mm = nc.tensor.matmul(bank[3][:, 0:1], wo_raw[:, j, :], cols[:, R_BV + j:R_BV + j + 1],
                                      start=(j == 0), stop=(j == JT - 1))
            mm.then_inc(by_ready, 1)
            pe.wait_ge(wt_done, DT)
            for b in range(NB):
                for d in range(DT):
                    mm = nc.tensor.matmul(bank[6 + b][:, :], modT[:, SHIFT2, d, b:b + 1].to_broadcast((P, P)),
                                          f32(wT[:, d, :]), start=(d == 0), stop=(d == DT - 1))
                mm.then_inc(shift_ready, 1)

            def bank_read(g, use):
                if use >= 0 or not (isinstance(g, int) and g == 0):
                    pe.wait_ge(*released(g, use))

            def qk_tile(g, t):
                m, j = t // JT, t % JT
                pe.wait_ge(cs_lod, 3 * g + m + 1)
                bank_read(g, qk_use(t) - 4)
                js = slice(j * P, (j + 1) * P)
                product3(bank[t % 4][:, :], wqkv_hi[:, m, js], wqkv_lo[:, m, js], cs_hi[:, m, :], cs_lo[:, m, :],
                         True, True).then_inc(qk_ready, 1)

            def values(g, b):
                pe.wait_ge(cs_lod, 3 * g + 3)
                for half in range(2):
                    bank_read(g, v_use(b, half) - 4)
                    ts, ns = slice(b * P, (b + 1) * P), slice(half * HE // 2, (half + 1) * HE // 2)
                    product3(bank[v_use(b, half) % 4][:, :], cs_hi[:, 2, ts], cs_lo[:, 2, ts], wqkv_hi[:, 2, ns], wqkv_lo[:, 2, ns],
                             True, True).then_inc(v_ready, 1)

            def scores(g, u):
                if u == 0:
                    pe.wait_ge(qk_act, JT * g + JT)
                    pe.wait_ge(qk_dve, JT * g + JT)
                for half in range(2):
                    bank_read(g, s_use(u, half) - 4)
                    nc.tensor.matmul(bank[s_use(u, half) % 4][:, :], ident_b[:, :], mask[:, :, :].rearrange("p h k -> p (h k)"),
                                     start=True, stop=False, skip_group_check=True)
                ts = slice(u // 2 * P, (u // 2 + 1) * P)
                for h in range(HB):
                    for half in range(2):
                        es, j = slice(half * E, (half + 1) * E), HB * (u % 2) + h
                        mm = nc.tensor.matmul(bank[s_use(u, half) % 4][:, h * P:(h + 1) * P], qh[es, j, ts], kh[es, j, ts],
                                              start=False, stop=True, skip_group_check=True)
                        if h == HB - 1:
                            mm.then_inc(s_ready, 1)

            def transpose_probs(g, u):
                for half in range(2):
                    pe.wait_ge(norm_done, 2 * UNITS * g + 2 * u + half + 1)
                    if u >= 1:
                        pe.wait_ge(pt_done, 2 * UNITS * g + 2 * (u - 1) + half + 1)
                    for h in range(HB):
                        mm = nc.tensor.transpose(bank[4 + half][:, h * P:(h + 1) * P], prob[:, u % 2, half * HB + h, :], ident[:, :])
                    mm.then_inc(pt_ready, 1)

            def outputs(g, u):
                pe.wait_ge(pt_done, 2 * UNITS * g + 2 * u + 2)
                if u % 2 == 0:
                    pe.wait_ge(v_act, BLK * g + u // 2 + 1)
                    pe.wait_ge(v_dve, BLK * g + u // 2 + 1)
                if u < 2:
                    pe.wait_ge(y16_done, BLK * g + u + 3)
                elif u == 5:
                    pe.wait_ge(y_lod, 2 * g + 1)
                else:
                    pe.wait_ge(o_lod, UNITS * g + {2: 1, 3: 2, 4: 4, 6: 5, 7: 6}[u])
                for h in range(HB):
                    for half in range(2):
                        head = HU * (u % 2) + 2 * h + half
                        mm = nc.tensor.matmul(bank[O_BANK[u]][half * E:(half + 1) * E, h * P:(h + 1) * P],
                                              vh[:, u // 2 % 2, head * E:(head + 1) * E], probT[:, u % 2, half * HB + h, :],
                                              start=True, stop=True, skip_group_check=True)
                mm.then_inc(o_ready, 1)

            def out_product(g, k):
                pe.wait_ge(o_lod, UNITS * g + 4 * (k + 1))
                for j in range(JT):
                    mm = product3(bank[WO_BANK[k]][:, 0:2 * P], wo_hi[:, j, :], wo_lo[:, j, :], oT_hi[:, j, :], oT_lo[:, j, :],
                                  j == 0, j == JT - 1)
                mm.then_inc(wo_ready, 1)

            def project(g, b):
                if b == 0:
                    pe.wait_ge(y_lod, 2 * g + 2)
                    pe.wait_ge(o_lod, UNITS * g + UNITS)
                elif b >= 2:
                    pe.wait_ge(x1_done, BLK * g + b - 1)
                ts, ds = slice(b * P, (b + 1) * P), bass.ds(g // GPB * D, D)
                product3(bank[6 + b % 2][:, :], yT_hi[:, ts], yT_lo[:, ts], pw_hi[:, ds], pw_lo[:, ds],
                         True, True).then_inc(pj_ready, 1)

            def norm_columns(g):
                for d in range(DT):
                    if d == 0:
                        pe.wait_ge(xn2_done, BLK * g + BLK)
                    if d >= 2:
                        pe.wait_ge(h2_lod, DT * g + d - 1)
                    for b in range(BLK):
                        mm = nc.tensor.transpose(bank[6 + d % 2][:, b * P:(b + 1) * P], xin[:, b, d * P:(d + 1) * P], ident[:, :])
                    mm.then_inc(t2_ready, 1)

            def feed_forward(g, b):
                if b == 0:
                    pe.wait_ge(h2_lod, DT * g + DT)
                elif b >= 2:
                    pe.wait_ge(y16_done, Y16_FREE + BLK * g + b - 1)
                for d in range(DT):
                    for half, h2 in enumerate((h2_hi, h2_lo)):
                        mm = nc.tensor.matmul(bank[6 + b % 2][:, :], h2[:, d, b * P:(b + 1) * P], wT[:, d, :],
                                              start=(d == 0 and half == 0), stop=(d == DT - 1 and half == 1))
                mm.then_inc(f_ready, 1)

            def attend(g, ahead=None):
                def fill(*tiles):
                    if ahead is not None:
                        for t in tiles:
                            qk_tile(ahead, t)

                for u in range(2, UNITS):
                    scores(g, u)
                    transpose_probs(g, u - 2)
                    if u == 7:
                        out_product(g, 0)
                    if u >= 3:
                        outputs(g, u - 3)
                    if u % 2 == 0:
                        values(g, u // 2)
                transpose_probs(g, 6)
                fill(0, 1)
                outputs(g, 5)
                fill(2, 3)
                transpose_probs(g, 7)
                fill(4, 5)
                outputs(g, 6)
                fill(6, 7)
                outputs(g, 7)
                fill(8, 9, 10, 11)
                out_product(g, 1)
                fill(12, 13)
                for b in range(BLK):
                    project(g, b)
                fill(14, 15)

            pe.wait_ge(c_done, C_FREE + 3 * G)
            pe.wait_ge(by_done, 1)
            pe.wait_ge(shift_done, NB)
            pe.wait_ge(pwlo_done, NB)
            pe.wait_ge(gb_done, NB)
            pe.wait_ge(wlo_done, 4)
            pe.wait_ge(mask_done, 4)
            for t in range(2 * JT):
                qk_tile(0, t)
            scores(0, 0)
            values(0, 0)
            scores(0, 1)
            with pe.Fori(0, G - 1) as i:
                attend(i, i + 1)
                scores(i + 1, 0)
                values(i + 1, 0)
                scores(i + 1, 1)
                norm_columns(i)
                for b in range(BLK):
                    feed_forward(i, b)
            attend(G - 1)
            norm_columns(G - 1)
            for b in range(BLK):
                feed_forward(G - 1, b)


_INS = ['L0_attn_inputs', 'L0_attn_conv_w', 'L0_attn_conv_b', 'L0_attn_wq', 'L0_attn_bq', 'L0_attn_wk', 'L0_attn_bk',
        'L0_attn_wv', 'L0_attn_bv', 'L0_attn_wo', 'L0_attn_bo', 'L0_attn_proj_w', 'L0_attn_proj_b', 'L0_ffn_weight',
        'L0_ffn_scales', 'L0_c', 'L0_wmod']


def kernel(**inputs):
    import numpy as _np
    import concourse.bacc as _bacc
    from concourse import mybir as _mybir
    from concourse.bass_utils import run_bass_kernel_spmd as _run

    nc = _bacc.Bacc("TRN2", target_bir_lowering=False, num_devices=1, dynamic_dma_scratch_size=1024)
    arrays, args = {}, []
    for name in _INS:
        a = _np.ascontiguousarray(inputs[name])
        arrays[f"in_{name}_dram"] = a
        args.append(nc.dram_tensor(f"in_{name}_dram", a.shape, _mybir.dt.from_np(a.dtype), kind="ExternalInput").ap())
    shape = inputs['L0_attn_inputs'].shape
    args.append(nc.dram_tensor("out_0_dram", shape, _mybir.dt.float32, kind="ExternalOutput").ap())
    adaln_block(nc, *args)
    r = _run(nc, [arrays], core_ids=[0])
    return r.results[0]["out_0_dram"]
```

```python
from contextlib import ExitStack

import concourse.bass as bass
from concourse import mybir

F32 = mybir.dt.float32
F32R = mybir.dt.float32r
F16 = mybir.dt.float16
BF16 = mybir.dt.bfloat16
ALU = mybir.AluOpType
ACT = mybir.ActivationFunctionType
AX_X = mybir.AxisListType.X

P = 128
EPS = 1e-5
NEG_INF = -1.0e9
GATE_FLOOR = 0.25


def adaln_block(nc, x, conv_w, conv_b, wq, bq, wk, bk, wv, bv, wo, bo, proj_w, proj_b,
                ffn_w, ffn_s, c, wmod, out):
    NB, L, D = x.shape
    TAPS, _, W3 = conv_w.shape
    W = W3 // 3
    _, H, E = wq.shape
    DT = D // P
    GT = 512
    BLK = GT // P
    T = NB * L
    G = T // GT
    GPB = L // GT
    HE = H * E
    JT = HE // P
    UNITS = 2 * BLK
    HU = H // 2
    HB = HU // 2
    QSCALE = float(E) ** -0.5
    assert W == P and E * 2 == P and G == 4 and GPB == 2 and NB == 2 and DT == 4
    SHIFT, SCALE1, GATE1, SHIFT2, SCALE2, GATE2 = range(6)

    x_rows = x.rearrange("b (g k p) d -> (b g) p k d", k=BLK, p=P)
    out_rows = out.rearrange("b (g k p) d -> (b g) k p d", k=BLK, p=P)
    conv_rows = conv_w.rearrange("t (k p) w -> p t k w", p=P)
    mod_rows = wmod.rearrange("(k p) (c n) -> c p k n", p=P, n=D)
    wo_rows = wo.rearrange("h e w -> (h e) w").rearrange("(j p) w -> p j w", p=P)

    with ExitStack() as ctx:
        def sb(name, shape, dt=F32):
            return ctx.enter_context(nc.sbuf_tensor(name, shape, dt))

        def sem(name):
            return ctx.enter_context(nc.semaphore(name))

        bank = [ctx.enter_context(nc.psum_tensor(f"bank{i}", [P, 512], F32)) for i in range(8)]

        half_area = sb("half_area", [P, 2 * TAPS * DT * W3 + 2 * DT * (GT + 2)], F32R)
        n_cw = TAPS * DT * W3

        def area(at, *shape):
            n = 1
            for s in shape:
                n *= s
            v = half_area[:, at:at + n]
            if len(shape) == 3:
                return v.rearrange("p (a b c) -> p a b c", a=shape[0], b=shape[1])
            if len(shape) == 2:
                return v.rearrange("p (a b) -> p a b", a=shape[0])
            return v

        cw_hi, cw_lo = area(0, TAPS, DT, W3), area(n_cw, TAPS, DT, W3)
        hT_hi, hT_lo = area(2 * n_cw, DT, GT + 2), area(2 * n_cw + DT * (GT + 2), DT, GT + 2)
        at = 0
        oT_hi = area(at, JT, 2 * P); at += JT * 2 * P
        oT_lo = area(at, JT, 2 * P); at += JT * 2 * P
        h2_hi = area(at, DT, GT); at += DT * GT
        h2_lo = area(at, DT, GT); at += DT * GT
        yT_hi = area(at, GT); at += GT
        yT_lo = area(at, GT); at += GT
        cs_hi = area(at, 3, GT); at += 3 * GT
        cs_lo = area(at, 3, GT); at += 3 * GT
        assert at <= 2 * n_cw + 2 * DT * (GT + 2)
        wqkv_hi = sb("wqkv_hi", [P, 3, HE], F32R)
        wqkv_lo = sb("wqkv_lo", [P, 3, HE], F32R)
        wo_hi = sb("wo_hi", [P, JT, W], F32R)
        wo_lo = sb("wo_lo", [P, JT, W], F32R)
        pw_hi = sb("pw_hi", [P, NB * D], F32R)
        pw_lo = sb("pw_lo", [P, NB * D], F32R)
        wT = sb("wT", [P, DT, D], F32R)
        halo_hi = sb("halo_hi", [P, DT, 2 * G], F32R)
        halo_lo = sb("halo_lo", [P, DT, 2 * G], F32R)

        work = sb("work", [P, 2 * JT * GT + 2 * HE + 4 * HU * P])
        mod_stage = [work[:, i * DT * D:(i + 1) * DT * D].rearrange("p (k n) -> p k n", k=DT) for i in range(2)]
        at = 2 * DT * D
        cw_raw = work[:, at:at + n_cw].rearrange("p (t k w) -> p t k w", t=TAPS, k=DT)
        pw_tmp = work[:, at:at + NB * D].rearrange("p (b d) -> p b d", b=NB)
        at += n_cw
        wqkv_raw = work[:, at:at + 3 * HE].rearrange("p (m n) -> p m n", m=3); at += 3 * HE
        wo_raw = work[:, at:at + JT * W].rearrange("p (j w) -> p j w", j=JT); at += JT * W
        pw_raw = work[:, at:at + D]; at += D
        pb_rows = work[:, at:at + D]; at += D
        assert at <= work.shape[1]
        at = 0
        qh = work[:, at:at + JT * GT].rearrange("p (j t) -> p j t", j=JT); at += JT * GT
        kh = work[:, at:at + JT * GT].rearrange("p (j t) -> p j t", j=JT); at += JT * GT
        vh = work[:, at:at + 2 * HE].rearrange("p (s n) -> p s n", s=2); at += 2 * HE
        prob = work[:, at:at + 2 * HU * P].rearrange("p (s h k) -> p s h k", s=2, h=HU); at += 2 * HU * P
        probT = work[:, at:at + 2 * HU * P].rearrange("p (s h k) -> p s h k", s=2, h=HU); at += 2 * HU * P
        assert at <= work.shape[1]

        cT = sb("cT", [P, 3 * T])
        xin = sb("xin", [P, BLK, D])
        xr = sb("xr", [P, BLK, D])
        w_raw16 = xr[:, 0:2, :].bitcast(F16)
        w16 = xr[:, 2:4, :].bitcast(F16)
        spare = sb("spare", [P, 2, GT])
        y16 = sb("y16", [P, 2, D], F16)
        gb_rows = sb("gb_rows", [P, NB * D])
        shift_rows = sb("shift_rows", [P, NB * D])
        pbga_rows = sb("pbga_rows", [P, NB * D])
        mask = sb("mask", [P, HB, P], BF16)
        ident = sb("ident", [P, P])
        ident_b = sb("ident_b", [P, P], BF16)
        ident_h = sb("ident_h", [P, P], F16)
        scales16 = sb("scales16", [P, BLK, DT], F16)

        NC = NB * DT
        c_rows = sb("c_rows", [NC, P])
        c_cols = sb("c_cols", [P, NC])
        R_CB, R_BQ, R_BK, R_BV, R_BO, NR = 0, 3, 3 + JT, 3 + 2 * JT, 3 + 3 * JT, 3 + 3 * JT + 1
        rows = sb("rows", [NR, P])
        cols = sb("cols", [P, NR])
        bq8 = sb("bq8", [P, JT])
        by = sb("by", [P, 1])
        silu = sb("silu", [P, 4, NC])
        modT = sb("modT", [P, 6, DT, NB])
        mod_row = gb_rows[0:NB, :].rearrange("p (s n) -> p s n", s=2)
        sb_cols = sb("sb_cols", [P, DT, 2 * NB], F32R)
        sel = sb("sel", [2 * NB, NB])
        shift_row = y16[0:2 * NB, :, :].rearrange("p s n -> p (s n)").bitcast(F32)
        gate_tmp = sb("gate_tmp", [P, 2, DT, NB])
        cur1 = sb("cur1", [P, 2, DT, 1])
        cur2 = sb("cur2", [P, 1, DT, 1])
        halo_x = sb("halo_x", [2 * NB, D])
        halo_f = sb("halo_f", [P, DT, NB, 2])
        halo_m = sb("halo_m", [P, DT, NB, 2])
        halo_st = sb("halo_st", [2 * NB, 12])
        stats = sb("stats", [P, BLK, 6])
        mv = sb("mv", [P, BLK, 2])
        vare = sb("vare", [P, BLK])
        rstd = sb("rstd", [P, BLK])
        neg_half = sb("neg_half", [P, BLK])
        neg_max = sb("neg_max", [P, 2, HU])
        row_sum = sb("row_sum", [P, 2, HU])
        row_inv = sb("row_inv", [P, 2, HU])
        credit = sb("credit", [P, 3])

        rows_in, halo_in, x_in, c_in = sem("rows_in"), sem("halo_in"), sem("x_in"), sem("c_in")
        cw_in = [sem(f"cw_in{d}") for d in range(DT)]
        mod_in = [sem("mod_in0"), sem("mod_in1")]
        wqkv_in, wo_in, pw_in, ffn_in, xr_in, out_sent = (sem("wqkv_in"), sem("wo_in"), sem("pw_in"), sem("ffn_in"),
                                                          sem("xr_in"), sem("out_sent"))
        ident_done, const_done, mask_done = sem("ident_done"), sem("const_done"), sem("mask_done")
        ccols_ready, ccols_done, cols_ready, cols_done, silu_exp, silu_step = (sem("ccols_ready"), sem("ccols_done"), sem("cols_ready"),
                                                                              sem("cols_done"), sem("silu_exp"), sem("silu_step"))
        mod_ready, modrow_done, modcol_ready, mod_done, gate_step = (sem("mod_ready"), sem("modrow_done"), sem("modcol_ready"),
                                                                     sem("mod_done"), sem("gate_step"))
        cwhi_done, cwlo_done = sem("cwhi_done"), sem("cwlo_done")
        whi_done, wlo_done = sem("whi_done"), sem("wlo_done")
        halo_step, halo_rstd, halo_ready, halo_hid, halo_lod = (sem("halo_step"), sem("halo_rstd"), sem("halo_ready"),
                                                                sem("halo_hid"), sem("halo_lod"))
        ga_ready, ga_done, gb_ready, gb_done = sem("ga_ready"), sem("ga_done"), sem("gb_ready"), sem("gb_done")
        pwhi_done, pwlo_done = sem("pwhi_done"), sem("pwlo_done")
        w16_done, wt_ready, wt_done = sem("w16_done"), sem("wt_ready"), sem("wt_done")
        sel_done, sbhi_done, sblo_done, shiftrow_ready, shiftrow_done = (sem("sel_done"), sem("sbhi_done"), sem("sblo_done"),
                                                                         sem("shiftrow_ready"), sem("shiftrow_done"))
        shift_ready, shift_done, by_ready, by_done = sem("shift_ready"), sem("shift_done"), sem("by_ready"), sem("by_done")
        st1, ag1, var1, rstd1, xn_done = sem("st1"), sem("ag1"), sem("var1"), sem("rstd1"), sem("xn_done")
        cur1_done, t1_ready, h_hid, h_full, h_lod, halo_put = (sem("cur1_done"), sem("t1_ready"), sem("h_hid"),
                                                               sem("h_full"), sem("h_lod"), sem("halo_put"))
        conv_tile, conv_ready, c_done = sem("conv_tile"), sem("conv_ready"), sem("c_done")
        cs_hid, cs_lod = sem("cs_hid"), sem("cs_lod")
        qk_ready, qk_act, qk_dve = sem("qk_ready"), sem("qk_act"), sem("qk_dve")
        v_ready, v_act = sem("v_ready"), sem("v_act")
        s_ready, max_done, exp_done, inv_done, norm_done = (sem("s_ready"), sem("max_done"), sem("exp_done"),
                                                            sem("inv_done"), sem("norm_done"))
        pt_ready, pt_done, o_ready, o_hid, o_lod = sem("pt_ready"), sem("pt_done"), sem("o_ready"), sem("o_hid"), sem("o_lod")
        wo_ready, y_hid, y_lod, pj_ready = sem("wo_ready"), sem("y_hid"), sem("y_lod"), sem("pj_ready")
        xrb_done, x1_done = sem("xrb_done"), sem("x1_done")
        st2, ag2, var2, rstd2, xn2_done, cur2_done = (sem("st2"), sem("ag2"), sem("var2"), sem("rstd2"),
                                                      sem("xn2_done"), sem("cur2_done"))
        t2_ready, h2_hid, h2_lod = sem("t2_ready"), sem("h2_hid"), sem("h2_lod")
        f_ready, y16_done, gy_done, out_ready = sem("f_ready"), sem("y16_done"), sem("gy_done"), sem("out_ready")
        Y16_FREE, OUT_FREE, C_FREE = BLK, 2, 3

        def f32(ap):
            return ap.bitcast(F32)

        def heads_of(bank_ap):
            return bank_ap[:, :].rearrange("p (h k) -> p h k", h=HB)

        block = ctx.enter_context(nc.Block())

        def s_bank(u, half):
            return bank[(2 * u + half) % 4]

        USES = 2 * JT + 2 * UNITS
        assert USES % 4 == 0 and 2 * JT % 4 == 0
        QK_DVE = (5, 7, 9, 13)
        QK_ACT = tuple(t for t in range(2 * JT) if t not in QK_DVE)

        def qk_count(tiles, g, upto):
            return len(tiles) * g + sum(t <= upto for t in tiles)

        def released(g, use):
            if use < 0:
                g, use = g - 1, use + USES
            if use < 2 * JT:
                return (qk_dve, qk_count(QK_DVE, g, use)) if use in QK_DVE else (qk_act, qk_count(QK_ACT, g, use))
            return exp_done, 2 * UNITS * g + use - 2 * JT + 1

        TURNS = [("out", 0), ("out", 1), ("out", 2), ("out", 3), ("out", 4), ("wo", 0), ("out", 5), ("proj", 0), ("proj", 1),
                 ("out", 6), ("norm", 0), ("norm", 1), ("out", 7), ("ffn", 0), ("wo", 1), ("ffn", 1), ("proj", 2), ("proj", 3),
                 ("norm", 2), ("norm", 3), ("ffn", 2), ("ffn", 3)]
        assert len(TURNS) % 2 == 0

        def turn_bank(kind, n):
            return bank[6 + TURNS.index((kind, n)) % 2]

        def turn_free(g, kind, n):
            at = TURNS.index((kind, n)) - 2
            kind, n = TURNS[at]
            if at < 0:
                g = g - 1
            if kind == "ffn":
                return y16_done, Y16_FREE + BLK * g + n + 1
            done, of_group, each = {"out": (o_lod, UNITS, 1), "wo": (y_lod, 2, 1), "proj": (x1_done, BLK, 1),
                                    "norm": (h2_lod, 2 * DT, 2)}[kind]
            return done, of_group * g + each * (n + 1)

        @block.sync
        def _(sp):
            sp.dma_start(c_rows[:, :], c.rearrange("b (k p) -> (b k) p", p=P)).then_inc(c_in, 16)
            for r in range(2):
                sp.dma_start(halo_x[NB * r:NB * (r + 1), :], x[:, GT - r, :]).then_inc(halo_in, 16)
            sp.dma_start(mod_stage[0], mod_rows[SCALE1]).then_inc(mod_in[0], 16)
            sp.dma_start(xin[:, :, :], x_rows[0]).then_inc(x_in, 16)
            sp.dma_start(mod_stage[1], mod_rows[SHIFT]).then_inc(mod_in[1], 16)
            for d in range(DT):
                sp.dma_start(cw_raw[:, :, d, :], conv_rows[:, :, d, :]).then_inc(cw_in[d], 16)
            sp.dma_start(rows[R_CB:R_BQ, :], conv_b.rearrange("(m p) -> m p", p=P)).then_inc(rows_in, 16)
            for at, bias in ((R_BQ, bq), (R_BK, bk), (R_BV, bv)):
                sp.dma_start(rows[at:at + JT, :], bias.rearrange("h e -> (h e)").rearrange("(j p) -> j p", p=P)).then_inc(rows_in, 16)
            sp.dma_start(rows[R_BO:NR, :], bo.rearrange("(a p) -> a p", a=1)).then_inc(rows_in, 16)
            for n, part in enumerate((GATE1, SHIFT2)):
                sp.wait_ge(mod_ready, n + 1)
                sp.dma_start(mod_stage[n], mod_rows[part]).then_inc(mod_in[n], 16)
            with sp.Fori(0, G - 1) as i:
                sp.wait_ge(t1_ready, i * DT + DT)
                sp.dma_start(xin[:, :, :], x_rows[i + 1]).then_inc(x_in, 16)
            for n, part in enumerate((SCALE2, GATE2)):
                sp.wait_ge(mod_ready, n + 3)
                sp.dma_start(mod_stage[n], mod_rows[part]).then_inc(mod_in[n], 16)
            sp.wait_ge(wt_ready, DT)
            sp.dma_start(xr[:, :, :], x_rows[0]).then_inc(xr_in, 16)

            def store(g):
                for b in range(BLK):
                    sp.wait_ge(out_ready, OUT_FREE + BLK * g + b + 1)
                    sp.dma_start(out_rows[g, b], xr[:, b, :]).then_inc(out_sent, 16)

            with sp.Fori(0, G - 1) as i:
                store(i)
                sp.wait_ge(out_sent, i * (16 * BLK) + 16 * BLK)
                sp.dma_start(xr[:, :, :], x_rows[i + 1]).then_inc(xr_in, 16)
            store(G - 1)
            sp.wait_ge(out_sent, 16 * BLK * G)

        @block.gpsimd
        def _(pool):
            nc.gpsimd.memset(ident[:, :], 0.0).then_inc(ident_done, 1)
            pool.wait_ge(ident_done, 1)
            nc.gpsimd.affine_select(out=ident[:, :], in_=ident[:, :], compare_op=ALU.not_equal, fill=1.0, base=0,
                                    pattern=[[-1, P]], channel_multiplier=1).then_inc(ident_done, 1)
            nc.gpsimd.memset(neg_half[:, :], -0.5).then_inc(const_done, 1)
            nc.gpsimd.memset(f32(halo_hi[:, :, :]), 0.0).then_inc(const_done, 1)
            nc.gpsimd.memset(f32(halo_lo[:, :, :]), 0.0).then_inc(const_done, 1)
            nc.gpsimd.memset(mask[:, :, :], 0.0).then_inc(mask_done, 1)
            nc.gpsimd.memset(credit[:, 0:1], 0.0).then_inc(out_ready, OUT_FREE)

            pool.wait_ge(const_done, 3)
            pool.wait_ge(halo_step, 3)
            nc.gpsimd.tensor_tensor(halo_st[:, 9:10], halo_st[:, 8:9], neg_half[0:2 * NB, 0:1], ALU.pow).then_inc(halo_rstd, 1)

            def rsqrt(var_sem, rstd_sem, count, first, last):
                pool.wait_ge(var_sem, count)
                nc.gpsimd.tensor_tensor(rstd[:, first:last], vare[:, first:last], neg_half[:, first:last], ALU.pow).then_inc(rstd_sem, 1)

            def modulation(g, first, last, dst, done):
                b = g // GPB
                nc.gpsimd.tensor_copy(dst, modT[:, first:last, :, bass.ds(b, 1)]).then_inc(done, 1)

            def activations(g, i=None):
                for d in range(DT):
                    n = DT * g + d
                    if i is not None and d < DT - 1:
                        pool.wait_ge(conv_tile, (DT - 1) * i + d + 1)
                    elif i is not None:
                        pool.wait_ge(conv_ready, 3 * i + 3)
                    for hT, halo in ((hT_hi, halo_hi), (hT_lo, halo_lo)):
                        nc.gpsimd.tensor_copy(hT[:, d, 0:GT + 2:GT + 1], halo[:, d, bass.ds(2 * g, 2)]).then_inc(halo_put, 1)
                    pool.wait_ge(h_hid, n + 1)
                    pool.wait_ge(h_full, n + 1)
                    nc.gpsimd.tensor_tensor(hT_lo[:, d, 1:GT + 1], spare[:, d % 2, :], f32(hT_hi[:, d, 1:GT + 1]),
                                            ALU.subtract).then_inc(h_lod, 1)

            rsqrt(var1, rstd1, 1, 0, BLK)
            pool.wait_ge(mod_done, 2)
            modulation(0, SHIFT, SCALE1 + 1, cur1[:, :, :, :], cur1_done)
            pool.wait_ge(halo_lod, 1)
            activations(0)
            nc.gpsimd.tensor_copy(ident_b[:, :], ident[:, :]).then_inc(mask_done, 1)
            nc.gpsimd.tensor_copy(ident_h[:, :], ident[:, :]).then_inc(mask_done, 1)
            pool.wait_ge(mask_done, 3)
            nc.gpsimd.affine_select(out=mask[:, :, :], in_=mask[:, :, :], compare_op=ALU.is_ge, fill=NEG_INF, base=0,
                                    pattern=[[0, HB], [-1, P]], channel_multiplier=1).then_inc(mask_done, 1)
            with pool.Fori(0, G - 1) as i:
                rsqrt(var1, rstd1, i + 2, 0, BLK)
                modulation(i + 1, SHIFT, SCALE1 + 1, cur1[:, :, :, :], cur1_done)
                activations(i + 1, i)
            for m in range(3):
                pool.wait_ge(whi_done, m + 1)
                nc.gpsimd.tensor_tensor(wqkv_lo[:, m, :], wqkv_raw[:, m, :], f32(wqkv_hi[:, m, :]), ALU.subtract).then_inc(wlo_done, 1)
            pool.wait_ge(whi_done, 4)
            nc.gpsimd.tensor_tensor(wo_lo[:, :, :], wo_raw, f32(wo_hi[:, :, :]), ALU.subtract).then_inc(wlo_done, 1)

            def normalise(g, u):
                for half in range(2):
                    n = 2 * UNITS * g + 2 * u + half + 1
                    pool.wait_ge(inv_done, n)
                    p = prob[:, u % 2, half * HB:(half + 1) * HB, :]
                    r = row_inv[:, u % 2, half * HB:(half + 1) * HB].unsqueeze(2).to_broadcast((P, HB, P))
                    nc.gpsimd.tensor_tensor(p, p, r, ALU.mult).then_inc(norm_done, 1)

            def residual_bias(g, b):
                pool.wait_ge(ga_done, NB)
                pool.wait_ge(xr_in, 16 * g + 16)
                nc.gpsimd.tensor_tensor(xr[:, b, :], xr[:, b, :], pbga_rows[:, bass.ds(g // GPB * D, D)],
                                        ALU.add).then_inc(xrb_done, 1)

            def final_add(g, b):
                pool.wait_ge(gy_done, BLK * g + b + 1)
                nc.gpsimd.tensor_tensor(xr[:, b, :], spare[:, b % 2, :], xr[:, b, :], ALU.add).then_inc(out_ready, 1)

            def attend(g):
                for u in range(2, UNITS):
                    normalise(g, u - 1)
                    if u >= UNITS - BLK:
                        residual_bias(g, u - UNITS + BLK)
                normalise(g, UNITS - 1)
                modulation(g, SCALE2, SCALE2 + 1, cur2[:, :, :, :], cur2_done)
                rsqrt(var2, rstd2, 2 * g + 1, 0, 2)
                final_add(g, 0)
                final_add(g, 1)
                rsqrt(var2, rstd2, 2 * g + 2, 2, BLK)

            pool.wait_ge(mod_done, 6)
            pool.wait_ge(ga_done, 2 * NB)
            normalise(0, 0)
            with pool.Fori(0, G - 1) as i:
                attend(i)
                normalise(i + 1, 0)
                final_add(i, 2)
                final_add(i, 3)
            attend(G - 1)
            final_add(G - 1, 2)
            final_add(G - 1, 3)

        @block.scalar
        def _(act):
            act.wait_ge(const_done, 3)
            nc.scalar.copy(credit[:, 2:3], neg_half[:, 0:1]).then_inc(c_done, C_FREE)
            act.wait_ge(ccols_done, 1)
            nc.scalar.activation(silu[:, 0, :], c_cols[:, :], ACT.Exp, scale=-1.0).then_inc(silu_exp, 1)
            def mod_rows_out(n):
                act.wait_ge(mod_ready, n + 1)
                if n >= 2:
                    act.wait_ge(modcol_ready, n - 1)
                nc.scalar.copy(mod_row[:, n % 2, :], bank[6 + n % 2][0:NB, :]).then_inc(modrow_done, 1)

            def cw_high(d):
                act.wait_ge(cw_in[d], 16)
                nc.scalar.copy(cw_hi[:, :, d, :], cw_raw[:, :, d, :]).then_inc(cwhi_done, 1)

            mod_rows_out(0)
            cw_high(0)
            mod_rows_out(1)
            act.wait_ge(halo_step, 6)
            act.wait_ge(const_done, 3)
            nc.scalar.copy(halo_hi[:, :, :].rearrange("p d (b s) -> p d b s", b=NB)[:, :, :, 1:3],
                           halo_f[:, :, :, :]).then_inc(halo_hid, 1)

            def activations(g, tiles, i=None):
                act.wait_ge(cur1_done, g + 1)
                for d in tiles:
                    act.wait_ge(t1_ready, DT * g + d + 1)
                    if i is not None and d < DT - 1:
                        act.wait_ge(conv_tile, (DT - 1) * i + d + 1)
                    elif i is not None:
                        act.wait_ge(conv_ready, 3 * i + 3)
                    nc.scalar.activation(hT_hi[:, d, 1:GT + 1], bank[4 + d % 2][:, :], ACT.Identity,
                                         bias=cur1[:, 0, d, :], scale=cur1[:, 1, d, :]).then_inc(h_hid, 1)

            def conv_out(g):
                act.wait_ge(cols_done, 1)
                for m in range(3):
                    act.wait_ge(conv_ready, 3 * g + m + 1)
                    nc.scalar.activation(cT[:, bass.ds(GT * g + m * T, GT)], bank[m][:, :], ACT.Identity,
                                         bias=cols[:, R_CB + m:R_CB + m + 1]).then_inc(c_done, 1)

            activations(0, (0, 1))
            for d in range(1, DT):
                cw_high(d)
                if d >= 2:
                    activations(0, (d,))
            for m, w in enumerate((wq, wk, wv)):
                act.dma_start(wqkv_raw[:, m, :], w.rearrange("w h e -> w (h e)")).then_inc(wqkv_in, 16)
            act.dma_start(wo_raw, wo_rows).then_inc(wo_in, 16)
            act.dma_start(pw_raw, proj_w).then_inc(pw_in, 16)
            act.dma_start(pb_rows, proj_b.rearrange("(a d) -> a d", a=1).to_broadcast((P, D))).then_inc(pw_in, 16)
            act.dma_start(scales16[:, :, :], ffn_s.rearrange("(o p) g -> p o g", p=P)).then_inc(ffn_in, 16)
            act.dma_start(w_raw16.rearrange("p a n -> p (a n)").rearrange("p (o n) -> p o n", o=BLK),
                          ffn_w.rearrange("(o p) n -> p o n", p=P)).then_inc(ffn_in, 16)
            act.wait_ge(wqkv_in, 48)
            for m in range(3):
                nc.scalar.copy(wqkv_hi[:, m, :], wqkv_raw[:, m, :]).then_inc(whi_done, 1)
            act.wait_ge(wo_in, 16)
            nc.scalar.copy(wo_hi[:, :, :], wo_raw).then_inc(whi_done, 1)
            with act.Fori(0, G - 1) as i:
                activations(i + 1, (0, 1), i)
                conv_out(i)
                activations(i + 1, (2, 3), i)
            for n in range(2, 6):
                mod_rows_out(n)
            act.wait_ge(mod_done, 4)
            nc.scalar.copy(sb_cols[:, :, 0:NB], modT[:, SHIFT2]).then_inc(sbhi_done, 1)
            for d in range(DT):
                act.wait_ge(wt_ready, d + 1)
                nc.scalar.copy(wT[:, d, :], bank[4 + d % 2][:, :].bitcast(F16)[:, 0:D]).then_inc(wt_done, 1)
            for b in range(NB):
                act.wait_ge(ga_done, NB + b + 1)
                nc.scalar.copy(pw_hi[:, b * D:(b + 1) * D], pw_tmp[:, b, :]).then_inc(pwhi_done, 1)
            conv_out(G - 1)

            def split(g, m):
                if isinstance(g, int):
                    act.wait_ge(c_done, C_FREE + 3 * G)
                if not isinstance(g, int):
                    if m < 2:
                        act.wait_ge(qk_ready, 2 * JT * (g - 1) + JT * (m + 1))
                    else:
                        act.wait_ge(v_ready, UNITS * (g - 1) + UNITS)
                nc.scalar.copy(cs_hi[:, m, :], cT[:, bass.ds(GT * g + m * T, GT)]).then_inc(cs_hid, 1)

            def qk_out(g, t):
                act.wait_ge(qk_ready, 2 * JT * g + t + 1)
                if t < JT:
                    nc.scalar.activation(qh[:, t, :], bank[t % 4][:, :], ACT.Identity, bias=bq8[:, t:t + 1],
                                         scale=QSCALE).then_inc(qk_act, 1)
                else:
                    nc.scalar.activation(kh[:, t - JT, :], bank[t % 4][:, :], ACT.Identity,
                                         bias=cols[:, R_BK + t - JT:R_BK + t - JT + 1]).then_inc(qk_act, 1)

            def values(g, u):
                act.wait_ge(v_ready, UNITS * g + u + 1)
                nc.scalar.copy(vh[:, u // 2 % 2, u % 2 * HE // 2:(u % 2 + 1) * HE // 2], bank[4][:, :]).then_inc(v_act, 1)

            def exponentials(g, u):
                for half in range(2):
                    n = 2 * UNITS * g + 2 * u + half + 1
                    act.wait_ge(max_done, n)
                    if u >= 2:
                        act.wait_ge(pt_ready, 2 * UNITS * g + 2 * (u - 2) + half + 1)
                    s = heads_of(s_bank(u, half))
                    for h in range(HB):
                        k = half * HB + h
                        ins = nc.scalar.activation(prob[:, u % 2, k, :], s[:, h, :], ACT.Exp,
                                                   bias=neg_max[:, u % 2, k:k + 1], accum_out=row_sum[:, u % 2, k:k + 1])
                    ins.then_inc(exp_done, 1)

            def o_high(g, u):
                act.wait_ge(o_ready, UNITS * g + u + 1)
                if u == 4:
                    act.wait_ge(wo_ready, 2 * g + 1)
                nc.scalar.copy(oT_hi[:, HB * (u % 2):HB * (u % 2 + 1), (u // 2 % 2) * P:(u // 2 % 2 + 1) * P],
                               heads_of(turn_bank("out", u))).then_inc(o_hid, 1)

            def y_high(g, k):
                act.wait_ge(wo_ready, 2 * g + k + 1)
                act.wait_ge(by_done, 1)
                nc.scalar.activation(yT_hi[:, 2 * P * k:2 * P * (k + 1)], turn_bank("wo", k)[:, 0:2 * P], ACT.Identity,
                                     bias=by[:, 0:1]).then_inc(y_hid, 1)

            def h2_high(g, n):
                act.wait_ge(cur2_done, g + 1)
                act.wait_ge(t2_ready, 4 * g + n + 1)
                for e in range(2):
                    d = 2 * (n % 2) + e
                    nc.scalar.activation(h2_hi[:, d, n // 2 * 2 * P:(n // 2 + 1) * 2 * P],
                                         turn_bank("norm", n)[:, e * 2 * P:(e + 1) * 2 * P], ACT.Copy,
                                         scale=cur2[:, 0, d, :]).then_inc(h2_hid, 1)

            def attend(g, ahead=None):
                def fill(*tiles):
                    if ahead is not None:
                        for t in tiles:
                            qk_out(ahead, t)

                for u in range(2, UNITS):
                    values(g, u)
                    exponentials(g, u)
                    if u == 7:
                        y_high(g, 0)
                    if u >= 3:
                        o_high(g, u - 3)
                    if ahead is not None and u in (3, 5):
                        split(ahead, (u - 3) // 2)
                if ahead is not None:
                    split(ahead, 2)
                fill(0, 1)
                o_high(g, 5)
                fill(2, 3)
                o_high(g, 6)
                fill(4, 6)
                h2_high(g, 0)
                h2_high(g, 1)
                fill(8)
                o_high(g, 7)
                y_high(g, 1)
                fill(10, 11, 12, 14, 15)

            for m in range(3):
                split(0, m)
            for t in QK_ACT:
                qk_out(0, t)
                if t == 0:
                    act.wait_ge(shiftrow_ready, 1)
                    nc.scalar.copy(shift_row[:, :], bank[6][0:2 * NB, :]).then_inc(shiftrow_done, 1)
            for b in range(NB):
                act.wait_ge(shift_ready, b + 1)
                nc.scalar.copy(shift_rows[:, b * D:(b + 1) * D], bank[(7, 4)[b]][:, :]).then_inc(shift_done, 1)
            values(0, 0)
            exponentials(0, 0)
            values(0, 1)
            exponentials(0, 1)
            with act.Fori(0, G - 1) as i:
                attend(i, i + 1)
                values(i + 1, 0)
                h2_high(i, 2)
                h2_high(i, 3)
                exponentials(i + 1, 0)
                values(i + 1, 1)
                exponentials(i + 1, 1)
            attend(G - 1)
            h2_high(G - 1, 2)
            h2_high(G - 1, 3)

        @block.vector
        def _(dve):
            nc.vector.memset(credit[:, 1:2], 0.0).then_inc(y16_done, Y16_FREE)
            dve.wait_ge(ccols_ready, 1)
            nc.vector.tensor_copy(c_cols[:, :], bank[6][:, 0:NC]).then_inc(ccols_done, 1)
            dve.wait_ge(silu_exp, 1)
            nc.vector.tensor_scalar(silu[:, 1, :], silu[:, 0, :], 1.0, None, ALU.add).then_inc(silu_step, 1)
            dve.wait_ge(silu_step, 1)
            nc.vector.reciprocal(silu[:, 2, :], silu[:, 1, :]).then_inc(silu_step, 1)
            dve.wait_ge(silu_step, 2)
            nc.vector.tensor_tensor(silu[:, 3, :], silu[:, 2, :], c_cols[:, :], ALU.mult).then_inc(silu_step, 1)

            def norm_stats(src, g, b, st):
                nc.vector.bn_stats(stats[:, b, :], src[:, b, :]).then_inc(st, 1)

            def norm_variance(g, st, ag, var, first=0, last=BLK):
                dve.wait_ge(st, BLK * g + last)
                nc.vector.memset(credit[:, 1:2], 0.0)
                for b in range(first, last):
                    nc.vector.bn_aggr(mv[:, b, :], stats[:, b, :]).then_inc(ag, 1)
                dve.wait_ge(ag, BLK * g + last)
                nc.vector.tensor_scalar(vare[:, first:last], mv[:, first:last, 1], EPS, None, ALU.add).then_inc(var, 1)

            def norm_apply(src, rs, count, done, first=0, last=BLK):
                dve.wait_ge(rs, count)
                for b in range(first, last):
                    nc.vector.tensor_scalar(xin[:, b, :], src[:, b, :], mv[:, b, 0:1], rstd[:, b:b + 1],
                                            ALU.subtract, ALU.mult).then_inc(done, 1)

            def norm1(g):
                dve.wait_ge(x_in, 16 * g + 16)
                for b in range(BLK):
                    norm_stats(xin, g, b, st1)
                norm_variance(g, st1, ag1, var1)
                norm_apply(xin, rstd1, g + 1, xn_done)

            dve.wait_ge(halo_in, 16 * 2)
            nc.vector.bn_stats(halo_st[:, 0:6], halo_x[:, :]).then_inc(halo_step, 1)
            dve.wait_ge(halo_step, 1)
            nc.vector.bn_aggr(halo_st[:, 6:8], halo_st[:, 0:6]).then_inc(halo_step, 1)
            dve.wait_ge(halo_step, 2)
            nc.vector.tensor_scalar(halo_st[:, 8:9], halo_st[:, 7:8], EPS, None, ALU.add).then_inc(halo_step, 1)
            dve.wait_ge(halo_rstd, 1)
            nc.vector.tensor_scalar(halo_x[:, :], halo_x[:, :], halo_st[:, 6:7], halo_st[:, 9:10],
                                    ALU.subtract, ALU.mult).then_inc(halo_step, 1)
            norm1(0)

            def mod_part(n, part):
                dve.wait_ge(modcol_ready, n + 1)
                src = bank[6 + n % 2][:, 0:DT * NB].rearrange("p (k b) -> p k b", b=NB)
                if part in (SCALE1, SCALE2):
                    nc.vector.tensor_scalar(modT[:, part], src, 1.0, None, ALU.add).then_inc(mod_done, 1)
                elif part in (SHIFT, SHIFT2):
                    nc.vector.tensor_copy(modT[:, part], src).then_inc(mod_done, 1)
                else:
                    k = 4 * (part == GATE2)
                    nc.vector.tensor_scalar(gate_tmp[:, 0], src, -1.0, GATE_FLOOR, ALU.mult, ALU.max).then_inc(gate_step, 1)
                    nc.vector.tensor_scalar(gate_tmp[:, 1], src, 0.0, 2.0, ALU.is_ge, ALU.mult).then_inc(gate_step, 1)
                    dve.wait_ge(gate_step, k + 2)
                    nc.vector.tensor_scalar(gate_tmp[:, 1], gate_tmp[:, 1], -1.0, None, ALU.add).then_inc(gate_step, 1)
                    nc.vector.tensor_tensor(gate_tmp[:, 0], src, gate_tmp[:, 0], ALU.max).then_inc(gate_step, 1)
                    dve.wait_ge(gate_step, k + 4)
                    nc.vector.tensor_tensor(modT[:, part], gate_tmp[:, 0], gate_tmp[:, 1], ALU.mult).then_inc(mod_done, 1)

            def cw_low(d):
                dve.wait_ge(cwhi_done, d + 1)
                nc.vector.tensor_tensor(cw_lo[:, :, d, :], cw_raw[:, :, d, :], f32(cw_hi[:, :, d, :]),
                                        ALU.subtract).then_inc(cwlo_done, 1)

            mod_part(0, SCALE1)
            cw_low(0)
            mod_part(1, SHIFT)
            dve.wait_ge(halo_ready, 1)
            dve.wait_ge(mod_done, 2)
            src = bank[5][:, 0:DT * 2 * NB].rearrange("p (k r b) -> p k b r", k=DT, b=NB)
            for k, (part, op, a) in enumerate(((SCALE1, ALU.mult, src), (SHIFT, ALU.add, halo_m[:, :, :, :]))):
                dve.wait_ge(halo_step, 4 + k)
                nc.vector.tensor_tensor((halo_m, halo_f)[k][:, :, :, :], a, modT[:, part].unsqueeze(3).to_broadcast((P, DT, NB, 2)),
                                        op).then_inc(halo_step, 1)
            dve.wait_ge(halo_hid, 1)
            hh, hl = (t[:, :, :].rearrange("p d (b s) -> p d b s", b=NB)[:, :, :, 1:3] for t in (halo_hi, halo_lo))
            nc.vector.tensor_tensor(hl, halo_f[:, :, :, :], f32(hh), ALU.subtract).then_inc(halo_lod, 1)

            def activations(g):
                dve.wait_ge(cur1_done, g + 1)
                for d in range(DT):
                    n = DT * g + d
                    dve.wait_ge(h_hid, n + 1)
                    if not isinstance(g, int) or n >= 2:
                        dve.wait_ge(h_lod, n - 1)
                    nc.vector.tensor_scalar(spare[:, d % 2, :], bank[4 + d % 2][:, :], cur1[:, 1, d, :], cur1[:, 0, d, :],
                                            ALU.mult, ALU.add).then_inc(h_full, 1)

            activations(0)
            for d in range(1, DT):
                cw_low(d)
            dve.wait_ge(cols_ready, 1)
            nc.vector.tensor_copy(cols[:, :], bank[3][:, 0:NR]).then_inc(cols_done, 1)
            dve.wait_ge(cols_done, 1)
            nc.vector.tensor_scalar(bq8[:, :], cols[:, R_BQ:R_BK], QSCALE, None, ALU.mult).then_inc(cols_done, 1)
            with dve.Fori(0, G - 1) as i:
                norm1(i + 1)
                activations(i + 1)

            dve.wait_ge(ffn_in, 32)
            wr = w_raw16.rearrange("p a n -> p (a n)").rearrange("p (o k n) -> p o k n", o=BLK, k=DT)
            ws = w16.rearrange("p a n -> p (a n)").rearrange("p (o k n) -> p o k n", o=BLK, k=DT)
            for o in range(BLK):
                nc.vector.tensor_tensor(ws[:, o], wr[:, o], scales16[:, o, :].unsqueeze(2).to_broadcast((P, DT, P)),
                                        ALU.mult).then_inc(w16_done, 1)
            for n, part in ((2, GATE1), (3, SHIFT2), (4, SCALE2), (5, GATE2)):
                mod_part(n, part)
            dve.wait_ge(pw_in, 32)
            for b in range(NB):
                dve.wait_ge(ga_ready, b + 1)
                nc.vector.tensor_tensor(pbga_rows[:, b * D:(b + 1) * D], bank[6 + b][:, :], pb_rows, ALU.mult).then_inc(ga_done, 1)
            for b in range(NB):
                nc.vector.tensor_tensor(pw_tmp[:, b, :], bank[6 + b][:, :], pw_raw, ALU.mult).then_inc(ga_done, 1)
            for b in range(NB):
                dve.wait_ge(gb_ready, b + 1)
                nc.vector.tensor_copy(gb_rows[:, b * D:(b + 1) * D], bank[3 + b][:, :]).then_inc(gb_done, 1)
            dve.wait_ge(sbhi_done, 1)
            nc.vector.tensor_tensor(sb_cols[:, :, NB:2 * NB], modT[:, SHIFT2], f32(sb_cols[:, :, 0:NB]), ALU.subtract).then_inc(sblo_done, 1)
            nc.vector.tensor_tensor(sel[:, :], ident[0:2 * NB, 0:NB], ident[0:2 * NB, NB:2 * NB], ALU.add).then_inc(sel_done, 1)
            for b in range(NB):
                dve.wait_ge(pwhi_done, b + 1)
                nc.vector.tensor_tensor(pw_lo[:, b * D:(b + 1) * D], pw_tmp[:, b, :], f32(pw_hi[:, b * D:(b + 1) * D]),
                                        ALU.subtract).then_inc(pwlo_done, 1)
            dve.wait_ge(by_ready, 1)
            nc.vector.tensor_scalar(by[:, :], bank[5][:, 0:1], cols[:, R_BO:R_BO + 1], None, ALU.add).then_inc(by_done, 1)

            def split(g, m):
                dve.wait_ge(cs_hid, 3 * g + m + 1)
                nc.vector.tensor_tensor(cs_lo[:, m, :], cT[:, bass.ds(GT * g + m * T, GT)], f32(cs_hi[:, m, :]),
                                        ALU.subtract).then_inc(cs_lod, 1)

            def qk_out(g, t):
                dve.wait_ge(qk_ready, 2 * JT * g + t + 1)
                if t < JT:
                    nc.vector.tensor_scalar(qh[:, t, :], bank[t % 4][:, :], cols[:, R_BQ + t:R_BQ + t + 1], QSCALE,
                                            ALU.add, ALU.mult).then_inc(qk_dve, 1)
                else:
                    nc.vector.tensor_scalar(kh[:, t - JT, :], bank[t % 4][:, :], cols[:, R_BK + t - JT:R_BK + t - JT + 1], None,
                                            ALU.add).then_inc(qk_dve, 1)

            def maxima(g, u):
                for half in range(2):
                    dve.wait_ge(s_ready, 2 * UNITS * g + 2 * u + half + 1)
                    nc.vector.tensor_reduce(neg_max[:, u % 2, half * HB:(half + 1) * HB], heads_of(s_bank(u, half)),
                                            AX_X, ALU.max, negate=True).then_inc(max_done, 1)

            def inverses(g, u):
                for half in range(2):
                    dve.wait_ge(exp_done, 2 * UNITS * g + 2 * u + half + 1)
                    nc.vector.reciprocal(row_inv[:, u % 2, half * HB:(half + 1) * HB],
                                         row_sum[:, u % 2, half * HB:(half + 1) * HB]).then_inc(inv_done, 1)

            def prob_columns(g, u):
                for half in range(2):
                    dve.wait_ge(pt_ready, 2 * UNITS * g + 2 * u + half + 1)
                    if u >= 2:
                        dve.wait_ge(o_ready, UNITS * g + u - 1)
                    nc.vector.tensor_copy(probT[:, u % 2, half * HB:(half + 1) * HB, :],
                                          heads_of(bank[4 + half])).then_inc(pt_done, 1)

            def o_low(g, u):
                dve.wait_ge(o_hid, UNITS * g + u + 1)
                js, ts = slice(HB * (u % 2), HB * (u % 2 + 1)), slice((u // 2 % 2) * P, (u // 2 % 2 + 1) * P)
                nc.vector.tensor_tensor(oT_lo[:, js, ts], heads_of(turn_bank("out", u)), f32(oT_hi[:, js, ts]),
                                        ALU.subtract).then_inc(o_lod, 1)

            def y_low(g, k):
                dve.wait_ge(y_hid, 2 * g + k + 1)
                ts = slice(2 * P * k, 2 * P * (k + 1))
                nc.vector.scalar_tensor_tensor(out=yT_lo[:, ts], in0=turn_bank("wo", k)[:, 0:2 * P], scalar=by[:, 0:1],
                                               in1=f32(yT_hi[:, ts]), op0=ALU.add, op1=ALU.subtract).then_inc(y_lod, 1)

            def residual(g, b):
                dve.wait_ge(pj_ready, BLK * g + b + 1)
                dve.wait_ge(xrb_done, BLK * g + b + 1)
                nc.vector.tensor_tensor(xr[:, b, :], turn_bank("proj", b)[:, :], xr[:, b, :], ALU.add).then_inc(x1_done, 1)
                dve.wait_ge(x1_done, BLK * g + b + 1)
                norm_stats(xr, g, b, st2)

            def h2_low(g, n):
                dve.wait_ge(h2_hid, 2 * DT * g + 2 * n + 2)
                for e in range(2):
                    d, ts = 2 * (n % 2) + e, slice(n // 2 * 2 * P, (n // 2 + 1) * 2 * P)
                    nc.vector.scalar_tensor_tensor(out=h2_lo[:, d, ts], in0=turn_bank("norm", n)[:, e * 2 * P:(e + 1) * 2 * P],
                                                   scalar=cur2[:, 0, d, :], in1=f32(h2_hi[:, d, ts]), op0=ALU.mult,
                                                   op1=ALU.subtract).then_inc(h2_lod, 1)

            def ffn_out(g, b):
                dve.wait_ge(f_ready, BLK * g + b + 1)
                nc.vector.tensor_tensor(y16[:, b % 2, :], turn_bank("ffn", b)[:, :], shift_rows[:, bass.ds(g // GPB * D, D)],
                                        ALU.add).then_inc(y16_done, 1)
                dve.wait_ge(y16_done, Y16_FREE + BLK * g + b + 1)
                dve.wait_ge(out_ready, BLK * g + b + 1)
                nc.vector.tensor_tensor(spare[:, b % 2, :], y16[:, b % 2, :], gb_rows[:, bass.ds(g // GPB * D, D)],
                                        ALU.mult).then_inc(gy_done, 1)

            def attend(g, ahead=None):
                def fill(*tiles):
                    if ahead is not None:
                        for t in tiles:
                            qk_out(ahead, t)

                for u in range(2, UNITS):
                    maxima(g, u)
                    inverses(g, u - 1)
                    prob_columns(g, u - 2)
                    if 3 <= u < 7:
                        o_low(g, u - 3)
                    if ahead is not None and u in (3, 5):
                        split(ahead, (u - 3) // 2)
                inverses(g, UNITS - 1)
                prob_columns(g, 6)
                y_low(g, 0)
                o_low(g, 4)
                if ahead is not None:
                    split(ahead, 2)
                o_low(g, 5)
                prob_columns(g, 7)
                residual(g, 0)
                residual(g, 1)
                norm_variance(g, st2, ag2, var2, 0, 2)
                o_low(g, 6)
                fill(5)
                norm_apply(xr, rstd2, 2 * g + 1, xn2_done, 0, 2)
                fill(7)
                h2_low(g, 0)
                h2_low(g, 1)
                fill(9)
                o_low(g, 7)
                ffn_out(g, 0)
                y_low(g, 1)
                ffn_out(g, 1)
                residual(g, 2)
                residual(g, 3)
                norm_variance(g, st2, ag2, var2, 2, BLK)
                fill(13)
                norm_apply(xr, rstd2, 2 * g + 2, xn2_done, 2, BLK)

            for m in range(3):
                split(0, m)
            for t in QK_DVE:
                qk_out(0, t)
            maxima(0, 0)
            maxima(0, 1)
            inverses(0, 0)
            with dve.Fori(0, G - 1) as i:
                attend(i, i + 1)
                maxima(i + 1, 0)
                h2_low(i, 2)
                h2_low(i, 3)
                maxima(i + 1, 1)
                inverses(i + 1, 0)
                ffn_out(i, 2)
                ffn_out(i, 3)
            attend(G - 1)
            h2_low(G - 1, 2)
            h2_low(G - 1, 3)
            ffn_out(G - 1, 2)
            ffn_out(G - 1, 3)

        @block.tensor
        def _(pe):
            pe.wait_ge(c_in, 16)
            pe.wait_ge(ident_done, 2)
            nc.tensor.transpose(bank[6][:, 0:NC], c_rows[:, :], ident[0:NC, 0:NC]).then_inc(ccols_ready, 1)

            def product3(dst, w_hi, w_lo, m_hi, m_lo, start, stop):
                nc.tensor.matmul(dst, w_hi, m_hi, start=start, stop=False)
                nc.tensor.matmul(dst, w_hi, m_lo, start=False, stop=False)
                return nc.tensor.matmul(dst, w_lo, m_hi, start=False, stop=stop)

            def mod_part(n):
                pe.wait_ge(mod_in[n % 2], 16 * (n // 2 + 1))
                if n >= 2:
                    pe.wait_ge(mod_done, n - 1)
                for k in range(DT):
                    mm = nc.tensor.matmul(bank[6 + n % 2][0:NB, :], silu[:, 3, :].rearrange("p (b k) -> p k b", b=NB)[:, k, :],
                                          mod_stage[n % 2][:, k, :], start=(k == 0), stop=(k == DT - 1))
                mm.then_inc(mod_ready, 1)

            def mod_columns(n):
                pe.wait_ge(modrow_done, n + 1)
                for d in range(DT):
                    mm = nc.tensor.transpose(bank[6 + n % 2][:, NB * d:NB * (d + 1)], mod_row[:, n % 2, d * P:(d + 1) * P],
                                             ident[0:NB, 0:NB])
                mm.then_inc(modcol_ready, 1)

            def activations(g, d, i=None):
                n = DT * g + d
                pe.wait_ge(xn_done, BLK * g + BLK)
                if not isinstance(g, int) or n >= 2:
                    pe.wait_ge(h_full, n - 1)
                for b in range(BLK):
                    mm = nc.tensor.transpose(bank[4 + d % 2][:, b * P:(b + 1) * P], xin[:, b, d * P:(d + 1) * P], ident[:, :])
                mm.then_inc(t1_ready, 1)

            pe.wait_ge(silu_step, 3)
            mod_part(0)
            mod_part(1)
            mod_columns(0)
            activations(0, 0)
            mod_columns(1)
            pe.wait_ge(halo_step, 4)
            for d in range(DT):
                mm = nc.tensor.transpose(bank[5][:, 2 * NB * d:2 * NB * (d + 1)], halo_x[:, d * P:(d + 1) * P],
                                         ident[0:2 * NB, 0:2 * NB])
            mm.then_inc(halo_ready, 1)
            pe.wait_ge(halo_step, 5)
            for d in range(1, DT):
                activations(0, d)

            def conv(g, d):
                pe.wait_ge(h_lod, DT * g + d + 1)
                pe.wait_ge(halo_put, 2 * (DT * g + d) + 2)
                pe.wait_ge(cwlo_done, d + 1)
                for m in range(3):
                    if d == 0:
                        pe.wait_ge(c_done, 3 * g + m + 1)
                    ws = slice(m * W, (m + 1) * W)
                    for t in range(TAPS):
                        mm = product3(bank[m][:, :], cw_hi[:, t, d, ws], cw_lo[:, t, d, ws],
                                      hT_hi[:, d, t:t + GT], hT_lo[:, d, t:t + GT],
                                      d == 0 and t == 0, d == DT - 1 and t == TAPS - 1)
                    if d == DT - 1:
                        mm.then_inc(conv_ready, 1)
                if d < DT - 1:
                    mm.then_inc(conv_tile, 1)

            pe.wait_ge(rows_in, 80)
            nc.tensor.transpose(bank[3][:, 0:NR], rows[:, :], ident[0:NR, 0:NR]).then_inc(cols_ready, 1)
            with pe.Fori(0, G - 1) as i:
                for d in range(DT - 1):
                    conv(i, d)
                activations(i + 1, 0)
                activations(i + 1, 1)
                conv(i, DT - 1)
                activations(i + 1, 2)
                activations(i + 1, 3)

            mod_part(2)
            mod_part(3)
            conv(G - 1, 0)
            mod_columns(2)
            mod_columns(3)
            conv(G - 1, 1)
            mod_part(4)
            mod_part(5)
            conv(G - 1, 2)
            mod_columns(4)
            mod_columns(5)
            pe.wait_ge(w16_done, BLK)
            pe.wait_ge(mask_done, 3)
            pe.wait_ge(h_full, DT * G)
            w16_rows = w16.rearrange("p a n -> p (a n)").rearrange("p (o n) -> p o n", o=BLK)

            def weight_columns(d):
                if d >= 2:
                    pe.wait_ge(wt_done, d - 1)
                for o in range(BLK):
                    mm = nc.tensor.transpose(bank[4 + d % 2][:, :].bitcast(F16)[:, o * P:(o + 1) * P],
                                             w16_rows[:, o, d * P:(d + 1) * P], ident_h[:, :])
                mm.then_inc(wt_ready, 1)

            def gate_rows(part, banks, ready):
                for b in range(NB):
                    for d in range(DT):
                        mm = nc.tensor.matmul(bank[banks[b]][:, d * P:(d + 1) * P],
                                              modT[:, part, d, b:b + 1].to_broadcast((P, P)), ident[:, :], start=True, stop=True)
                    mm.then_inc(ready, 1)

            weight_columns(0)
            weight_columns(1)
            pe.wait_ge(mod_done, 6)
            gate_rows(GATE1, (6, 7), ga_ready)
            weight_columns(2)
            weight_columns(3)
            pe.wait_ge(wt_done, 3)
            gate_rows(GATE2, (3, 4), gb_ready)
            conv(G - 1, DT - 1)
            pe.wait_ge(wo_in, 16)
            pe.wait_ge(wt_done, DT)
            for j in range(JT):
                mm = nc.tensor.matmul(bank[5][:, 0:1], wo_raw[:, j, :], cols[:, R_BV + j:R_BV + j + 1],
                                      start=(j == 0), stop=(j == JT - 1))
            mm.then_inc(by_ready, 1)
            pe.wait_ge(sblo_done, 1)
            pe.wait_ge(ga_done, 2 * NB)
            for d in range(DT):
                mm = nc.tensor.matmul(bank[6][0:2 * NB, :], sb_cols[:, d, :], wT[:, d, :], start=(d == 0), stop=(d == DT - 1))
            mm.then_inc(shiftrow_ready, 1)

            def bank_read(g, use):
                if use >= 0 or not (isinstance(g, int) and g == 0):
                    pe.wait_ge(*released(g, use))

            def qk_tile(g, t):
                m, j = t // JT, t % JT
                pe.wait_ge(cs_lod, 3 * g + m + 1)
                bank_read(g, t - 4)
                js = slice(j * P, (j + 1) * P)
                product3(bank[t % 4][:, :], wqkv_hi[:, m, js], wqkv_lo[:, m, js], cs_hi[:, m, :], cs_lo[:, m, :],
                         True, True).then_inc(qk_ready, 1)

            def values(g, u):
                pe.wait_ge(cs_lod, 3 * g + 3)
                if u >= 3:
                    pe.wait_ge(pt_done, 2 * UNITS * g + 2 * u - 5)
                elif u == 0 and not isinstance(g, int):
                    pe.wait_ge(pt_done, 2 * UNITS * g - 1)
                elif u > 0:
                    pe.wait_ge(v_act, UNITS * g + u)
                ts, ns = slice(u // 2 * P, (u // 2 + 1) * P), slice(u % 2 * HE // 2, (u % 2 + 1) * HE // 2)
                product3(bank[4][:, :], cs_hi[:, 2, ts], cs_lo[:, 2, ts], wqkv_hi[:, 2, ns], wqkv_lo[:, 2, ns],
                         True, True).then_inc(v_ready, 1)

            def scores(g, u):
                if u < 2:
                    last = 2 * JT - 1 - (JT // 2 if u == 0 else 0)
                    pe.wait_ge(qk_act, qk_count(QK_ACT, g, last))
                    pe.wait_ge(qk_dve, qk_count(QK_DVE, g, last))
                for half in range(2):
                    bank_read(g, 2 * JT + 2 * u + half - 4)
                    nc.tensor.matmul(s_bank(u, half)[:, :], ident_b[:, :], mask[:, :, :].rearrange("p h k -> p (h k)"),
                                     start=True, stop=False, skip_group_check=True)
                ts = slice(u // 2 * P, (u // 2 + 1) * P)
                for h in range(HB):
                    for half in range(2):
                        es, j = slice(half * E, (half + 1) * E), HB * (u % 2) + h
                        mm = nc.tensor.matmul(s_bank(u, half)[:, h * P:(h + 1) * P], qh[es, j, ts], kh[es, j, ts],
                                              start=False, stop=True, skip_group_check=True)
                        if h == HB - 1:
                            mm.then_inc(s_ready, 1)

            def transpose_probs(g, u):
                for half in range(2):
                    pe.wait_ge(norm_done, 2 * UNITS * g + 2 * u + half + 1)
                    if half == 0:
                        pe.wait_ge(v_act, UNITS * g + min(u + 3, UNITS))
                    if u >= 1:
                        pe.wait_ge(pt_done, 2 * UNITS * g + 2 * (u - 1) + half + 1)
                    for h in range(HB):
                        mm = nc.tensor.transpose(bank[4 + half][:, h * P:(h + 1) * P], prob[:, u % 2, half * HB + h, :], ident[:, :])
                    mm.then_inc(pt_ready, 1)

            def my_turn(g, kind, n):
                if TURNS.index((kind, n)) >= 2 or not (isinstance(g, int) and g == 0):
                    pe.wait_ge(*turn_free(g, kind, n))

            def outputs(g, u):
                pe.wait_ge(pt_done, 2 * UNITS * g + 2 * u + 2)
                pe.wait_ge(v_act, UNITS * g + u + 1)
                my_turn(g, "out", u)
                for h in range(HB):
                    for half in range(2):
                        head = HU * (u % 2) + 2 * h + half
                        mm = nc.tensor.matmul(turn_bank("out", u)[half * E:(half + 1) * E, h * P:(h + 1) * P],
                                              vh[:, u // 2 % 2, head * E:(head + 1) * E], probT[:, u % 2, half * HB + h, :],
                                              start=True, stop=True, skip_group_check=True)
                mm.then_inc(o_ready, 1)

            def out_product(g, k):
                pe.wait_ge(o_lod, UNITS * g + 4 * (k + 1))
                my_turn(g, "wo", k)
                for j in range(JT):
                    mm = product3(turn_bank("wo", k)[:, 0:2 * P], wo_hi[:, j, :], wo_lo[:, j, :], oT_hi[:, j, :], oT_lo[:, j, :],
                                  j == 0, j == JT - 1)
                mm.then_inc(wo_ready, 1)

            def project(g, b):
                pe.wait_ge(y_lod, 2 * g + b // 2 + 1)
                my_turn(g, "proj", b)
                ts, ds = slice(b * P, (b + 1) * P), bass.ds(g // GPB * D, D)
                product3(turn_bank("proj", b)[:, :], yT_hi[:, ts], yT_lo[:, ts], pw_hi[:, ds], pw_lo[:, ds],
                         True, True).then_inc(pj_ready, 1)

            def norm_columns(g, n):
                pe.wait_ge(xn2_done, BLK * g + 2 * (n // 2) + 2)
                my_turn(g, "norm", n)
                for e in range(2):
                    d = 2 * (n % 2) + e
                    for r in range(2):
                        mm = nc.tensor.transpose(turn_bank("norm", n)[:, (2 * e + r) * P:(2 * e + r + 1) * P],
                                                 xin[:, n // 2 * 2 + r, d * P:(d + 1) * P], ident[:, :])
                mm.then_inc(t2_ready, 1)

            def feed_forward(g, b):
                pe.wait_ge(h2_lod, 2 * DT * g + DT * (b // 2 + 1))
                my_turn(g, "ffn", b)
                for d in range(DT):
                    for half, h2 in enumerate((h2_hi, h2_lo)):
                        mm = nc.tensor.matmul(turn_bank("ffn", b)[:, :], h2[:, d, b * P:(b + 1) * P], wT[:, d, :],
                                              start=(d == 0 and half == 0), stop=(d == DT - 1 and half == 1))
                mm.then_inc(f_ready, 1)

            def attend(g, ahead=None):
                def fill(*tiles):
                    if ahead is not None:
                        for t in tiles:
                            qk_tile(ahead, t)

                for u in range(2, UNITS):
                    scores(g, u)
                    values(g, u)
                    if u >= 3:
                        outputs(g, u - 3)
                    transpose_probs(g, u - 2)
                    if u == 7:
                        out_product(g, 0)
                transpose_probs(g, 6)
                fill(0, 1)
                outputs(g, 5)
                transpose_probs(g, 7)
                fill(2)
                project(g, 0)
                fill(3)
                project(g, 1)
                outputs(g, 6)
                fill(4, 5, 6, 7)
                norm_columns(g, 0)
                norm_columns(g, 1)
                fill(8, 9)
                outputs(g, 7)
                feed_forward(g, 0)
                out_product(g, 1)
                feed_forward(g, 1)
                project(g, 2)
                fill(10)
                project(g, 3)
                fill(11, 12, 13, 14, 15)

            pe.wait_ge(c_done, C_FREE + 3 * G)
            pe.wait_ge(wlo_done, 4)
            for t in range(2 * JT):
                qk_tile(0, t)
            pe.wait_ge(gb_done, NB)
            pe.wait_ge(sel_done, 1)
            pe.wait_ge(shiftrow_done, 1)
            for b in range(NB):
                nc.tensor.matmul(bank[(7, 4)[b]][:, :], sel[:, b:b + 1].to_broadcast((2 * NB, P)), shift_row[:, :],
                                 start=True, stop=True).then_inc(shift_ready, 1)
            pe.wait_ge(by_done, 1)
            pe.wait_ge(shift_done, NB)
            pe.wait_ge(pwlo_done, NB)
            pe.wait_ge(mask_done, 4)
            scores(0, 0)
            values(0, 0)
            scores(0, 1)
            values(0, 1)
            with pe.Fori(0, G - 1) as i:
                attend(i, i + 1)
                scores(i + 1, 0)
                values(i + 1, 0)
                norm_columns(i, 2)
                norm_columns(i, 3)
                scores(i + 1, 1)
                values(i + 1, 1)
                feed_forward(i, 2)
                feed_forward(i, 3)
            attend(G - 1)
            norm_columns(G - 1, 2)
            norm_columns(G - 1, 3)
            feed_forward(G - 1, 2)
            feed_forward(G - 1, 3)


_INS = ['L0_attn_inputs', 'L0_attn_conv_w', 'L0_attn_conv_b', 'L0_attn_wq', 'L0_attn_bq', 'L0_attn_wk', 'L0_attn_bk',
        'L0_attn_wv', 'L0_attn_bv', 'L0_attn_wo', 'L0_attn_bo', 'L0_attn_proj_w', 'L0_attn_proj_b', 'L0_ffn_weight',
        'L0_ffn_scales', 'L0_c', 'L0_wmod']


def kernel(**inputs):
    import numpy as _np
    import concourse.bacc as _bacc
    from concourse import mybir as _mybir
    from concourse.bass_utils import run_bass_kernel_spmd as _run

    nc = _bacc.Bacc("TRN2", target_bir_lowering=False, num_devices=1, dynamic_dma_scratch_size=1024)
    arrays, args = {}, []
    for name in _INS:
        a = _np.ascontiguousarray(inputs[name])
        arrays[f"in_{name}_dram"] = a
        args.append(nc.dram_tensor(f"in_{name}_dram", a.shape, _mybir.dt.from_np(a.dtype), kind="ExternalInput").ap())
    shape = inputs['L0_attn_inputs'].shape
    args.append(nc.dram_tensor("out_0_dram", shape, _mybir.dt.float32, kind="ExternalOutput").ap())
    adaln_block(nc, *args)
    r = _run(nc, [arrays], core_ids=[0])
    return r.results[0]["out_0_dram"]
```

```python
from contextlib import ExitStack

import concourse.bass as bass
from concourse import mybir

F32 = mybir.dt.float32
F32R = mybir.dt.float32r
F16 = mybir.dt.float16
BF16 = mybir.dt.bfloat16
ALU = mybir.AluOpType
ACT = mybir.ActivationFunctionType
AX_X = mybir.AxisListType.X

P = 128
EPS = 1e-5
NEG_INF = -1.0e9
GATE_FLOOR = 0.25


def adaln_block(nc, x, conv_w, conv_b, wq, bq, wk, bk, wv, bv, wo, bo, proj_w, proj_b,
                ffn_w, ffn_s, c, wmod, out):
    NB, L, D = x.shape
    TAPS, _, W3 = conv_w.shape
    W = W3 // 3
    _, H, E = wq.shape
    DT = D // P
    GT = 512
    BLK = GT // P
    T = NB * L
    G = T // GT
    GPB = L // GT
    HE = H * E
    JT = HE // P
    UNITS = 2 * BLK
    HU = H // 2
    HB = HU // 2
    QSCALE = float(E) ** -0.5
    assert W == P and E * 2 == P and G == 4 and GPB == 2 and NB == 2 and DT == 4
    SHIFT, SCALE1, GATE1, SHIFT2, SCALE2, GATE2 = range(6)

    x_rows = x.rearrange("b (g k p) d -> (b g) p k d", k=BLK, p=P)
    out_rows = out.rearrange("b (g k p) d -> (b g) k p d", k=BLK, p=P)
    conv_rows = conv_w.rearrange("t (k p) w -> p t k w", p=P)
    mod_rows = wmod.rearrange("(k p) (c n) -> c p k n", p=P, n=D)
    wo_rows = wo.rearrange("h e w -> (h e) w").rearrange("(j p) w -> p j w", p=P)

    with ExitStack() as ctx:
        def sb(name, shape, dt=F32):
            return ctx.enter_context(nc.sbuf_tensor(name, shape, dt))

        def sem(name):
            return ctx.enter_context(nc.semaphore(name))

        bank = [ctx.enter_context(nc.psum_tensor(f"bank{i}", [P, 512], F32)) for i in range(8)]

        NM = TAPS + 1
        GH = GT // 2
        n_cu, n_cx = DT * NM * W3, NM * GH
        half_area = sb("half_area", [P, 2 * n_cu + 4 * n_cx], F32R)

        def area(at, *shape):
            n = 1
            for s in shape:
                n *= s
            v = half_area[:, at:at + n]
            if len(shape) == 3:
                return v.rearrange("p (a b c) -> p a b c", a=shape[0], b=shape[1])
            if len(shape) == 2:
                return v.rearrange("p (a b) -> p a b", a=shape[0])
            return v

        cu_hi, cu_lo = area(0, DT, NM, W3), area(n_cu, DT, NM, W3)
        cx_hi, cx_lo = area(2 * n_cu, 2, n_cx), area(2 * n_cu + 2 * n_cx, 2, n_cx)
        at = 0
        oT_hi = area(at, JT, 2 * P); at += JT * 2 * P
        oT_lo = area(at, JT, 2 * P); at += JT * 2 * P
        yT_hi = area(at, GT); at += GT
        yT_lo = area(at, GT); at += GT
        pw_hi = area(at, NB * D); at += NB * D
        assert at >= n_cu
        cs_hi = area(at, 3, GT); at += 3 * GT
        cs_lo = area(at, 3, GT); at += 3 * GT
        assert at <= 2 * n_cu - NM * W3
        pw_lo = area(at, NB * D); at += NB * D
        h2_hi = area(at, DT, GT); at += DT * GT
        h2_lo = area(at, DT, GT); at += DT * GT
        wT = area(at, DT, D); at += DT * D
        assert at <= 2 * n_cu + 4 * n_cx
        wqkv_hi = sb("wqkv_hi", [P, 3, HE], F32R)
        wqkv_lo = sb("wqkv_lo", [P, 3, HE], F32R)
        wo_hi = sb("wo_hi", [P, JT, W], F32R)
        wo_lo = sb("wo_lo", [P, JT, W], F32R)
        work = sb("work", [P, 2 * JT * GT + 2 * HE + 4 * HU * P])
        mod_stage = [work[:, i * DT * D:(i + 1) * DT * D].rearrange("p (k n) -> p k n", k=DT) for i in range(2)]
        at = 2 * DT * D
        cw_raw = work[:, at:at + TAPS * DT * W3].rearrange("p (t k w) -> p t k w", t=TAPS, k=DT); at += TAPS * DT * W3
        wqkv_raw = work[:, at:at + 3 * HE].rearrange("p (m n) -> p m n", m=3); at += 3 * HE
        wo_raw = work[:, at:at + JT * W].rearrange("p (j w) -> p j w", j=JT); at += JT * W
        pw_raw = work[:, at:at + D]; at += D
        pb_rows = work[:, at:at + D]; at += D
        c_m3 = work[:, at:at + 2 * GH].rearrange("p (s i) -> p s i", s=2); at += 2 * GH
        assert at <= work.shape[1]
        at = 0
        qh = work[:, at:at + JT * GT].rearrange("p (j t) -> p j t", j=JT); at += JT * GT
        kh = work[:, at:at + JT * GT].rearrange("p (j t) -> p j t", j=JT); at += JT * GT
        vh = work[:, at:at + 2 * HE].rearrange("p (s n) -> p s n", s=2); at += 2 * HE
        prob = work[:, at:at + 2 * HU * P].rearrange("p (s h k) -> p s h k", s=2, h=HU); at += 2 * HU * P
        probT = work[:, at:at + 2 * HU * P].rearrange("p (s h k) -> p s h k", s=2, h=HU); at += 2 * HU * P
        assert at <= work.shape[1]

        cT = sb("cT", [P, 3 * T])
        xin = sb("xin", [P, BLK, D])
        xr = sb("xr", [P, BLK, D])
        w16 = xr[:, 2:4, :].bitcast(F16)
        spare = sb("spare", [P, 2, GT + 2])
        pw_tmp = xin[:, 0:NB, :]
        y16 = sb("y16", [P, 2, D], F16)
        gb_rows = sb("gb_rows", [P, NB * D])
        shift_rows = sb("shift_rows", [P, NB * D])
        pbga_rows = sb("pbga_rows", [P, NB * D])
        cx = [xr[:, 0:2, :].rearrange("p a n -> p (a n)"), shift_rows[:, :]]
        cu_sum = [t[:, 0:2 * W3].rearrange("p (s w) -> p s w", s=2)
                  for t in (pbga_rows, xr[:, 2:4, :].rearrange("p a n -> p (a n)"))]
        c_mid = y16[:, :, :].rearrange("p s n -> p (s n)").bitcast(F32).rearrange("p (s i) -> p s i", s=2)
        mask = sb("mask", [P, HB, P], BF16)
        ident = sb("ident", [P, P])
        ident_b = sb("ident_b", [P, P], BF16)
        ident_h = sb("ident_h", [P, P], F16)
        scales16 = sb("scales16", [P, BLK, DT], F16)

        NC = NB * DT
        c_rows = sb("c_rows", [NC, P])
        c_cols = sb("c_cols", [P, NC])
        R_CB, R_BQ, R_BK, R_BV, R_BO, NR = 0, 3, 3 + JT, 3 + 2 * JT, 3 + 3 * JT, 3 + 3 * JT + 1
        rows = sb("rows", [NR, P])
        cols = sb("cols", [P, NR])
        bq8 = sb("bq8", [P, JT])
        by = sb("by", [P, 1])
        silu = sb("silu", [P, 4, NC])
        modT = sb("modT", [P, 6, DT, NB])
        mod_row = gb_rows[0:NB, :].rearrange("p (s n) -> p s n", s=2)
        sb_cols = sb("sb_cols", [P, DT, 2 * NB], F32R)
        sel = sb("sel", [2 * NB, NB])
        shift_row = y16[0:2 * NB, :, :].rearrange("p s n -> p (s n)").bitcast(F32)
        gate_tmp = sb("gate_tmp", [P, 2, DT, NB])
        cur1 = sb("cur1", [P, 2, DT, 1])
        cur2 = sb("cur2", [P, 1, DT, 1])
        halo_x = sb("halo_x", [2 * NB, D])
        halo = sb("halo", [P, DT, 2 * G])
        halo_m = sb("halo_m", [P, DT, NB, 2])
        halo_st = sb("halo_st", [2 * NB, 12])
        stats = sb("stats", [P, BLK, 6])
        mv = sb("mv", [P, BLK, 2])
        vare = sb("vare", [P, BLK])
        rstd = sb("rstd", [P, BLK])
        neg_half = sb("neg_half", [P, BLK])
        neg_max = sb("neg_max", [P, 2, HU])
        row_sum = sb("row_sum", [P, 2, HU])
        row_inv = sb("row_inv", [P, 2, HU])
        credit = sb("credit", [P, 3])

        rows_in, halo_in, c_in = sem("rows_in"), sem("halo_in"), sem("c_in")
        x_in = [sem("x_in0"), sem("x_in1")]
        cw_in = [sem(f"cw_in{d}") for d in range(DT)]
        mod_in = [sem("mod_in0"), sem("mod_in1")]
        wqkv_in, wo_in, pw_in, ffn_in, xr_in, out_sent = (sem("wqkv_in"), sem("wo_in"), sem("pw_in"), sem("ffn_in"),
                                                          sem("xr_in"), sem("out_sent"))
        ident_done, const_done, mask_done = sem("ident_done"), sem("const_done"), sem("mask_done")
        ccols_ready, ccols_done, cols_ready, cols_done, silu_exp, silu_step = (sem("ccols_ready"), sem("ccols_done"), sem("cols_ready"),
                                                                              sem("cols_done"), sem("silu_exp"), sem("silu_step"))
        mod_ready, modrow_done, modcol_ready, mod_done, gate_step = (sem("mod_ready"), sem("modrow_done"), sem("modcol_ready"),
                                                                     sem("mod_done"), sem("gate_step"))
        cusum_done = [sem(f"cusum_done{d}") for d in range(DT)]
        cuhi_done, culo_done = sem("cuhi_done"), sem("culo_done")
        whi_done, wlo_done = sem("whi_done"), sem("wlo_done")
        halo_step, halo_rstd, halo_ready = sem("halo_step"), sem("halo_rstd"), sem("halo_ready")
        ga_ready, ga_done, gb_ready, gb_done = sem("ga_ready"), sem("ga_done"), sem("gb_ready"), sem("gb_done")
        pwhi_done, pwlo_done = sem("pwhi_done"), sem("pwlo_done")
        w16_done, wt_ready, wt_done = sem("w16_done"), sem("wt_ready"), sem("wt_done")
        sel_done, sbhi_done, sblo_done, shiftrow_ready, shiftrow_done = (sem("sel_done"), sem("sbhi_done"), sem("sblo_done"),
                                                                         sem("shiftrow_ready"), sem("shiftrow_done"))
        shift_ready, shift_done, by_ready, by_done = sem("shift_ready"), sem("shift_done"), sem("by_ready"), sem("by_done")
        st1, ag1, var1, rstd1, xn_done = sem("st1"), sem("ag1"), sem("var1"), sem("rstd1"), sem("xn_done")
        cur1_done, t1_ready, h_done, halo_put = sem("cur1_done"), sem("t1_ready"), sem("h_done"), sem("halo_put")
        cx_done, cx_hid, cx_lod, c_m3_done, c_half = (sem("cx_done"), sem("cx_hid"), sem("cx_lod"), sem("c_m3_done"),
                                                        sem("c_half"))
        conv_tile, conv_ready, c_done = sem("conv_tile"), sem("conv_ready"), sem("c_done")
        cs_hid, cs_pool, cs_lod = sem("cs_hid"), sem("cs_pool"), sem("cs_lod")
        qk_ready, qk_act, qk_dve = sem("qk_ready"), sem("qk_act"), sem("qk_dve")
        v_ready, v_act = sem("v_ready"), sem("v_act")
        s_ready, max_done, exp_done, inv_done, norm_done = (sem("s_ready"), sem("max_done"), sem("exp_done"),
                                                            sem("inv_done"), sem("norm_done"))
        pt_ready, pt_done, o_ready, o_hid, o_lod = sem("pt_ready"), sem("pt_done"), sem("o_ready"), sem("o_hid"), sem("o_lod")
        wo_ready, y_hid, y_lod, pj_ready = sem("wo_ready"), sem("y_hid"), sem("y_lod"), sem("pj_ready")
        xrb_done, x1_done, last_ready, last_probs = sem("xrb_done"), sem("x1_done"), sem("last_ready"), sem("last_probs")
        st2, ag2, var2, rstd2, xn2_done, cur2_done = (sem("st2"), sem("ag2"), sem("var2"), sem("rstd2"),
                                                      sem("xn2_done"), sem("cur2_done"))
        t2_ready, h2_hid, h2_lod = sem("t2_ready"), sem("h2_hid"), sem("h2_lod")
        f_ready, y16_done, gy_done, out_ready = sem("f_ready"), sem("y16_done"), sem("gy_done"), sem("out_ready")
        Y16_FREE, OUT_FREE, C_FREE = BLK, 2, 3

        def f32(ap):
            return ap.bitcast(F32)

        def heads_of(bank_ap):
            return bank_ap[:, :].rearrange("p (h k) -> p h k", h=HB)

        block = ctx.enter_context(nc.Block())

        def mod_bank(n):
            return bank[2] if n == 2 else bank[6 + n % 2]

        def s_bank(u, half):
            return bank[(2 * u + half) % 4]

        USES = 2 * JT + 2 * UNITS
        assert USES % 4 == 0 and 2 * JT % 4 == 0
        QK_DVE = (5, 7, 9, 13)
        QK_ACT = tuple(t for t in range(2 * JT) if t not in QK_DVE)

        def qk_count(tiles, g, upto):
            return len(tiles) * g + sum(t <= upto for t in tiles)

        def released(g, use):
            if use < 0:
                g, use = g - 1, use + USES
            if use < 2 * JT:
                return (qk_dve, qk_count(QK_DVE, g, use)) if use in QK_DVE else (qk_act, qk_count(QK_ACT, g, use))
            return exp_done, 2 * UNITS * g + use - 2 * JT + 1

        TURNS = [(kind, n, 6 + at % 2) for at, (kind, n) in enumerate(
            [("out", 0), ("out", 1), ("out", 2), ("out", 3), ("out", 4), ("wo", 0), ("out", 5), ("proj", 0), ("proj", 1),
             ("out", 6), ("out", 7), ("norm", 0), ("norm", 1), ("wo", 1), ("ffn", 0), ("ffn", 1), ("proj", 2), ("proj", 3),
             ("norm", 2), ("norm", 3), ("ffn", 2), ("ffn", 3)])]
        assert len(TURNS) % 2 == 0
        LAST_TURNS = TURNS[:6] + [("score", 2 * UNITS - 4 + k, k) for k in range(4)] + [("probs", k, 4 + k) for k in range(2)] + [
            ("out", 5, 2), ("proj", 0, 0), ("proj", 1, 1), ("out", 6, 3), ("out", 7, 6), ("wo", 1, 7), ("norm", 0, 2), ("norm", 1, 3),
            ("proj", 2, 0), ("proj", 3, 1), ("ffn", 0, 4), ("ffn", 1, 5), ("norm", 2, 2), ("norm", 3, 3), ("ffn", 2, 6), ("ffn", 3, 7)]

        def halves(u):
            return (0, 1) if u >= UNITS - 2 else (1, 0)

        def find_turn(g, kind, n):
            turns = LAST_TURNS if isinstance(g, int) and g == G - 1 else TURNS
            return turns, [t[:2] for t in turns].index((kind, n))

        def turn_bank(g, kind, n):
            turns, at = find_turn(g, kind, n)
            return bank[turns[at][2]]

        def turn_free(g, kind, n):
            turns, at = find_turn(g, kind, n)
            before = [t for t in turns[:at] if t[2] == turns[at][2]]
            if not before:
                before, g = [t for t in TURNS if t[2] == turns[at][2]], g - 1
            kind, n, _ = before[-1]
            if kind == "ffn":
                return y16_done, Y16_FREE + BLK * g + n + 1
            if kind == "probs":
                return last_probs, 2
            done, of_group, each = {"out": (o_lod, UNITS, 1), "wo": (y_lod, 2, 1), "proj": (x1_done, BLK, 1),
                                    "norm": (h2_lod, 2 * DT, 2), "score": (exp_done, 2 * UNITS, 1)}[kind]
            return done, of_group * g + each * (n + 1)

        last_half_bank = bank[0]

        def column_parts(g, b):
            parts = 2 if isinstance(g, int) and b == BLK - 1 else 1
            return [slice(k * D // parts, (k + 1) * D // parts) for k in range(parts)]

        def weight_sums(eng, nc_eng, d):
            eng.wait_ge(cw_in[d], 16)
            if d >= 2:
                eng.wait_ge(cuhi_done, 3 * (d - 1))
                eng.wait_ge(culo_done, 3 * (d - 1))
            sums, done = cu_sum[d % 2], cusum_done[d]
            nc_eng.tensor_tensor(sums[:, 0, :], cw_raw[:, 0, d, :], cw_raw[:, 2, d, :], ALU.add).then_inc(done, 1)
            eng.wait_ge(done, 1)
            nc_eng.tensor_tensor(sums[:, 1, :], sums[:, 0, :], cw_raw[:, 1, d, :], ALU.subtract).then_inc(done, 1)
            nc_eng.tensor_tensor(sums[:, 0, :], sums[:, 0, :], cw_raw[:, 1, d, :], ALU.add).then_inc(done, 1)

        @block.sync
        def _(sp):
            def load_tokens(g):
                for r in range(2):
                    bs = slice(r * BLK // 2, (r + 1) * BLK // 2)
                    sp.dma_start(xin[:, bs, :], x_rows[g][:, bs, :]).then_inc(x_in[r], 16)

            sp.dma_start(c_rows[:, :], c.rearrange("b (k p) -> (b k) p", p=P)).then_inc(c_in, 16)
            for r in range(2):
                sp.dma_start(halo_x[NB * r:NB * (r + 1), :], x[:, GT - r, :]).then_inc(halo_in, 16)
            sp.dma_start(mod_stage[0], mod_rows[SCALE1]).then_inc(mod_in[0], 16)
            load_tokens(0)
            sp.dma_start(mod_stage[1], mod_rows[SHIFT]).then_inc(mod_in[1], 16)
            for d in range(DT):
                sp.dma_start(cw_raw[:, :, d, :], conv_rows[:, :, d, :]).then_inc(cw_in[d], 16)
                if d == 0:
                    sp.dma_start(rows[R_CB:R_BQ, :], conv_b.rearrange("(m p) -> m p", p=P)).then_inc(rows_in, 16)
                    for at, bias in ((R_BQ, bq), (R_BK, bk), (R_BV, bv)):
                        sp.dma_start(rows[at:at + JT, :], bias.rearrange("h e -> (h e)").rearrange("(j p) -> j p", p=P)).then_inc(rows_in, 16)
                    sp.dma_start(rows[R_BO:NR, :], bo.rearrange("(a p) -> a p", a=1)).then_inc(rows_in, 16)
                    for n, part in enumerate((GATE1, SHIFT2)):
                        sp.wait_ge(mod_ready, n + 1)
                        sp.dma_start(mod_stage[n], mod_rows[part]).then_inc(mod_in[n], 16)
            with sp.Fori(0, G - 1) as i:
                sp.wait_ge(t1_ready, i * DT + DT)
                load_tokens(i + 1)
            for n, part in enumerate((SCALE2, GATE2)):
                sp.wait_ge(mod_ready, n + 3)
                sp.dma_start(mod_stage[n], mod_rows[part]).then_inc(mod_in[n], 16)
            sp.wait_ge(wt_ready, DT)
            sp.dma_start(xr[:, :, :], x_rows[0]).then_inc(xr_in, 16)

            def store(g):
                for b in range(BLK):
                    for k, ns in enumerate(column_parts(g, b)):
                        if isinstance(g, int) and b == BLK - 1:
                            sp.wait_ge(last_ready, k + 1)
                        else:
                            sp.wait_ge(out_ready, OUT_FREE + BLK * g + b + 1)
                        sp.dma_start(out_rows[g, b][:, ns], xr[:, b, ns]).then_inc(out_sent, 16)

            with sp.Fori(0, G - 1) as i:
                store(i)
                sp.wait_ge(out_sent, i * (16 * BLK) + 16 * BLK)
                sp.dma_start(xr[:, :, :], x_rows[i + 1]).then_inc(xr_in, 16)
            store(G - 1)
            sp.wait_ge(out_sent, 16 * (BLK * G - 1 + len(column_parts(G - 1, BLK - 1))))

        @block.gpsimd
        def _(pool):
            nc.gpsimd.memset(ident[:, :], 0.0).then_inc(ident_done, 1)
            pool.wait_ge(ident_done, 1)
            nc.gpsimd.affine_select(out=ident[:, :], in_=ident[:, :], compare_op=ALU.not_equal, fill=1.0, base=0,
                                    pattern=[[-1, P]], channel_multiplier=1).then_inc(ident_done, 1)
            nc.gpsimd.memset(neg_half[:, :], -0.5).then_inc(const_done, 1)
            nc.gpsimd.memset(halo[:, :, :], 0.0).then_inc(const_done, 1)
            nc.gpsimd.memset(mask[:, :, :], 0.0).then_inc(mask_done, 1)
            nc.gpsimd.memset(credit[:, 0:1], 0.0).then_inc(out_ready, OUT_FREE)

            pool.wait_ge(ident_done, 2)
            nc.gpsimd.tensor_copy(ident_b[:, :], ident[:, :]).then_inc(mask_done, 1)
            nc.gpsimd.tensor_copy(ident_h[:, :], ident[:, :]).then_inc(mask_done, 1)
            pool.wait_ge(mask_done, 3)
            nc.gpsimd.affine_select(out=mask[:, :, :], in_=mask[:, :, :], compare_op=ALU.is_ge, fill=NEG_INF, base=0,
                                    pattern=[[0, HB], [-1, P]], channel_multiplier=1).then_inc(mask_done, 1)

            pool.wait_ge(const_done, 2)
            pool.wait_ge(halo_step, 3)
            nc.gpsimd.tensor_tensor(halo_st[:, 9:10], halo_st[:, 8:9], neg_half[0:2 * NB, 0:1], ALU.pow).then_inc(halo_rstd, 1)

            def rsqrt(var_sem, rstd_sem, count, first, last):
                pool.wait_ge(var_sem, count)
                nc.gpsimd.tensor_tensor(rstd[:, first:last], vare[:, first:last], neg_half[:, first:last], ALU.pow).then_inc(rstd_sem, 1)

            def modulation(g, first, last, dst, done):
                b = g // GPB
                nc.gpsimd.tensor_copy(dst, modT[:, first:last, :, bass.ds(b, 1)]).then_inc(done, 1)

            def edges(g, d):
                n = DT * g + d
                if not isinstance(g, int) or n >= 2:
                    pool.wait_ge(cx_done, 3 * n - 3)
                nc.gpsimd.tensor_copy(spare[:, d % 2, 0:GT + 2:GT + 1], halo[:, d, bass.ds(2 * g, 2)]).then_inc(halo_put, 1)

            def inputs_low(g, d):
                pool.wait_ge(cx_hid, DT * g + d + 1)
                nc.gpsimd.tensor_tensor(cx_lo[:, d % 2, :], cx[d % 2], f32(cx_hi[:, d % 2, :]), ALU.subtract).then_inc(cx_lod, 1)

            rsqrt(var1, rstd1, 1, 0, BLK)
            pool.wait_ge(mod_done, 2)
            modulation(0, SHIFT, SCALE1 + 1, cur1[:, :, :, :], cur1_done)
            pool.wait_ge(halo_step, 6)
            edges(0, 0)
            edges(0, 1)
            inputs_low(0, 0)
            edges(0, 2)
            inputs_low(0, 1)
            edges(0, 3)
            weight_sums(pool, nc.gpsimd, 3)
            with pool.Fori(0, G - 1) as i:
                inputs_low(i, 2)
                rsqrt(var1, rstd1, i + 2, 0, BLK)
                pool.wait_ge(h_done, DT * i + DT)
                modulation(i + 1, SHIFT, SCALE1 + 1, cur1[:, :, :, :], cur1_done)
                edges(i + 1, 0)
                edges(i + 1, 1)
                inputs_low(i, 3)
                inputs_low(i + 1, 0)
                edges(i + 1, 2)
                inputs_low(i + 1, 1)
                edges(i + 1, 3)
            inputs_low(G - 1, 2)
            for m in range(3):
                pool.wait_ge(whi_done, m + 1)
                nc.gpsimd.tensor_tensor(wqkv_lo[:, m, :], wqkv_raw[:, m, :], f32(wqkv_hi[:, m, :]), ALU.subtract).then_inc(wlo_done, 1)
            pool.wait_ge(whi_done, 4)
            nc.gpsimd.tensor_tensor(wo_lo[:, :, :], wo_raw, f32(wo_hi[:, :, :]), ALU.subtract).then_inc(wlo_done, 1)
            inputs_low(G - 1, 3)

            def split(g, m):
                pool.wait_ge(c_done, C_FREE + 3 * G)
                pool.wait_ge(qk_ready, 2 * JT * (g - 1) + JT * (m + 1))
                nc.gpsimd.tensor_copy(cs_hi[:, m, :], cT[:, bass.ds(GT * g + m * T, GT)]).then_inc(cs_pool, 1)

            def normalise(g, u):
                for half in range(2):
                    n = 2 * UNITS * g + 2 * u + half + 1
                    pool.wait_ge(inv_done, n)
                    p = prob[:, u % 2, half * HB:(half + 1) * HB, :]
                    r = row_inv[:, u % 2, half * HB:(half + 1) * HB].unsqueeze(2).to_broadcast((P, HB, P))
                    nc.gpsimd.tensor_tensor(p, p, r, ALU.mult).then_inc(norm_done, 1)

            def residual_bias(g, b):
                pool.wait_ge(ga_done, NB)
                pool.wait_ge(xr_in, 16 * g + 16)
                nc.gpsimd.tensor_tensor(xr[:, b, :], xr[:, b, :], pbga_rows[:, bass.ds(g // GPB * D, D)],
                                        ALU.add).then_inc(xrb_done, 1)

            def final_add(g, b):
                pool.wait_ge(gy_done, BLK * g + b + 1)
                nc.gpsimd.tensor_tensor(xr[:, b, :], spare[:, b % 2, 0:D], xr[:, b, :], ALU.add).then_inc(out_ready, 1)

            def units(g, ahead=None):
                for u in range(2, UNITS):
                    normalise(g, u - 1)
                    if ahead is not None and u in (2, 3):
                        split(ahead, u - 2)
                    if u >= UNITS - BLK + 1:
                        residual_bias(g, u - UNITS + BLK - 1)
                normalise(g, UNITS - 1)
                residual_bias(g, BLK - 1)
                modulation(g, SCALE2, SCALE2 + 1, cur2[:, :, :, :], cur2_done)
                rsqrt(var2, rstd2, 2 * g + 1, 0, 2)

            pool.wait_ge(mod_done, 6)
            pool.wait_ge(ga_done, 2 * NB)
            normalise(0, 0)
            with pool.Fori(0, G - 1) as i:
                units(i, i + 1)
                final_add(i, 0)
                final_add(i, 1)
                rsqrt(var2, rstd2, 2 * i + 2, 2, BLK)
                normalise(i + 1, 0)
                final_add(i, 2)
                final_add(i, 3)
            units(G - 1)
            rsqrt(var2, rstd2, 2 * G, 2, BLK)
            for b in range(BLK - 1):
                final_add(G - 1, b)

        @block.scalar
        def _(act):
            act.wait_ge(const_done, 2)
            nc.scalar.copy(credit[:, 2:3], neg_half[:, 0:1]).then_inc(c_done, C_FREE)
            act.wait_ge(ccols_done, 1)
            nc.scalar.activation(silu[:, 0, :], c_cols[:, :], ACT.Exp, scale=-1.0).then_inc(silu_exp, 1)

            def mod_rows_out(n):
                act.wait_ge(mod_ready, n + 1)
                if n >= 2:
                    act.wait_ge(modcol_ready, n - 1)
                nc.scalar.copy(mod_row[:, n % 2, :], mod_bank(n)[0:NB, :]).then_inc(modrow_done, 1)

            def weights_high_outer(d):
                act.wait_ge(cw_in[d], 16)
                nc.scalar.copy(cu_hi[:, d, 0, :], cw_raw[:, 0, d, :]).then_inc(cuhi_done, 1)
                nc.scalar.activation(cu_hi[:, d, 1, :], cw_raw[:, 2, d, :], ACT.Copy, scale=-1.0).then_inc(cuhi_done, 1)

            def weights_high_inner(d):
                act.wait_ge(cusum_done[d], 3)
                nc.scalar.activation(cu_hi[:, d, 2:4, :], cu_sum[d % 2], ACT.Copy, scale=0.5).then_inc(cuhi_done, 1)

            mod_rows_out(0)
            weights_high_outer(0)
            mod_rows_out(1)
            weights_high_inner(0)

            def activations(g, d):
                n = DT * g + d
                if d == 0:
                    act.wait_ge(cur1_done, g + 1)
                if not isinstance(g, int) or n >= 2:
                    act.wait_ge(cx_done, 3 * n - 3)
                act.wait_ge(t1_ready, n + 1)
                nc.scalar.activation(spare[:, d % 2, 1:GT + 1], bank[6 + d % 2][:, :], ACT.Identity,
                                     bias=cur1[:, 0, d, :], scale=cur1[:, 1, d, :]).then_inc(h_done, 1)

            def inputs_high(g, d):
                act.wait_ge(cx_done, 3 * (DT * g + d) + 3)
                if d >= 2:
                    act.wait_ge(conv_tile, (DT - 1) * g + d - 1)
                elif not isinstance(g, int) and d == 0:
                    act.wait_ge(conv_tile, (DT - 1) * g)
                elif not isinstance(g, int):
                    act.wait_ge(conv_ready, 3 * g)
                nc.scalar.copy(cx_hi[:, d % 2, :], cx[d % 2]).then_inc(cx_hid, 1)

            def conv_out(g):
                for m in range(3):
                    act.wait_ge(conv_ready, 3 * g + m + 1)
                    if m == 2:
                        act.wait_ge(c_half, 6 * g + 2)
                    nc.scalar.copy(c_m3[:, m % 2, :], bank[2 * m + 1][:, GH:2 * GH]).then_inc(c_m3_done, 1)

            activations(0, 0)
            activations(0, 1)
            inputs_high(0, 0)
            activations(0, 2)
            mod_rows_out(2)
            weights_high_outer(1)
            weights_high_inner(1)
            inputs_high(0, 1)
            activations(0, 3)
            weights_high_outer(2)
            weights_high_inner(2)
            inputs_high(0, 2)
            weights_high_outer(3)
            weights_high_inner(3)
            for m, w in enumerate((wq, wk, wv)):
                act.dma_start(wqkv_raw[:, m, :], w.rearrange("w h e -> w (h e)")).then_inc(wqkv_in, 16)
            act.dma_start(wo_raw, wo_rows).then_inc(wo_in, 16)
            act.dma_start(pw_raw, proj_w).then_inc(pw_in, 16)
            act.dma_start(pb_rows, proj_b.rearrange("(a d) -> a d", a=1).to_broadcast((P, D))).then_inc(pw_in, 16)
            act.dma_start(scales16[:, :, :], ffn_s.rearrange("(o p) g -> p o g", p=P)).then_inc(ffn_in, 16)
            act.wait_ge(culo_done, 3 * DT)
            act.dma_start(w16.rearrange("p a n -> p (a n)").rearrange("p (o n) -> p o n", o=BLK),
                          ffn_w.rearrange("(o p) n -> p o n", p=P)).then_inc(ffn_in, 16)
            mod_rows_out(3)
            with act.Fori(0, G - 1) as i:
                inputs_high(i, 3)
                activations(i + 1, 0)
                activations(i + 1, 1)
                inputs_high(i + 1, 0)
                conv_out(i)
                inputs_high(i + 1, 1)
                activations(i + 1, 2)
                activations(i + 1, 3)
                inputs_high(i + 1, 2)
            act.wait_ge(wqkv_in, 48)
            for m in range(3):
                nc.scalar.copy(wqkv_hi[:, m, :], wqkv_raw[:, m, :]).then_inc(whi_done, 1)
            act.wait_ge(wo_in, 16)
            nc.scalar.copy(wo_hi[:, :, :], wo_raw).then_inc(whi_done, 1)
            act.wait_ge(mod_done, 4)
            nc.scalar.copy(sb_cols[:, :, 0:NB], modT[:, SHIFT2]).then_inc(sbhi_done, 1)
            inputs_high(G - 1, 3)
            mod_rows_out(4)
            mod_rows_out(5)

            def split(g, m):
                if isinstance(g, int):
                    act.wait_ge(conv_tile, (DT - 1) * G)
                else:
                    act.wait_ge(v_ready, UNITS * (g - 1) + UNITS)
                nc.scalar.copy(cs_hi[:, m, :], cT[:, bass.ds(GT * g + m * T, GT)]).then_inc(cs_hid, 1)

            def qk_out(g, t):
                act.wait_ge(qk_ready, 2 * JT * g + t + 1)
                if t < JT:
                    nc.scalar.activation(qh[:, t, :], bank[t % 4][:, :], ACT.Identity, bias=bq8[:, t:t + 1],
                                         scale=QSCALE).then_inc(qk_act, 1)
                else:
                    nc.scalar.activation(kh[:, t - JT, :], bank[t % 4][:, :], ACT.Identity,
                                         bias=cols[:, R_BK + t - JT:R_BK + t - JT + 1]).then_inc(qk_act, 1)

            def values(g, u):
                act.wait_ge(v_ready, UNITS * g + u + 1)
                nc.scalar.copy(vh[:, u // 2 % 2, u % 2 * HE // 2:(u % 2 + 1) * HE // 2], bank[4][:, :]).then_inc(v_act, 1)

            def exponentials(g, u):
                for half in range(2):
                    n = 2 * UNITS * g + 2 * u + half + 1
                    act.wait_ge(max_done, n)
                    if u >= 2:
                        act.wait_ge(pt_ready, 2 * UNITS * g + 2 * (u - 2) + halves(u - 2).index(half) + 1)
                    s = heads_of(s_bank(u, half))
                    for h in range(HB):
                        k = half * HB + h
                        ins = nc.scalar.activation(prob[:, u % 2, k, :], s[:, h, :], ACT.Exp,
                                                   bias=neg_max[:, u % 2, k:k + 1], accum_out=row_sum[:, u % 2, k:k + 1])
                    ins.then_inc(exp_done, 1)

            def o_high(g, u):
                act.wait_ge(o_ready, UNITS * g + u + 1)
                if u == 4:
                    act.wait_ge(wo_ready, 2 * g + 1)
                nc.scalar.copy(oT_hi[:, HB * (u % 2):HB * (u % 2 + 1), (u // 2 % 2) * P:(u // 2 % 2 + 1) * P],
                               heads_of(turn_bank(g, "out", u))).then_inc(o_hid, 1)

            def y_high(g, k):
                act.wait_ge(wo_ready, 2 * g + k + 1)
                act.wait_ge(by_done, 1)
                nc.scalar.activation(yT_hi[:, 2 * P * k:2 * P * (k + 1)], turn_bank(g, "wo", k)[:, 0:2 * P], ACT.Identity,
                                     bias=by[:, 0:1]).then_inc(y_hid, 1)

            def h2_high(g, n):
                act.wait_ge(cur2_done, g + 1)
                act.wait_ge(t2_ready, 4 * g + n + 1)
                for e in range(2):
                    d = 2 * (n % 2) + e
                    nc.scalar.activation(h2_hi[:, d, n // 2 * 2 * P:(n // 2 + 1) * 2 * P],
                                         turn_bank(g, "norm", n)[:, e * 2 * P:(e + 1) * 2 * P], ACT.Copy,
                                         scale=cur2[:, 0, d, :]).then_inc(h2_hid, 1)

            def units(g):
                for u in range(2, UNITS):
                    values(g, u)
                    exponentials(g, u)
                    if u == 7 and isinstance(g, int):
                        y_high(g, 0)
                    if u >= 3:
                        o_high(g, u - 3)
                    if u == 7 and not isinstance(g, int):
                        y_high(g, 0)

            def finish(g, ahead):
                def fill(*tiles):
                    for t in tiles:
                        qk_out(ahead, t)

                split(ahead, 2)
                fill(0, 1)
                o_high(g, 5)
                fill(2, 3)
                o_high(g, 6)
                fill(4)
                o_high(g, 7)
                fill(6)
                h2_high(g, 0)
                h2_high(g, 1)
                fill(8)
                y_high(g, 1)
                fill(10, 11, 12, 14, 15)

            for m in range(3):
                split(0, m)
            conv_out(G - 1)
            for t in QK_ACT:
                qk_out(0, t)
                if t in (8, 11):
                    for d in ((0, 1), (2, 3))[t == 11]:
                        act.wait_ge(wt_ready, d + 1)
                        nc.scalar.copy(wT[:, d, :], bank[6 + d % 2][:, :].bitcast(F16)[:, 0:D]).then_inc(wt_done, 1)
            for b in range(NB):
                act.wait_ge(ga_done, NB + b + 1)
                nc.scalar.copy(pw_hi[:, b * D:(b + 1) * D], pw_tmp[:, b, :]).then_inc(pwhi_done, 1)
            act.wait_ge(shiftrow_ready, 1)
            nc.scalar.copy(shift_row[:, :], bank[5][0:2 * NB, :]).then_inc(shiftrow_done, 1)
            exponentials(0, 0)
            values(0, 0)
            for b in range(NB):
                act.wait_ge(shift_ready, b + 1)
                nc.scalar.copy(shift_rows[:, b * D:(b + 1) * D], bank[6 + b][:, :]).then_inc(shift_done, 1)
            values(0, 1)
            exponentials(0, 1)
            with act.Fori(0, G - 1) as i:
                units(i)
                finish(i, i + 1)
                values(i + 1, 0)
                h2_high(i, 2)
                h2_high(i, 3)
                exponentials(i + 1, 0)
                values(i + 1, 1)
                exponentials(i + 1, 1)
            units(G - 1)
            o_high(G - 1, 5)
            act.wait_ge(o_ready, UNITS * G - 2)
            for at, half in enumerate(halves(UNITS - 1)):
                act.wait_ge(pt_ready, 2 * UNITS * G - 1 + at)
                nc.scalar.copy(probT[:, (UNITS - 1) % 2, half * HB:(half + 1) * HB, :], heads_of(bank[4 + half])).then_inc(last_probs, 1)
            o_high(G - 1, 6)
            o_high(G - 1, 7)
            y_high(G - 1, 1)
            h2_high(G - 1, 0)
            h2_high(G - 1, 1)
            h2_high(G - 1, 2)
            h2_high(G - 1, 3)

        @block.vector
        def _(dve):
            nc.vector.memset(credit[:, 1:2], 0.0).then_inc(y16_done, Y16_FREE)
            dve.wait_ge(ccols_ready, 1)
            nc.vector.tensor_copy(c_cols[:, :], bank[6][:, 0:NC]).then_inc(ccols_done, 1)
            dve.wait_ge(silu_exp, 1)
            nc.vector.tensor_scalar(silu[:, 1, :], silu[:, 0, :], 1.0, None, ALU.add).then_inc(silu_step, 1)
            dve.wait_ge(silu_step, 1)
            nc.vector.reciprocal(silu[:, 2, :], silu[:, 1, :]).then_inc(silu_step, 1)
            dve.wait_ge(silu_step, 2)
            nc.vector.tensor_tensor(silu[:, 3, :], silu[:, 2, :], c_cols[:, :], ALU.mult).then_inc(silu_step, 1)

            def norm_stats(src, g, b, st):
                nc.vector.bn_stats(stats[:, b, :], src[:, b, :]).then_inc(st, 1)

            def norm_variance(g, st, ag, var, first=0, last=BLK):
                dve.wait_ge(st, BLK * g + last)
                nc.vector.memset(credit[:, 1:2], 0.0)
                for b in range(first, last):
                    nc.vector.bn_aggr(mv[:, b, :], stats[:, b, :]).then_inc(ag, 1)
                dve.wait_ge(ag, BLK * g + last)
                nc.vector.tensor_scalar(vare[:, first:last], mv[:, first:last, 1], EPS, None, ALU.add).then_inc(var, 1)

            def norm_apply(src, rs, count, done, first=0, last=BLK):
                dve.wait_ge(rs, count)
                for b in range(first, last):
                    nc.vector.tensor_scalar(xin[:, b, :], src[:, b, :], mv[:, b, 0:1], rstd[:, b:b + 1],
                                            ALU.subtract, ALU.mult).then_inc(done, 1)

            def norm1(g):
                for b in range(BLK):
                    if b % (BLK // 2) == 0:
                        dve.wait_ge(x_in[b * 2 // BLK], 16 * g + 16)
                    norm_stats(xin, g, b, st1)
                norm_variance(g, st1, ag1, var1)
                norm_apply(xin, rstd1, g + 1, xn_done)

            dve.wait_ge(halo_in, 16 * 2)
            nc.vector.bn_stats(halo_st[:, 0:6], halo_x[:, :]).then_inc(halo_step, 1)
            dve.wait_ge(halo_step, 1)
            nc.vector.bn_aggr(halo_st[:, 6:8], halo_st[:, 0:6]).then_inc(halo_step, 1)
            dve.wait_ge(halo_step, 2)
            nc.vector.tensor_scalar(halo_st[:, 8:9], halo_st[:, 7:8], EPS, None, ALU.add).then_inc(halo_step, 1)
            dve.wait_ge(halo_rstd, 1)
            nc.vector.tensor_scalar(halo_x[:, :], halo_x[:, :], halo_st[:, 6:7], halo_st[:, 9:10],
                                    ALU.subtract, ALU.mult).then_inc(halo_step, 1)
            norm1(0)

            def mod_part(n, part):
                dve.wait_ge(modcol_ready, n + 1)
                src = bank[6 + n % 2][:, 0:DT * NB].rearrange("p (k b) -> p k b", b=NB)
                if part in (SCALE1, SCALE2):
                    nc.vector.tensor_scalar(modT[:, part], src, 1.0, None, ALU.add).then_inc(mod_done, 1)
                elif part in (SHIFT, SHIFT2):
                    nc.vector.tensor_copy(modT[:, part], src).then_inc(mod_done, 1)
                else:
                    k = 4 * (part == GATE2)
                    nc.vector.tensor_scalar(gate_tmp[:, 0], src, -1.0, GATE_FLOOR, ALU.mult, ALU.max).then_inc(gate_step, 1)
                    nc.vector.tensor_scalar(gate_tmp[:, 1], src, 0.0, 2.0, ALU.is_ge, ALU.mult).then_inc(gate_step, 1)
                    dve.wait_ge(gate_step, k + 2)
                    nc.vector.tensor_scalar(gate_tmp[:, 1], gate_tmp[:, 1], -1.0, None, ALU.add).then_inc(gate_step, 1)
                    nc.vector.tensor_tensor(gate_tmp[:, 0], src, gate_tmp[:, 0], ALU.max).then_inc(gate_step, 1)
                    dve.wait_ge(gate_step, k + 4)
                    nc.vector.tensor_tensor(modT[:, part], gate_tmp[:, 0], gate_tmp[:, 1], ALU.mult).then_inc(mod_done, 1)

            def weights_low(d):
                dve.wait_ge(cusum_done[d], 3)
                dve.wait_ge(cuhi_done, 3 * d + 3)
                nc.vector.tensor_tensor(cu_lo[:, d, 0, :], cw_raw[:, 0, d, :], f32(cu_hi[:, d, 0, :]), ALU.subtract).then_inc(culo_done, 1)
                for m, src, scale in ((slice(1, 2), cw_raw[:, 2:3, d, :], -1.0), (slice(2, 4), cu_sum[d % 2], 0.5)):
                    nc.vector.scalar_tensor_tensor(out=cu_lo[:, d, m, :], in0=src, scalar=scale, in1=f32(cu_hi[:, d, m, :]),
                                                   op0=ALU.mult, op1=ALU.subtract).then_inc(culo_done, 1)

            weight_sums(dve, nc.vector, 0)
            mod_part(0, SCALE1)
            mod_part(1, SHIFT)
            dve.wait_ge(halo_ready, 1)
            dve.wait_ge(mod_done, 2)
            dve.wait_ge(const_done, 2)
            src = bank[5][:, 0:DT * 2 * NB].rearrange("p (k r b) -> p k b r", k=DT, b=NB)
            inner = halo[:, :, :].rearrange("p d (b s) -> p d b s", b=NB)[:, :, :, 1:3]
            for k, (part, op, dst, a) in enumerate(((SCALE1, ALU.mult, halo_m[:, :, :, :], src),
                                                    (SHIFT, ALU.add, inner, halo_m[:, :, :, :]))):
                dve.wait_ge(halo_step, 4 + k)
                nc.vector.tensor_tensor(dst, a, modT[:, part].unsqueeze(3).to_broadcast((P, DT, NB, 2)),
                                        op).then_inc(halo_step, 1)

            def inputs(g, d):
                n = DT * g + d
                dve.wait_ge(halo_put, n + 1)
                dve.wait_ge(h_done, n + 1)
                if not isinstance(g, int) or n >= 2:
                    dve.wait_ge(cx_lod, n - 1)
                h, c4 = spare[:, d % 2, :], cx[d % 2]
                nc.vector.tensor_tensor(c4[:, 0:GT].rearrange("p (s i) -> p i s", s=2), h[:, 0:GT].rearrange("p (i s) -> p i s", s=2),
                                        h[:, 2:GT + 2].rearrange("p (i s) -> p i s", s=2), ALU.subtract).then_inc(cx_done, 1)
                nc.vector.tensor_tensor(c4[:, GT:GT + GH], h[:, 1:GT + 1:2], h[:, 2:GT + 2:2], ALU.add).then_inc(cx_done, 1)
                nc.vector.tensor_tensor(c4[:, GT + GH:2 * GT], h[:, 2:GT + 2:2], h[:, 1:GT + 1:2], ALU.subtract).then_inc(cx_done, 1)

            def conv_out(g, outs=(0, 1, 2)):
                for m in outs:
                    dve.wait_ge(c_m3_done, 3 * g + m + 1)
                    if m == 0:
                        dve.wait_ge(cols_done, 1)
                    m1_m4 = bank[2 * m][:, :].rearrange("p (s i) -> p s i", s=2)
                    m2 = bank[2 * m + 1][:, 0:GH]
                    dve.wait_ge(c_done, C_FREE + 3 * g + m)
                    nc.vector.tensor_tensor(c_mid[:, 0, :], m2, c_m3[:, m % 2, :], ALU.add).then_inc(c_half, 1)
                    nc.vector.tensor_tensor(c_mid[:, 1, :], m2, c_m3[:, m % 2, :], ALU.subtract).then_inc(c_half, 1)
                    dve.wait_ge(c_half, 6 * g + 2 * m + 2)
                    nc.vector.scalar_tensor_tensor(out=cT[:, bass.ds(GT * g + m * T, GT)].rearrange("p (i s) -> p s i", s=2),
                                                   in0=m1_m4, scalar=cols[:, R_CB + m:R_CB + m + 1], in1=c_mid,
                                                   op0=ALU.add, op1=ALU.add).then_inc(c_done, 1)

            inputs(0, 0)
            weights_low(0)
            dve.wait_ge(cols_ready, 1)
            nc.vector.tensor_copy(cols[:, :], bank[4][:, 0:NR]).then_inc(cols_done, 1)
            inputs(0, 1)
            dve.wait_ge(cols_done, 1)
            nc.vector.tensor_scalar(bq8[:, :], cols[:, R_BQ:R_BK], QSCALE, None, ALU.mult).then_inc(cols_done, 1)
            weight_sums(dve, nc.vector, 1)
            weights_low(1)
            inputs(0, 2)
            weight_sums(dve, nc.vector, 2)
            weights_low(2)
            def norm1_begin(g):
                for b in range(BLK):
                    if b % (BLK // 2) == 0:
                        dve.wait_ge(x_in[b * 2 // BLK], 16 * g + 16)
                    norm_stats(xin, g, b, st1)
                norm_variance(g, st1, ag1, var1)

            norm1_begin(1)
            weights_low(3)
            def group_step(g):
                inputs(g, 3)
                norm_apply(xin, rstd1, g + 2, xn_done)
                inputs(g + 1, 0)
                inputs(g + 1, 1)
                conv_out(g)
                inputs(g + 1, 2)

            with dve.Fori(0, G - 2) as i:
                group_step(i)
                norm1_begin(i + 2)
            group_step(G - 2)
            dve.wait_ge(ffn_in, 32)
            ws = w16.rearrange("p a n -> p (a n)").rearrange("p (o k n) -> p o k n", o=BLK, k=DT)
            for o in range(BLK):
                nc.vector.tensor_tensor(ws[:, o], ws[:, o], scales16[:, o, :].unsqueeze(2).to_broadcast((P, DT, P)),
                                        ALU.mult).then_inc(w16_done, 1)
            mod_part(2, GATE1)
            mod_part(3, SHIFT2)
            inputs(G - 1, 3)
            dve.wait_ge(pw_in, 32)
            for b in range(NB):
                dve.wait_ge(ga_ready, b + 1)
                nc.vector.tensor_tensor(pbga_rows[:, b * D:(b + 1) * D], bank[6 + b][:, :], pb_rows, ALU.mult).then_inc(ga_done, 1)
            for b in range(NB):
                nc.vector.tensor_tensor(pw_tmp[:, b, :], bank[6 + b][:, :], pw_raw, ALU.mult).then_inc(ga_done, 1)
            dve.wait_ge(sbhi_done, 1)
            nc.vector.tensor_tensor(sb_cols[:, :, NB:2 * NB], modT[:, SHIFT2], f32(sb_cols[:, :, 0:NB]), ALU.subtract).then_inc(sblo_done, 1)
            nc.vector.tensor_tensor(sel[:, :], ident[0:2 * NB, 0:NB], ident[0:2 * NB, NB:2 * NB], ALU.add).then_inc(sel_done, 1)
            mod_part(4, SCALE2)
            mod_part(5, GATE2)

            def split(g, m):
                if isinstance(g, int):
                    dve.wait_ge(cs_hid, m + 1)
                elif m < 2:
                    dve.wait_ge(cs_pool, 2 * (g - 1) + m + 1)
                else:
                    dve.wait_ge(cs_hid, g + 3)
                nc.vector.tensor_tensor(cs_lo[:, m, :], cT[:, bass.ds(GT * g + m * T, GT)], f32(cs_hi[:, m, :]),
                                        ALU.subtract).then_inc(cs_lod, 1)

            def qk_out(g, t):
                dve.wait_ge(qk_ready, 2 * JT * g + t + 1)
                if t < JT:
                    nc.vector.tensor_scalar(qh[:, t, :], bank[t % 4][:, :], cols[:, R_BQ + t:R_BQ + t + 1], QSCALE,
                                            ALU.add, ALU.mult).then_inc(qk_dve, 1)
                else:
                    nc.vector.tensor_scalar(kh[:, t - JT, :], bank[t % 4][:, :], cols[:, R_BK + t - JT:R_BK + t - JT + 1], None,
                                            ALU.add).then_inc(qk_dve, 1)

            def maxima(g, u):
                for half in range(2):
                    dve.wait_ge(s_ready, 2 * UNITS * g + 2 * u + half + 1)
                    nc.vector.tensor_reduce(neg_max[:, u % 2, half * HB:(half + 1) * HB], heads_of(s_bank(u, half)),
                                            AX_X, ALU.max, negate=True).then_inc(max_done, 1)

            def inverses(g, u):
                for half in range(2):
                    dve.wait_ge(exp_done, 2 * UNITS * g + 2 * u + half + 1)
                    nc.vector.reciprocal(row_inv[:, u % 2, half * HB:(half + 1) * HB],
                                         row_sum[:, u % 2, half * HB:(half + 1) * HB]).then_inc(inv_done, 1)

            def prob_columns(g, u):
                for at, half in enumerate(halves(u)):
                    dve.wait_ge(pt_ready, 2 * UNITS * g + 2 * u + at + 1)
                    if u >= 2:
                        dve.wait_ge(o_ready, UNITS * g + u - 1)
                    nc.vector.tensor_copy(probT[:, u % 2, half * HB:(half + 1) * HB, :],
                                          heads_of(bank[4 + half])).then_inc(pt_done, 1)

            def o_low(g, u):
                dve.wait_ge(o_hid, UNITS * g + u + 1)
                js, ts = slice(HB * (u % 2), HB * (u % 2 + 1)), slice((u // 2 % 2) * P, (u // 2 % 2 + 1) * P)
                nc.vector.tensor_tensor(oT_lo[:, js, ts], heads_of(turn_bank(g, "out", u)), f32(oT_hi[:, js, ts]),
                                        ALU.subtract).then_inc(o_lod, 1)

            def y_low(g, k):
                dve.wait_ge(y_hid, 2 * g + k + 1)
                ts = slice(2 * P * k, 2 * P * (k + 1))
                nc.vector.scalar_tensor_tensor(out=yT_lo[:, ts], in0=turn_bank(g, "wo", k)[:, 0:2 * P], scalar=by[:, 0:1],
                                               in1=f32(yT_hi[:, ts]), op0=ALU.add, op1=ALU.subtract).then_inc(y_lod, 1)

            def residual(g, b):
                dve.wait_ge(pj_ready, BLK * g + b + 1)
                dve.wait_ge(xrb_done, BLK * g + b + 1)
                nc.vector.tensor_tensor(xr[:, b, :], turn_bank(g, "proj", b)[:, :], xr[:, b, :], ALU.add).then_inc(x1_done, 1)
                dve.wait_ge(x1_done, BLK * g + b + 1)
                norm_stats(xr, g, b, st2)

            def h2_low(g, n):
                dve.wait_ge(h2_hid, 2 * DT * g + 2 * n + 2)
                for e in range(2):
                    d, ts = 2 * (n % 2) + e, slice(n // 2 * 2 * P, (n // 2 + 1) * 2 * P)
                    nc.vector.scalar_tensor_tensor(out=h2_lo[:, d, ts], in0=turn_bank(g, "norm", n)[:, e * 2 * P:(e + 1) * 2 * P],
                                                   scalar=cur2[:, 0, d, :], in1=f32(h2_hi[:, d, ts]), op0=ALU.mult,
                                                   op1=ALU.subtract).then_inc(h2_lod, 1)

            def ffn_out(g, b):
                dve.wait_ge(f_ready, BLK * g + b + 1)
                nc.vector.tensor_tensor(y16[:, b % 2, :], turn_bank(g, "ffn", b)[:, :], shift_rows[:, bass.ds(g // GPB * D, D)],
                                        ALU.add).then_inc(y16_done, 1)
                dve.wait_ge(y16_done, Y16_FREE + BLK * g + b + 1)
                dve.wait_ge(out_ready, BLK * g + b + 1)
                nc.vector.tensor_tensor(spare[:, b % 2, 0:D], y16[:, b % 2, :], gb_rows[:, bass.ds(g // GPB * D, D)],
                                        ALU.mult).then_inc(gy_done, 1)

            def units(g, ahead=None):
                for u in range(2, UNITS):
                    maxima(g, u)
                    inverses(g, u - 1)
                    prob_columns(g, u - 2)
                    if ahead is not None and u in (3, 5):
                        split(ahead, (u - 3) // 2)
                    if 3 <= u < 7:
                        o_low(g, u - 3)
                inverses(g, UNITS - 1)
                if isinstance(g, int):
                    y_low(g, 0)
                    prob_columns(g, 6)
                    o_low(g, 4)
                else:
                    o_low(g, 4)
                    prob_columns(g, 6)
                    y_low(g, 0)

            def finish(g, ahead):
                def fill(*tiles):
                    for t in tiles:
                        qk_out(ahead, t)

                split(ahead, 2)
                o_low(g, 5)
                prob_columns(g, 7)
                residual(g, 0)
                residual(g, 1)
                norm_variance(g, st2, ag2, var2, 0, 2)
                o_low(g, 6)
                fill(5)
                norm_apply(xr, rstd2, 2 * g + 1, xn2_done, 0, 2)
                o_low(g, 7)
                fill(7)
                h2_low(g, 0)
                h2_low(g, 1)
                fill(9)
                y_low(g, 1)
                ffn_out(g, 0)
                ffn_out(g, 1)
                residual(g, 2)
                residual(g, 3)
                norm_variance(g, st2, ag2, var2, 2, BLK)
                fill(13)
                norm_apply(xr, rstd2, 2 * g + 2, xn2_done, 2, BLK)

            split(0, 0)
            split(0, 1)
            conv_out(G - 1, (0, 1))
            for b in range(NB):
                dve.wait_ge(gb_ready, b + 1)
                nc.vector.tensor_copy(gb_rows[:, b * D:(b + 1) * D], bank[6 + b][:, :]).then_inc(gb_done, 1)
            conv_out(G - 1, (2,))
            split(0, 2)
            for t in QK_DVE:
                qk_out(0, t)
            dve.wait_ge(by_ready, 1)
            nc.vector.tensor_scalar(by[:, :], bank[4][:, 0:1], cols[:, R_BO:R_BO + 1], None, ALU.add).then_inc(by_done, 1)
            for b in range(NB):
                dve.wait_ge(pwhi_done, b + 1)
                nc.vector.tensor_tensor(pw_lo[:, b * D:(b + 1) * D], pw_tmp[:, b, :], f32(pw_hi[:, b * D:(b + 1) * D]),
                                        ALU.subtract).then_inc(pwlo_done, 1)
            maxima(0, 0)
            maxima(0, 1)
            inverses(0, 0)
            with dve.Fori(0, G - 1) as i:
                units(i, i + 1)
                finish(i, i + 1)
                maxima(i + 1, 0)
                h2_low(i, 2)
                h2_low(i, 3)
                maxima(i + 1, 1)
                inverses(i + 1, 0)
                ffn_out(i, 2)
                ffn_out(i, 3)
            units(G - 1)
            o_low(G - 1, 5)
            residual(G - 1, 0)
            residual(G - 1, 1)
            o_low(G - 1, 6)
            o_low(G - 1, 7)
            norm_variance(G - 1, st2, ag2, var2, 0, 2)
            norm_apply(xr, rstd2, 2 * G - 1, xn2_done, 0, 2)
            y_low(G - 1, 1)
            h2_low(G - 1, 0)
            h2_low(G - 1, 1)
            residual(G - 1, 2)
            residual(G - 1, 3)
            norm_variance(G - 1, st2, ag2, var2, 2, BLK)
            norm_apply(xr, rstd2, 2 * G, xn2_done, 2, BLK)
            ffn_out(G - 1, 0)
            h2_low(G - 1, 2)
            h2_low(G - 1, 3)
            ffn_out(G - 1, 1)
            ffn_out(G - 1, 2)
            b = BLK - 1
            for k, ns in enumerate(column_parts(G - 1, b)):
                n = BLK * G + k
                dve.wait_ge(f_ready, n)
                nc.vector.tensor_tensor(y16[:, b % 2, ns], (last_half_bank if k == 1 else turn_bank(G - 1, "ffn", b))[:, ns],
                                        shift_rows[:, (NB - 1) * D + ns.start:(NB - 1) * D + ns.stop], ALU.add).then_inc(y16_done, 1)
                dve.wait_ge(y16_done, Y16_FREE + n)
                if k == 0:
                    dve.wait_ge(out_ready, BLK * G)
                nc.vector.tensor_tensor(spare[:, b % 2, ns], y16[:, b % 2, ns],
                                        gb_rows[:, (NB - 1) * D + ns.start:(NB - 1) * D + ns.stop], ALU.mult).then_inc(gy_done, 1)
                dve.wait_ge(gy_done, n)
                nc.vector.tensor_tensor(xr[:, b, ns], spare[:, b % 2, ns], xr[:, b, ns], ALU.add).then_inc(last_ready, 1)

        @block.tensor
        def _(pe):
            pe.wait_ge(c_in, 16)
            pe.wait_ge(ident_done, 2)
            nc.tensor.transpose(bank[6][:, 0:NC], c_rows[:, :], ident[0:NC, 0:NC]).then_inc(ccols_ready, 1)

            def product3(dst, w_hi, w_lo, m_hi, m_lo, start, stop, **how):
                nc.tensor.matmul(dst, w_hi, m_hi, start=start, stop=False, **how)
                nc.tensor.matmul(dst, w_hi, m_lo, start=False, stop=False, **how)
                return nc.tensor.matmul(dst, w_lo, m_hi, start=False, stop=stop, **how)

            def mod_part(n):
                pe.wait_ge(mod_in[n % 2], 16 * (n // 2 + 1))
                if n >= 4:
                    pe.wait_ge(mod_done, n - 1)
                for k in range(DT):
                    mm = nc.tensor.matmul(mod_bank(n)[0:NB, :], silu[:, 3, :].rearrange("p (b k) -> p k b", b=NB)[:, k, :],
                                          mod_stage[n % 2][:, k, :], start=(k == 0), stop=(k == DT - 1))
                mm.then_inc(mod_ready, 1)

            def mod_columns(n):
                pe.wait_ge(modrow_done, n + 1)
                for d in range(DT):
                    mm = nc.tensor.transpose(bank[6 + n % 2][:, NB * d:NB * (d + 1)], mod_row[:, n % 2, d * P:(d + 1) * P],
                                             ident[0:NB, 0:NB])
                mm.then_inc(modcol_ready, 1)

            def activations(g, d):
                n = DT * g + d
                pe.wait_ge(xn_done, BLK * g + BLK)
                if not isinstance(g, int) or n >= 2:
                    pe.wait_ge(h_done, n - 1)
                for b in range(BLK):
                    mm = nc.tensor.transpose(bank[6 + d % 2][:, b * P:(b + 1) * P], xin[:, b, d * P:(d + 1) * P], ident[:, :])
                mm.then_inc(t1_ready, 1)

            pe.wait_ge(silu_step, 3)
            mod_part(0)
            mod_part(1)
            mod_columns(0)
            mod_columns(1)
            pe.wait_ge(halo_step, 4)
            for d in range(DT):
                mm = nc.tensor.transpose(bank[5][:, 2 * NB * d:2 * NB * (d + 1)], halo_x[:, d * P:(d + 1) * P],
                                         ident[0:2 * NB, 0:2 * NB])
            mm.then_inc(halo_ready, 1)
            pe.wait_ge(rows_in, 80)
            nc.tensor.transpose(bank[4][:, 0:NR], rows[:, :], ident[0:NR, 0:NR]).then_inc(cols_ready, 1)
            pe.wait_ge(mod_done, 2)
            for d in range(DT):
                if d == 2:
                    mod_part(2)
                activations(0, d)

            def conv(g, d, ahead=None):
                pe.wait_ge(cx_lod, DT * g + d + 1)
                pe.wait_ge(culo_done, 3 * d + 3)
                for m in range(3):
                    if m == 2 and ahead is not None:
                        activations(ahead, 0)
                        activations(ahead, 1)
                    if d == 0:
                        pe.wait_ge(c_done, 3 * g + m + 1)
                        if m == 1:
                            pe.wait_ge(modrow_done, 3)
                        elif m == 2:
                            pe.wait_ge(halo_step, 5)
                            pe.wait_ge(cols_done, 1)
                    ws = slice(m * W, (m + 1) * W)
                    for k in range(NM):
                        ts = slice(k * GH, (k + 1) * GH)
                        mm = product3(bank[2 * m + k // 2][:, (k % 2) * GH:(k % 2 + 1) * GH], cu_hi[:, d, k, ws], cu_lo[:, d, k, ws],
                                      cx_hi[:, d % 2, ts], cx_lo[:, d % 2, ts],
                                      d == 0 and k % 2 == 0, d == DT - 1, skip_group_check=True)
                    if d == DT - 1:
                        mm.then_inc(conv_ready, 1)
                if d < DT - 1:
                    mm.then_inc(conv_tile, 1)

            def conv_last_tile(g):
                conv(g, DT - 1)
                activations(g + 1, 2)
                activations(g + 1, 3)

            conv(0, 0)
            conv(0, 1)
            pe.wait_ge(h_done, DT)
            mod_part(3)
            conv(0, 2)
            pe.wait_ge(modrow_done, 4)
            activations(1, 0)
            activations(1, 1)
            with pe.Fori(0, G - 2) as i:
                conv_last_tile(i)
                conv(i + 1, 0)
                conv(i + 1, 1)
                conv(i + 1, 2, i + 2)
            conv_last_tile(G - 2)

            def gate_rows(part, ready):
                for b in range(NB):
                    for d in range(DT):
                        mm = nc.tensor.matmul(bank[6 + b][:, d * P:(d + 1) * P],
                                              modT[:, part, d, b:b + 1].to_broadcast((P, P)), ident[:, :], start=True, stop=True)
                    mm.then_inc(ready, 1)

            conv(G - 1, 0)
            pe.wait_ge(h_done, DT * G)
            mod_columns(2)
            mod_columns(3)
            conv(G - 1, 1)
            pe.wait_ge(mod_done, 4)
            gate_rows(GATE1, ga_ready)
            conv(G - 1, 2)
            pe.wait_ge(ga_done, 2 * NB)
            mod_part(4)
            mod_part(5)
            mod_columns(4)
            mod_columns(5)
            conv(G - 1, DT - 1)
            pe.wait_ge(mod_done, 6)
            gate_rows(GATE2, gb_ready)
            w16_rows = w16.rearrange("p a n -> p (a n)").rearrange("p (o n) -> p o n", o=BLK)

            def weight_columns(d):
                if d >= 2:
                    pe.wait_ge(wt_done, d - 1)
                for o in range(BLK):
                    mm = nc.tensor.transpose(bank[6 + d % 2][:, :].bitcast(F16)[:, o * P:(o + 1) * P],
                                             w16_rows[:, o, d * P:(d + 1) * P], ident_h[:, :])
                mm.then_inc(wt_ready, 1)


            def bank_read(g, use):
                if use >= 0 or not (isinstance(g, int) and g == 0):
                    pe.wait_ge(*released(g, use))
                else:
                    pe.wait_ge(c_done, C_FREE + 3 * G - (2 if use < -2 else 1))

            def qk_tile(g, t):
                m, j = t // JT, t % JT
                pe.wait_ge(cs_lod, 3 * g + m + 1)
                bank_read(g, t - 4)
                js = slice(j * P, (j + 1) * P)
                product3(bank[t % 4][:, :], wqkv_hi[:, m, js], wqkv_lo[:, m, js], cs_hi[:, m, :], cs_lo[:, m, :],
                         True, True).then_inc(qk_ready, 1)

            def values(g, u):
                pe.wait_ge(cs_lod, 3 * g + 3)
                if u >= 3:
                    pe.wait_ge(pt_done, 2 * UNITS * g + 2 * (u - 3) + halves(u - 3).index(0) + 1)
                elif u == 0 and not isinstance(g, int):
                    pe.wait_ge(pt_done, 2 * UNITS * g - 1)
                elif u > 0:
                    pe.wait_ge(v_act, UNITS * g + u)
                ts, ns = slice(u // 2 * P, (u // 2 + 1) * P), slice(u % 2 * HE // 2, (u % 2 + 1) * HE // 2)
                product3(bank[4][:, :], cs_hi[:, 2, ts], cs_lo[:, 2, ts], wqkv_hi[:, 2, ns], wqkv_lo[:, 2, ns],
                         True, True).then_inc(v_ready, 1)

            def scores(g, u):
                if u < 2:
                    last = 2 * JT - 1 - (JT // 2 if u == 0 else 0)
                    pe.wait_ge(qk_act, qk_count(QK_ACT, g, last))
                    pe.wait_ge(qk_dve, qk_count(QK_DVE, g, last))
                for half in range(2):
                    bank_read(g, 2 * JT + 2 * u + half - 4)
                    nc.tensor.matmul(s_bank(u, half)[:, :], ident_b[:, :], mask[:, :, :].rearrange("p h k -> p (h k)"),
                                     start=True, stop=False, skip_group_check=True)
                ts = slice(u // 2 * P, (u // 2 + 1) * P)
                for h in range(HB):
                    for half in range(2):
                        es, j = slice(half * E, (half + 1) * E), HB * (u % 2) + h
                        mm = nc.tensor.matmul(s_bank(u, half)[:, h * P:(h + 1) * P], qh[es, j, ts], kh[es, j, ts],
                                              start=False, stop=True, skip_group_check=True)
                        if h == HB - 1:
                            mm.then_inc(s_ready, 1)

            def transpose_probs(g, u):
                for at, half in enumerate(halves(u)):
                    pe.wait_ge(norm_done, 2 * UNITS * g + 2 * u + half + 1)
                    if half == 0:
                        pe.wait_ge(v_act, UNITS * g + min(u + 3, UNITS))
                    if u >= 1:
                        pe.wait_ge(pt_done, 2 * UNITS * g + 2 * (u - 1) + halves(u - 1).index(half) + 1)
                    for h in range(HB):
                        mm = nc.tensor.transpose(bank[4 + half][:, h * P:(h + 1) * P], prob[:, u % 2, half * HB + h, :], ident[:, :])
                    mm.then_inc(pt_ready, 1)

            def my_turn(g, kind, n):
                pe.wait_ge(*turn_free(g, kind, n))

            def outputs(g, u):
                if isinstance(g, int) and u == UNITS - 1:
                    pe.wait_ge(last_probs, 2)
                else:
                    pe.wait_ge(pt_done, 2 * UNITS * g + 2 * u + 2)
                pe.wait_ge(v_act, UNITS * g + u + 1)
                my_turn(g, "out", u)
                for h in range(HB):
                    for half in range(2):
                        head = HU * (u % 2) + 2 * h + half
                        mm = nc.tensor.matmul(turn_bank(g, "out", u)[half * E:(half + 1) * E, h * P:(h + 1) * P],
                                              vh[:, u // 2 % 2, head * E:(head + 1) * E], probT[:, u % 2, half * HB + h, :],
                                              start=True, stop=True, skip_group_check=True)
                mm.then_inc(o_ready, 1)

            def out_product(g, k):
                pe.wait_ge(o_lod, UNITS * g + 4 * (k + 1))
                my_turn(g, "wo", k)
                for j in range(JT):
                    mm = product3(turn_bank(g, "wo", k)[:, 0:2 * P], wo_hi[:, j, :], wo_lo[:, j, :], oT_hi[:, j, :], oT_lo[:, j, :],
                                  j == 0, j == JT - 1)
                mm.then_inc(wo_ready, 1)

            def project(g, b):
                pe.wait_ge(pwlo_done, NB)
                pe.wait_ge(y_lod, 2 * g + b // 2 + 1)
                my_turn(g, "proj", b)
                ts, ds = slice(b * P, (b + 1) * P), bass.ds(g // GPB * D, D)
                product3(turn_bank(g, "proj", b)[:, :], yT_hi[:, ts], yT_lo[:, ts], pw_hi[:, ds], pw_lo[:, ds],
                         True, True).then_inc(pj_ready, 1)

            def norm_columns(g, n):
                pe.wait_ge(xn2_done, BLK * g + 2 * (n // 2) + 2)
                my_turn(g, "norm", n)
                for e in range(2):
                    d = 2 * (n % 2) + e
                    for r in range(2):
                        mm = nc.tensor.transpose(turn_bank(g, "norm", n)[:, (2 * e + r) * P:(2 * e + r + 1) * P],
                                                 xin[:, n // 2 * 2 + r, d * P:(d + 1) * P], ident[:, :])
                mm.then_inc(t2_ready, 1)

            def feed_forward(g, b):
                my_turn(g, "ffn", b)
                for k, ns in enumerate(column_parts(g, b)):
                    if k == 1:
                        pe.wait_ge(x1_done, BLK * G - 1)
                    dst = last_half_bank if k == 1 else turn_bank(g, "ffn", b)
                    for d in range(DT):
                        if d % 2 == 0:
                            pe.wait_ge(h2_lod, 2 * DT * g + DT * (b // 2) + d + 2)
                        for half, h2 in enumerate((h2_hi, h2_lo)):
                            mm = nc.tensor.matmul(dst[:, ns], h2[:, d, b * P:(b + 1) * P], wT[:, d, ns],
                                                  start=(d == 0 and half == 0), stop=(d == DT - 1 and half == 1))
                    mm.then_inc(f_ready, 1)

            def units(g):
                for u in range(2, UNITS):
                    scores(g, u)
                    values(g, u)
                    if u >= 3:
                        outputs(g, u - 3)
                    transpose_probs(g, u - 2)
                    if u == 7:
                        out_product(g, 0)
                transpose_probs(g, 6)

            def finish(g, ahead):
                def fill(*tiles):
                    for t in tiles:
                        qk_tile(ahead, t)

                fill(0, 1)
                outputs(g, 5)
                transpose_probs(g, 7)
                fill(2)
                project(g, 0)
                fill(3)
                project(g, 1)
                outputs(g, 6)
                fill(4, 5)
                outputs(g, 7)
                fill(6, 7)
                norm_columns(g, 0)
                norm_columns(g, 1)
                fill(8, 9)
                out_product(g, 1)
                feed_forward(g, 0)
                feed_forward(g, 1)
                project(g, 2)
                fill(10)
                project(g, 3)
                fill(11, 12, 13, 14, 15)

            pe.wait_ge(wlo_done, 4)
            for t in range(2 * JT):
                if t == 4:
                    pe.wait_ge(w16_done, BLK)
                    pe.wait_ge(mask_done, 3)
                    pe.wait_ge(gb_done, NB)
                    weight_columns(0)
                    weight_columns(1)
                elif t == 12:
                    weight_columns(2)
                    weight_columns(3)
                qk_tile(0, t)
                if t >= JT:
                    if t == JT:
                        pe.wait_ge(c_done, C_FREE + 3 * G)
                        pe.wait_ge(wo_in, 16)
                    j = t - JT
                    mm = nc.tensor.matmul(bank[4][:, 0:1], wo_raw[:, j, :], cols[:, R_BV + j:R_BV + j + 1],
                                          start=(j == 0), stop=(j == JT - 1))
            mm.then_inc(by_ready, 1)
            pe.wait_ge(sblo_done, 1)
            pe.wait_ge(wt_done, DT)
            for d in range(DT):
                mm = nc.tensor.matmul(bank[5][0:2 * NB, :], sb_cols[:, d, :], wT[:, d, :], start=(d == 0), stop=(d == DT - 1))
            mm.then_inc(shiftrow_ready, 1)
            pe.wait_ge(mask_done, 4)
            scores(0, 0)
            pe.wait_ge(sel_done, 1)
            pe.wait_ge(shiftrow_done, 1)
            for b in range(NB):
                nc.tensor.matmul(bank[6 + b][:, :], sel[:, b:b + 1].to_broadcast((2 * NB, P)), shift_row[:, :],
                                 start=True, stop=True).then_inc(shift_ready, 1)
            pe.wait_ge(by_done, 1)
            values(0, 0)
            scores(0, 1)
            values(0, 1)
            pe.wait_ge(shift_done, NB)
            with pe.Fori(0, G - 1) as i:
                units(i)
                finish(i, i + 1)
                scores(i + 1, 0)
                values(i + 1, 0)
                norm_columns(i, 2)
                norm_columns(i, 3)
                scores(i + 1, 1)
                values(i + 1, 1)
                feed_forward(i, 2)
                feed_forward(i, 3)
            units(G - 1)
            outputs(G - 1, 5)
            project(G - 1, 0)
            project(G - 1, 1)
            transpose_probs(G - 1, 7)
            outputs(G - 1, 6)
            outputs(G - 1, 7)
            out_product(G - 1, 1)
            norm_columns(G - 1, 0)
            norm_columns(G - 1, 1)
            project(G - 1, 2)
            project(G - 1, 3)
            feed_forward(G - 1, 0)
            feed_forward(G - 1, 1)
            norm_columns(G - 1, 2)
            norm_columns(G - 1, 3)
            feed_forward(G - 1, 2)
            feed_forward(G - 1, 3)


_INS = ['L0_attn_inputs', 'L0_attn_conv_w', 'L0_attn_conv_b', 'L0_attn_wq', 'L0_attn_bq', 'L0_attn_wk', 'L0_attn_bk',
        'L0_attn_wv', 'L0_attn_bv', 'L0_attn_wo', 'L0_attn_bo', 'L0_attn_proj_w', 'L0_attn_proj_b', 'L0_ffn_weight',
        'L0_ffn_scales', 'L0_c', 'L0_wmod']


def kernel(**inputs):
    import numpy as _np
    import concourse.bacc as _bacc
    from concourse import mybir as _mybir
    from concourse.bass_utils import run_bass_kernel_spmd as _run

    nc = _bacc.Bacc("TRN2", target_bir_lowering=False, num_devices=1, dynamic_dma_scratch_size=1024)
    arrays, args = {}, []
    for name in _INS:
        a = _np.ascontiguousarray(inputs[name])
        arrays[f"in_{name}_dram"] = a
        args.append(nc.dram_tensor(f"in_{name}_dram", a.shape, _mybir.dt.from_np(a.dtype), kind="ExternalInput").ap())
    shape = inputs['L0_attn_inputs'].shape
    args.append(nc.dram_tensor("out_0_dram", shape, _mybir.dt.float32, kind="ExternalOutput").ap())
    adaln_block(nc, *args)
    r = _run(nc, [arrays], core_ids=[0])
    return r.results[0]["out_0_dram"]
```
